# Optimizing a Trainium2 kernel written in Bass

```python
import numpy as np
import jax
import jax.numpy as jnp

def _softmax(x, axis=-1):
    return jax.nn.softmax(x, axis=axis)

def _gelu(x):
    return jax.nn.gelu(x, approximate=True)

def _silu(x):
    return jax.nn.silu(x)

def _sigmoid(x):
    return jax.nn.sigmoid(x)

def _layernorm(x, axis=-1, eps=1e-05):
    m = jnp.mean(x, axis=axis, keepdims=True)
    v = jnp.var(x, axis=axis, keepdims=True)
    return (x - m) / jnp.sqrt(v + eps)

def _scatter_add(tgt, idx, src, axis=0):
    return tgt.at[idx].add(src)

def _segment_sum(src, seg, n):
    return jax.ops.segment_sum(src, seg, n)
kernel_name = 'mk_metaformer_d2_conv_nchw128_r2_36a2cf'

def setup_inputs(seed: int=0):
    np.random.seed(seed)
    _w = jnp.asarray

    def _rec_inputs():
        import jax
        import jax.numpy as jnp
        _gk = jax.random.key(seed)
        x = -0.000125 + 0.9999 * jax.random.normal(jax.random.fold_in(_gk, 1), (4, 64, 128, 128), jnp.float32)
        return x
    x = _rec_inputs()

    def _L0_conv_setup():
        import jax, jax.numpy as jnp
        import numpy as np
        C = 64
        B, H, W = (4, 128, 128)

        def haar_dwt(x):
            b_, c_, h_, w_ = x.shape
            xr = x.reshape(b_, c_, h_ // 2, 2, w_ // 2, 2)
            a = xr[:, :, :, 0, :, 0]
            b = xr[:, :, :, 0, :, 1]
            c = xr[:, :, :, 1, :, 0]
            d = xr[:, :, :, 1, :, 1]
            ll = (a + b + c + d) * 0.5
            lh = (a + b - c - d) * 0.5
            hl = (a - b + c - d) * 0.5
            hh = (a - b - c + d) * 0.5
            return (ll, lh, hl, hh)

        def haar_idwt(ll, lh, hl, hh):
            a = (ll + lh + hl + hh) * 0.5
            b = (ll + lh - hl - hh) * 0.5
            c = (ll - lh + hl - hh) * 0.5
            d = (ll - lh - hl + hh) * 0.5
            b_, c_, h2, w2 = ll.shape
            out = jnp.stack([jnp.stack([a, b], axis=-1), jnp.stack([c, d], axis=-1)], axis=-2)
            out = out.transpose(0, 1, 2, 4, 3, 5)
            return out.reshape(b_, c_, 2 * h2, 2 * w2)
        key = jax.random.key(seed)
        kx, = jax.random.split(key, 1)
        x = jax.random.normal(kx, (B, C, H, W), dtype=jnp.float32)
        s_ll = jnp.ones((C,), jnp.float32)
        s_lh = jnp.full((C,), 0.5, jnp.float32)
        s_hl = jnp.full((C,), 0.5, jnp.float32)
        s_hh = jnp.zeros((C,), jnp.float32)
        w1 = np.zeros((C, 4 * C), np.float32)
        w2 = np.zeros((4 * C, C), np.float32)
        idx = np.arange(C)
        for j in range(4):
            w1[idx, idx + j * C] = 0.5
            w2[idx + j * C, idx] = 0.5
        return {'x': x, 's_ll': s_ll, 's_lh': s_lh, 's_hl': s_hl, 's_hh': s_hh, 'w1': jnp.asarray(w1), 'b1': jnp.zeros((C,), jnp.float32), 'w2': jnp.asarray(w2), 'b2': jnp.zeros((4 * C,), jnp.float32)}
    _L0_conv_all = _L0_conv_setup()
    _L0_conv_in = {k: v for k, v in _L0_conv_all.items() if k in ('s_ll', 's_lh', 's_hl', 's_hh', 'w1', 'b1', 'w2', 'b2')}
    del _L0_conv_all

    def _L0_ffn_setup():
        import jax, jax.numpy as jnp
        import numpy as np
        B, S, D, E, H, O, K = (256, 1024, 64, 32, 256, 64, 8)
        key = jax.random.key(seed)
        k0, k1, k2, k3 = jax.random.split(key, 4)
        x = jax.random.normal(k0, (B, S, D), dtype=jnp.float32)
        gate_w = jax.random.normal(k1, (E, D), dtype=jnp.float32) * (1.0 / np.sqrt(D))
        gate_b = jnp.zeros((E,), dtype=jnp.float32)
        weight1 = jax.random.uniform(k2, (E, D + 1, H), dtype=jnp.float32, minval=-1.0, maxval=1.0) * (1.0 / np.sqrt(D + 1))
        weight2 = jax.random.uniform(k3, (E, H + 1, O), dtype=jnp.float32, minval=-1.0, maxval=1.0) * (1.0 / np.sqrt(H + 1))
        return {'x': x, 'gate_w': gate_w, 'gate_b': gate_b, 'weight1': weight1, 'weight2': weight2}
    _L0_ffn_all = _L0_ffn_setup()
    _L0_ffn_in = {k: v for k, v in _L0_ffn_all.items() if k in ('gate_w', 'gate_b', 'weight1', 'weight2')}
    del _L0_ffn_all

    def _L1_conv_setup():
        import jax, jax.numpy as jnp
        import numpy as np
        from jax import lax
        C = 64
        KS = 9
        PAD = KS // 2

        def _conv1d(r, w):
            return lax.conv_general_dilated(r, w, window_strides=(1,), padding=[(PAD, PAD)], dimension_numbers=('NCH', 'OIH', 'NCH'))

        def _pass_once(x, w, vertical, reverse):
            if not vertical:
                x = jnp.transpose(x, (0, 1, 3, 2))
            if reverse:
                x = jnp.flip(x, axis=2)
            xs = jnp.moveaxis(x, 2, 0)

            def step(carry, xi):
                y = xi + jax.nn.relu(_conv1d(carry, w))
                return (y, y)
            _, ys = lax.scan(step, xs[0], xs[1:])
            out = jnp.concatenate([xs[:1], ys], axis=0)
            out = jnp.moveaxis(out, 0, 2)
            if reverse:
                out = jnp.flip(out, axis=2)
            if not vertical:
                out = jnp.transpose(out, (0, 1, 3, 2))
            return out
        key = jax.random.key(seed)
        kx, k1, k2, k3, k4 = jax.random.split(key, 5)
        B, H, W = (8, 64, 128)
        std = (1.0 / (C * KS)) ** 0.5
        x = jax.random.normal(kx, (B, C, H, W), dtype=jnp.float32)
        w_ud = jax.random.normal(k1, (C, C, KS), dtype=jnp.float32) * std
        w_du = jax.random.normal(k2, (C, C, KS), dtype=jnp.float32) * std
        w_lr = jax.random.normal(k3, (C, C, KS), dtype=jnp.float32) * std
        w_rl = jax.random.normal(k4, (C, C, KS), dtype=jnp.float32) * std
        return {'x': x, 'w_ud': w_ud, 'w_du': w_du, 'w_lr': w_lr, 'w_rl': w_rl}
    _L1_conv_all = _L1_conv_setup()
    _L1_conv_in = {k: v for k, v in _L1_conv_all.items() if k in ('w_ud', 'w_du', 'w_lr', 'w_rl')}
    del _L1_conv_all

    def _L1_ffn_setup():
        import jax, jax.numpy as jnp
        import numpy as np
        B, N, D, C, E, K = (8, 4096, 64, 64, 8, 2)
        key = jax.random.key(seed)
        k0, k1, k2 = jax.random.split(key, 3)
        x = jax.random.normal(k0, (B, N, D), dtype=jnp.float32)
        router_w = jax.random.normal(k1, (D, E), dtype=jnp.float32) * 0.05
        router_b = jnp.zeros((E,), dtype=jnp.float32)
        expert_w = jax.random.normal(k2, (E, D, C), dtype=jnp.float32) * (1.0 / np.sqrt(D))
        expert_b = jnp.zeros((E, C), dtype=jnp.float32)
        return {'x': x, 'router_w': router_w, 'router_b': router_b, 'expert_w': expert_w, 'expert_b': expert_b}
    _L1_ffn_all = _L1_ffn_setup()
    _L1_ffn_in = {k: v for k, v in _L1_ffn_all.items() if k in ('router_w', 'router_b', 'expert_w', 'expert_b')}
    del _L1_ffn_all
    return {'x': x, 'L0_conv_s_ll': _L0_conv_in['s_ll'], 'L0_conv_s_lh': _L0_conv_in['s_lh'], 'L0_conv_s_hl': _L0_conv_in['s_hl'], 'L0_conv_s_hh': _L0_conv_in['s_hh'], 'L0_conv_w1': _L0_conv_in['w1'], 'L0_conv_b1': _L0_conv_in['b1'], 'L0_conv_w2': _L0_conv_in['w2'], 'L0_conv_b2': _L0_conv_in['b2'], 'L0_ffn_gate_w': _L0_ffn_in['gate_w'], 'L0_ffn_gate_b': _L0_ffn_in['gate_b'], 'L0_ffn_weight1': _L0_ffn_in['weight1'], 'L0_ffn_weight2': _L0_ffn_in['weight2'], 'L1_conv_w_ud': _L1_conv_in['w_ud'], 'L1_conv_w_du': _L1_conv_in['w_du'], 'L1_conv_w_lr': _L1_conv_in['w_lr'], 'L1_conv_w_rl': _L1_conv_in['w_rl'], 'L1_ffn_router_w': _L1_ffn_in['router_w'], 'L1_ffn_router_b': _L1_ffn_in['router_b'], 'L1_ffn_expert_w': _L1_ffn_in['expert_w'], 'L1_ffn_expert_b': _L1_ffn_in['expert_b']}

def reference(x, L0_conv_s_ll, L0_conv_s_lh, L0_conv_s_hl, L0_conv_s_hh, L0_conv_w1, L0_conv_b1, L0_conv_w2, L0_conv_b2, L0_ffn_gate_w, L0_ffn_gate_b, L0_ffn_weight1, L0_ffn_weight2, L1_conv_w_ud, L1_conv_w_du, L1_conv_w_lr, L1_conv_w_rl, L1_ffn_router_w, L1_ffn_router_b, L1_ffn_expert_w, L1_ffn_expert_b):
    import jax
    import jax.numpy as jnp

    def _L0_conv_ref(x, s_ll, s_lh, s_hl, s_hh, w1, b1, w2, b2):
        import jax, jax.numpy as jnp
        import numpy as np
        C = 64
        B, H, W = (4, 128, 128)

        def haar_dwt(x):
            b_, c_, h_, w_ = x.shape
            xr = x.reshape(b_, c_, h_ // 2, 2, w_ // 2, 2)
            a = xr[:, :, :, 0, :, 0]
            b = xr[:, :, :, 0, :, 1]
            c = xr[:, :, :, 1, :, 0]
            d = xr[:, :, :, 1, :, 1]
            ll = (a + b + c + d) * 0.5
            lh = (a + b - c - d) * 0.5
            hl = (a - b + c - d) * 0.5
            hh = (a - b - c + d) * 0.5
            return (ll, lh, hl, hh)

        def haar_idwt(ll, lh, hl, hh):
            a = (ll + lh + hl + hh) * 0.5
            b = (ll + lh - hl - hh) * 0.5
            c = (ll - lh + hl - hh) * 0.5
            d = (ll - lh - hl + hh) * 0.5
            b_, c_, h2, w2 = ll.shape
            out = jnp.stack([jnp.stack([a, b], axis=-1), jnp.stack([c, d], axis=-1)], axis=-2)
            out = out.transpose(0, 1, 2, 4, 3, 5)
            return out.reshape(b_, c_, 2 * h2, 2 * w2)
        orig_dtype = x.dtype
        xf = x.astype(jnp.float32)
        ll, lh, hl, hh = haar_dwt(xf)
        ll = ll * jnp.exp(s_ll)[None, :, None, None]
        lh = lh * jnp.exp(s_lh)[None, :, None, None]
        hl = hl * jnp.exp(s_hl)[None, :, None, None]
        hh = hh * jnp.exp(s_hh)[None, :, None, None]
        subbands = jnp.concatenate([ll, lh, hl, hh], axis=1)
        low_proj = jnp.einsum('bchw,oc->bohw', subbands, w1) + b1[None, :, None, None]
        restored = jnp.einsum('bchw,oc->bohw', low_proj, w2) + b2[None, :, None, None]
        ll_r, lh_r, hl_r, hh_r = jnp.split(restored, 4, axis=1)
        rec = haar_idwt(ll_r, lh_r, hl_r, hh_r)
        return rec.astype(orig_dtype)

    def _L0_ffn_ref(x, gate_w, gate_b, weight1, weight2):
        import jax, jax.numpy as jnp
        import numpy as np
        B, S, D, E, H, O, K = (256, 1024, 64, 32, 256, 64, 8)
        Bn, Sn, Dn = x.shape
        logits = jnp.einsum('bsd,ed->bse', x, gate_w) + gate_b
        probs = jax.nn.softmax(logits, axis=1)
        vals, idx = jax.lax.top_k(probs.transpose(0, 2, 1), K)
        topv = vals.transpose(0, 2, 1)
        topi = idx.transpose(0, 2, 1)
        flat_idx = topi.reshape(Bn, K * E)
        gathered = jnp.take_along_axis(x, flat_idx[:, :, None], axis=1)
        gathered = gathered.reshape(Bn, K, E, Dn)
        pooled = jnp.einsum('bked,bke->bed', gathered, topv)
        ones = jnp.ones((E, Bn, 1), dtype=x.dtype)
        h = jnp.concatenate([pooled.transpose(1, 0, 2), ones], axis=-1)
        h = jax.nn.gelu(jnp.einsum('ebd,edh->ebh', h, weight1), approximate=False)
        h = jnp.concatenate([h, ones], axis=-1)
        out = jnp.einsum('ebh,eho->ebo', h, weight2)
        out = out.transpose(1, 0, 2)
        weighted = jnp.einsum('beo,bke->bkeo', out, topv).reshape(Bn, K * E, O)
        outputs = jnp.zeros((Bn, Sn, O), dtype=x.dtype)
        outputs = outputs.at[jnp.arange(Bn)[:, None], flat_idx].add(weighted)
        return outputs

    def _L1_conv_ref(x, w_ud, w_du, w_lr, w_rl):
        import jax, jax.numpy as jnp
        import numpy as np
        from jax import lax
        C = 64
        KS = 9
        PAD = KS // 2

        def _conv1d(r, w):
            return lax.conv_general_dilated(r, w, window_strides=(1,), padding=[(PAD, PAD)], dimension_numbers=('NCH', 'OIH', 'NCH'))

        def _pass_once(x, w, vertical, reverse):
            if not vertical:
                x = jnp.transpose(x, (0, 1, 3, 2))
            if reverse:
                x = jnp.flip(x, axis=2)
            xs = jnp.moveaxis(x, 2, 0)

            def step(carry, xi):
                y = xi + jax.nn.relu(_conv1d(carry, w))
                return (y, y)
            _, ys = lax.scan(step, xs[0], xs[1:])
            out = jnp.concatenate([xs[:1], ys], axis=0)
            out = jnp.moveaxis(out, 0, 2)
            if reverse:
                out = jnp.flip(out, axis=2)
            if not vertical:
                out = jnp.transpose(out, (0, 1, 3, 2))
            return out
        x = _pass_once(x, w_ud, vertical=True, reverse=False)
        x = _pass_once(x, w_du, vertical=True, reverse=True)
        x = _pass_once(x, w_lr, vertical=False, reverse=False)
        x = _pass_once(x, w_rl, vertical=False, reverse=True)
        return x

    def _L1_ffn_ref(x, router_w, router_b, expert_w, expert_b):
        import jax, jax.numpy as jnp
        import numpy as np
        B, N, D, C, E, K = (8, 4096, 64, 64, 8, 2)
        router_probs = jax.nn.softmax(x @ router_w + router_b, axis=-1)
        top_p, top_i = jax.lax.top_k(router_probs, K)
        top_p = top_p / jnp.sum(top_p, axis=-1, keepdims=True)
        expert_out = jnp.einsum('bnd,edc->bnec', x, expert_w) + expert_b
        gathered = jnp.take_along_axis(expert_out, top_i[..., None], axis=2)
        return jnp.einsum('bnk,bnkc->bnc', top_p, gathered)

    def _gn(v, G=32, eps=1e-05):
        B_, C_, H_, W_ = v.shape
        g = v.reshape(B_, G, C_ // G, H_, W_)
        m = jnp.mean(g, axis=(2, 3, 4), keepdims=True)
        s = jnp.var(g, axis=(2, 3, 4), keepdims=True)
        return ((g - m) / jnp.sqrt(s + eps)).reshape(v.shape)

    def _ln_c(v, eps=1e-06):
        m = jnp.mean(v, axis=1, keepdims=True)
        s = jnp.var(v, axis=1, keepdims=True)
        return (v - m) / jnp.sqrt(s + eps)

    def _ln_t(v, eps=1e-05):
        m = jnp.mean(v, axis=-1, keepdims=True)
        s = jnp.var(v, axis=-1, keepdims=True)
        return (v - m) / jnp.sqrt(s + eps)

    def _to_tokens(v):
        B_, C_, H_, W_ = v.shape
        return v.reshape(B_, C_, H_ * W_).transpose(0, 2, 1)

    def _from_tokens(t, like):
        B_, C_, H_, W_ = like.shape
        return t.transpose(0, 2, 1).reshape(B_, C_, H_, W_)
    x = x + _L0_conv_ref(_ln_c(x), L0_conv_s_ll, L0_conv_s_lh, L0_conv_s_hl, L0_conv_s_hh, L0_conv_w1, L0_conv_b1, L0_conv_w2, L0_conv_b2)
    t = _to_tokens(x)
    t = t + _L0_ffn_ref(_ln_t(t), L0_ffn_gate_w, L0_ffn_gate_b, L0_ffn_weight1, L0_ffn_weight2)
    x = _from_tokens(t, x)
    x = x + _L1_conv_ref(_ln_c(x), L1_conv_w_ud, L1_conv_w_du, L1_conv_w_lr, L1_conv_w_rl)
    t = _to_tokens(x)
    t = t + _L1_ffn_ref(_ln_t(t), L1_ffn_router_w, L1_ffn_router_b, L1_ffn_expert_w, L1_ffn_expert_b)
    x = _from_tokens(t, x)
    return x

_drawn_inputs = setup_inputs


def setup_inputs(seed=0):
    import zlib

    import numpy as np

    out = dict(_drawn_inputs(seed))
    spreads = {'L0_conv_s_ll': (1.0, 0.2),
     'L0_conv_s_lh': (0.5, 0.6),
     'L0_conv_s_hl': (0.5, 0.6),
     'L0_conv_s_hh': (0.0, 0.8),
     'L0_conv_b1': (0.0, 0.467),
     'L0_conv_b2': (0.0, 0.1),
     'L0_ffn_gate_b': (0.0, 0.8),
     'L1_ffn_router_b': (0.0, 0.1),
     'L1_ffn_expert_b': (0.0, 0.8)}
    factors = {'L0_ffn_gate_w': 8.0, 'L0_ffn_weight1': 8.0, 'L0_ffn_weight2': 8.0}
    for name, (base, spread) in spreads.items():
        noise = np.random.default_rng([zlib.crc32(name.encode()), seed]).standard_normal(out[name].shape)
        drawn = base * np.exp(spread * noise) if base else spread * noise
        out[name] = jnp.asarray(drawn.astype(out[name].dtype))
    for name, factor in factors.items():
        out[name] = (out[name] * factor).astype(out[name].dtype)
    return out
```

```python
import numpy as np

import concourse.bass as bass
from concourse import mybir
from contextlib import ExitStack

F32 = mybir.dt.float32
F32R = mybir.dt.float32r
BF16 = mybir.dt.bfloat16
U32 = mybir.dt.uint32
ACT = mybir.ActivationFunctionType
ALU = mybir.AluOpType
AXX = mybir.AxisListType.X

P = 128
B, C, H, W = 4, 64, 128, 128
HP, WP = H // 2, W // 2
JR = 4
N = JR * W
NG = HP // JR
CHUNKS = NG * B
SLOT = B * HP * WP
TOK = HP * W
E0, HID, K0 = 32, 256, 8
E1 = 8
TAPS = 9
ND = 5
PAD = 8
SENTINEL = 2.0
EPS_C, EPS_T = 1e-6, 1e-5


def back(k, u, steps, unroll):
    return k + (u - steps) // unroll, (u - steps) % unroll


def valid(k, u, unroll, total):
    return not isinstance(k, int) or 0 <= k * unroll + u < total


def wait(engine, sem, count):
    if not isinstance(count, int) or count > 0:
        engine.wait_ge(sem, count)


def settle(engine, sem):
    engine.sem_inc(sem, 1)


def pipelined(engine, step, total, unroll, lag, tail=0):
    for u in range(unroll):
        step(0, u)
    with engine.Fori(1, total // unroll - tail) as k:
        for u in range(unroll):
            step(k, u)
    for t in range(total - tail * unroll, total + lag):
        step(t // unroll, t % unroll)


LN_EXP_SET = 6


def load_ln_exp(nc, act):
    act.add_instruction(mybir.InstLoadActFuncSet(
        act_func_set_id=LN_EXP_SET, name=nc.get_next_instruction_name(), engine=mybir.EngineType.Activation, ins=[], outs=[]))


class Chain:

    def __init__(self, engine, sem, base=0, count=0):
        self.engine, self.sem, self.base, self.count = engine, sem, base, count

    def __call__(self, instruction):
        self.count += 1
        instruction.then_inc(self.sem, 1)
        self.engine.wait_ge(self.sem, self.base + self.count)


def bcast(ap, axis, count):
    out = ap.unsqueeze(axis)
    shape = list(out.shape)
    shape[axis] = count
    return out.to_broadcast(shape)


class Mem:

    def __init__(self, nc, ctx, phase):
        self.nc, self.ctx, self.phase = nc, ctx, phase

    def sb(self, name, shape, dt=F32):
        return self.ctx.enter_context(self.nc.sbuf_tensor(f"{self.phase}_{name}", shape, dt))

    def ps(self, name, shape=(P, 512), dt=F32):
        return self.ctx.enter_context(self.nc.psum_tensor(f"{self.phase}_{name}", list(shape), dt))

    def sem(self, name):
        return self.ctx.enter_context(self.nc.semaphore(f"{self.phase}_{name}"))

    def sems(self, name, n):
        return [self.sem(f"{name}{i}") for i in range(n)]


class Views:

    def __init__(self, tensor, at):
        self.tensor, self.at = tensor, at

    def take(self, *shape, parts=P):
        n = int(np.prod(shape))
        v = self.tensor[0:parts, self.at:self.at + n]
        self.at += n
        assert self.at <= self.tensor.shape[1]
        if len(shape) == 1:
            return v
        names = "abcde"[:len(shape)]
        sizes = {c: s for c, s in zip(names, shape)}
        return v.rearrange(f"p ({' '.join(names)}) -> p {' '.join(names)}", **sizes)


def setup_block0(nc, g, a):
    with ExitStack() as ctx:
        m = Mem(nc, ctx, "su")
        w1n = m.sb("w1n", [C, 4, 2, C])
        w2n = m.sb("w2n", [P, 4, C + 1])
        s4 = m.sb("s4", [P, 4])
        gwn = m.sb("gwn", [E0, 2, C])
        es = m.sb("es", [P, 4])
        sg = m.sb("sg", [P, 1])
        tmp = m.sb("tmp", [P, 4, C + 1])
        bcomb = m.sb("bcomb", [P, 2, C + 1])
        gtb = m.sb("gtb", [P, 2 * E0])
        psT = m.ps("psT")
        psG = m.ps("psG")
        psB = m.ps("psB")
        loaded, ident_ready, const_ready = m.sem("loaded"), m.sem("ident"), m.sem("const")
        turned, gate_blocks, gate_centred = m.sem("turned"), m.sem("gblk"), m.sem("gcen")
        rec_ready, rec_turned, exp_ready, chain, done = (
            m.sem("rec"), m.sem("recT"), m.sem("es"), m.sem("chain"), m.sem("done"))
        NL = 2 * 8 + 1 + 4 + 1
        with nc.Block() as block:
            @block.sync
            def _(sp):
                def load(dst, src):
                    sp.dma_start(dst, src, allow_slow_non_contiguous=True).then_inc(loaded, 16)

                for h in range(2):
                    part = slice(h * C, h * C + C)
                    load(w1n[:, :, h], a["w1"].rearrange("o (j c) -> o j c", j=4))
                    load(gwn[:, h], a["gate_w"])
                    load(w2n[part, :, 0:C], a["w2"].rearrange("(j c) o -> c j o", j=4))
                    load(w2n[part, :, C:C + 1], a["b2"].rearrange("(j c o) -> c j o", j=4, o=1))
                    for j, s in enumerate(("s_ll", "s_lh", "s_hl", "s_hh")):
                        load(s4[part, j:j + 1], a[s].rearrange("(c o) -> c o", o=1))
                load(g.b1[:], a["b1"].rearrange("(c o) -> c o", o=1))
                for q in range(4):
                    load(g.gate_b[q * E0:q * E0 + E0, :], a["gate_b"].rearrange("(e o) -> e o", o=1))
                load(g.w2bias[:], a["weight2"][:, HID:HID + 1, :].rearrange("e h o -> e (h o)"))
                sp.dma_start(g.W1[0:C + 1], a["weight1"].rearrange("e d h -> d e h")
                             ).then_inc(g.experts_loaded, 16)
                for t in range(2):
                    sp.dma_start(g.W2[:, :, t, :], a["weight2"][:, t * P:t * P + P, :].rearrange(
                        "e p o -> p e o")).then_inc(g.experts_loaded, 16)
                sp.wait_ge(loaded, 16 * NL)

            @block.gpsimd
            def _(pool):
                pool.memset(g.ident, 0.0).then_inc(ident_ready, 1)
                pool.wait_ge(ident_ready, 1)
                pool.affine_select(out=g.ident, in_=g.ident, compare_op=ALU.not_equal, fill=1.0,
                                   base=0, pattern=[[-1, P]], channel_multiplier=1).then_inc(ident_ready, 1)

            @block.vector
            def _(dve):
                link = Chain(dve, chain)
                link(dve.memset(g.J[:], 0.0))
                dve.memset(g.J[0:C, 0:C], 1.0 / C)
                dve.memset(g.J[C:P, C:P], 1.0 / C)
                dve.memset(g.eps[:, 0:1], EPS_C)
                dve.memset(g.eps[:, 1:2], EPS_T)
                dve.memset(gtb[:], 0.0)
                dve.memset(g.D[:], 0.0)
                for low in g.lowS:
                    dve.memset(low[C:C + 1], 1.0)
                dve.memset(g.E[:, TOK:TOK + PAD], SENTINEL)
                dve.memset(sg[0:C], 1.0)
                link(dve.memset(sg[C:P], -1.0))
                dve.wait_ge(ident_ready, 2)
                dve.tensor_tensor(g.Cm[:], g.ident, g.J[:], ALU.subtract).then_inc(const_ready, 1)
                dve.wait_ge(loaded, 16 * NL)
                dve.scalar_tensor_tensor(tmp[:, 0], w2n[:, 1], sg[:], w2n[:, 0], ALU.mult, ALU.add)
                link(dve.scalar_tensor_tensor(tmp[:, 1], w2n[:, 3], sg[:], w2n[:, 2], ALU.mult, ALU.add))
                dve.tensor_tensor(tmp[:, 2], tmp[:, 0], tmp[:, 1], ALU.add)
                link(dve.tensor_tensor(tmp[:, 3], tmp[:, 0], tmp[:, 1], ALU.subtract))
                dve.tensor_scalar(bcomb[:], tmp[:, 2:4], 0.5, None, ALU.mult).then_inc(rec_ready, 1)
                dve.wait_ge(turned, 1)
                for h in range(2):
                    last = dve.tensor_copy(gtb[h * C:h * C + C, h * E0:h * E0 + E0],
                                           psG[h * C:h * C + C, 0:E0])
                last.then_inc(gate_blocks, 1)
                dve.wait_ge(exp_ready, 1)
                link(dve.tensor_scalar(es[:], es[:], 0.5, None, ALU.mult))
                dve.tensor_tensor(es[:, 1:2], es[:, 1:2], sg[:], ALU.mult)
                link(dve.tensor_tensor(es[:, 3:4], es[:, 3:4], sg[:], ALU.mult))
                T = psT[:, 0:4 * C].rearrange("p (j o) -> p j o", j=4)
                dve.tensor_scalar(tmp[:, 0, 0:C], T[:, 0], es[:, 0:1], None, ALU.mult)
                link(dve.tensor_scalar(tmp[:, 1, 0:C], T[:, 2], es[:, 2:3], None, ALU.mult))
                dve.scalar_tensor_tensor(tmp[:, 2, 0:C], T[:, 1], es[:, 1:2], tmp[:, 0, 0:C], ALU.mult, ALU.add)
                link(dve.scalar_tensor_tensor(tmp[:, 3, 0:C], T[:, 3], es[:, 3:4], tmp[:, 1, 0:C],
                                              ALU.mult, ALU.add))
                dve.tensor_tensor(g.Alow[:, 0], tmp[:, 2, 0:C], tmp[:, 3, 0:C], ALU.add)
                link(dve.tensor_tensor(g.Alow[:, 1], tmp[:, 2, 0:C], tmp[:, 3, 0:C], ALU.subtract))
                dve.wait_ge(rec_turned, 1)
                link(dve.tensor_copy(g.Brec[0:C + 1],
                                     psB[0:C + 1, 0:2 * P].rearrange("p (v c) -> p v c", v=2)))
                dve.wait_ge(gate_centred, 1)
                link(dve.tensor_copy(g.Gc, psG[:, 256:256 + 2 * E0]))

            @block.scalar
            def _(act):
                act.wait_ge(loaded, 16 * NL)
                act.activation(es[:], s4[:], ACT.Exp).then_inc(exp_ready, 1)

            @block.tensor
            def _(pe):
                pe.wait_ge(ident_ready, 2)
                pe.wait_ge(loaded, 16 * NL)
                for j in range(4):
                    pe.transpose(psT[:, j * C:j * C + C], w1n[:, j].rearrange("o h c -> o (h c)"), g.ident[0:C, 0:C])
                pe.transpose(psG[:, 0:E0], gwn[:].rearrange("e h c -> e (h c)"), g.ident[0:E0, 0:E0]).then_inc(turned, 1)
                pe.wait_ge(rec_ready, 1)
                for v in range(2):
                    last = pe.transpose(psB[0:C + 1, v * P:v * P + P], bcomb[:, v], g.ident)
                last.then_inc(rec_turned, 1)
                pe.wait_ge(const_ready, 1)
                pe.wait_ge(gate_blocks, 1)
                pe.matmul(psG[:, 256:256 + 2 * E0], g.Cm[:], gtb[:], start=True, stop=True,
                          ).then_inc(gate_centred, 1)


def wavelet_mixer(nc, g, a):
    U = 8
    S_VAR, S_LOW, S_REC, S_TOK, S_TVAR = 1, 2, 3, 4, 5
    AHEAD = 2
    LAG = S_TVAR + 1
    with ExitStack() as ctx:
        m = Mem(nc, ctx, "wm")
        xc = [m.ps("xc0"), m.ps("xc1")]
        vl, rec, tc, tt, lg, tv = (m.ps(n) for n in ("vl", "rec", "tc", "tt", "lg", "tv"))
        xin, x1_out, tok_out = m.sems("xin", U), m.sems("x1o", U), m.sems("tko", 4)
        s = {n: m.sem(n) for n in (
            "centred", "squared", "var", "lnv", "rstd", "normed", "low", "low_s", "rec", "x1",
            "tcentred", "tsquared", "tturned", "tcopied", "logits", "tvar", "tln", "trstd", "glog", "settled")}
        xr, sq, rr, nn, lowS, tsq, ts, trs = g.xr, g.sq, g.rr, g.nn, g.lowS, g.tsq, g.ts, g.trs
        x_src = a["x"].rearrange("b c (j t) w -> b t c j w", t=2)
        tok_dst = g.x1tok.rearrange("b j w x -> b w j x")
        with nc.Block() as block:
            @block.sync
            def _(sp):
                def load(k, u):
                    wait(sp, x1_out[u], k * 16)
                    settle(sp, s["settled"])
                    wait(sp, s["logits"], k * U + u - U + 1)
                    wait(sp, s["tturned"], k * U + u - U + 1)
                    rows = k * (JR * U // B) + (u // B) * JR
                    for t in range(2):
                        sp.dma_start(xr[u][t * C:t * C + C].rearrange("p (j w) -> p j w", j=JR),
                                     x_src[u % B, t][:, bass.ds(rows, JR), :]).then_inc(xin[u], 16)

                def step(k, u):
                    kk, uu = back(k, u, -AHEAD, U)
                    if valid(kk, uu, U, CHUNKS):
                        load(kk, uu)
                    k3, u3 = back(k, u, S_REC, U)
                    if valid(k3, u3, U, CHUNKS):
                        wait(sp, s["x1"], k3 * U + u3 + 1)
                        sp.dma_start(g.x1s[bass.ds(k3 * U + u3, 1)].rearrange("t p n -> p (t n)"),
                                     xr[u3]).then_inc(x1_out[u3], 16)
                    k4, u4 = back(k, u, S_TOK, U)
                    if valid(k4, u4, U, CHUNKS):
                        wait(sp, s["tcopied"], k4 * U + u4 + 1)
                        rows = k4 * (JR * U // B) + (u4 // B) * JR
                        sp.dma_start(tok_dst[u4 % B][:, bass.ds(rows, JR), :],
                                     ts[u4 % 4].rearrange("p (j x) -> p j x", j=JR)
                                     ).then_inc(tok_out[u4 % 4], 16)
                for u in range(AHEAD):
                    load(0, u)
                pipelined(sp, step, CHUNKS, U, LAG, tail=1)
                for u in range(U):
                    sp.wait_ge(x1_out[u], 16 * (CHUNKS // U))
                for u in range(4):
                    sp.wait_ge(tok_out[u], 16 * (CHUNKS // 4))

            @block.tensor
            def _(pe):
                def step(k, u):
                    c1, u1 = back(k, u, S_VAR, U)
                    if valid(c1, u1, U, CHUNKS):
                        n = c1 * U + u1
                        wait(pe, s["squared"], n + 1)
                        wait(pe, s["low_s"], n - 1)
                        wait(pe, s["lnv"], n)
                        pe.matmul(vl[:], g.J[:], sq[u1 % 2], start=True, stop=True).then_inc(s["var"], 1)
                    if valid(k, u, U, CHUNKS):
                        n = k * U + u
                        wait(pe, xin[u], k * 32 + 32)
                        wait(pe, s["normed"], n - 1)
                        pe.matmul(xc[u % 2][:], g.Cm[:], xr[u], start=True, stop=True
                                  ).then_inc(s["centred"], 1)
                    c3, u3 = back(k, u, S_REC, U)
                    if valid(c3, u3, U, CHUNKS):
                        n = c3 * U + u3
                        wait(pe, s["low_s"], n + 1)
                        wait(pe, s["x1"], n)
                        for v in range(2):
                            last = pe.matmul(rec[:, v * (N // 2):(v + 1) * (N // 2)], g.Brec[0:C + 1, v],
                                             lowS[u3 % 2], start=True, stop=True)
                        last.then_inc(s["rec"], 1)
                    c2, u2 = back(k, u, S_LOW, U)
                    if valid(c2, u2, U, CHUNKS):
                        n = c2 * U + u2
                        wait(pe, s["normed"], n + 1)
                        wait(pe, s["lnv"], n + 2 if not isinstance(n, int) else min(n + 2, CHUNKS))
                        nv = nn[u2 % 2].rearrange("p (q v) -> p v q", v=2)
                        for v in range(2):
                            last = pe.matmul(vl[0:C, 0:N // 2], g.Alow[:, v], nv[:, v],
                                             start=(v == 0), stop=(v == 1))
                        last.then_inc(s["low"], 1)
                    c4, u4 = back(k, u, S_TOK, U)
                    if valid(c4, u4, U, CHUNKS):
                        n = c4 * U + u4
                        wait(pe, s["x1"], n + 1)
                        wait(pe, s["tsquared"], n)
                        pe.matmul(tc[:], g.Cm[:], xr[u4], start=True, stop=True).then_inc(s["tcentred"], 1)
                        wait(pe, s["tcopied"], n)
                        for j in range(JR):
                            last = pe.transpose(tt[:, j * P:j * P + P], xr[u4][:, j * W:j * W + W], g.ident)
                        last.then_inc(s["tturned"], 1)
                    c5, u5 = back(k, u, S_TVAR, U)
                    if valid(c5, u5, U, CHUNKS):
                        n = c5 * U + u5
                        half = u5 % 2
                        wait(pe, s["tsquared"], n + 1)
                        if half == 0:
                            wait(pe, s["tln"], c5 * (U // 2) + u5 // 2)
                        pe.matmul(tv[half * C:half * C + C, :], g.J[:, C - E0:C + E0], tsq[u5 % 2],
                                  start=True, stop=True).then_inc(s["tvar"], 1)
                        if half == 0:
                            wait(pe, s["glog"], c5 * (U // 2) + u5 // 2)
                        pe.matmul(lg[half * C:half * C + C, :], g.Gc, xr[u5], start=True, stop=True
                                  ).then_inc(s["logits"], 1)
                pipelined(pe, step, CHUNKS, U, LAG)

            @block.scalar
            def _(act):
                load_ln_exp(nc, act)

                def step(k, u):
                    if valid(k, u, U, CHUNKS):
                        n = k * U + u
                        wait(act, s["centred"], n + 1)
                        wait(act, s["var"], n - 1)
                        act.activation(sq[u % 2], xc[u % 2][:], ACT.Square).then_inc(s["squared"], 1)
                    c1, u1 = back(k, u, S_VAR, U)
                    if valid(c1, u1, U, CHUNKS):
                        n = c1 * U + u1
                        wait(act, s["var"], n + 1)
                        wait(act, s["normed"], n - 1)
                        act.activation(rr[u1 % 2], vl[:], ACT.Ln, bias=g.eps[:, 0:1]).then_inc(s["lnv"], 1)
                        act.wait_ge(s["lnv"], n + 1)
                        act.activation(rr[u1 % 2], rr[u1 % 2], ACT.Exp, scale=-0.5).then_inc(s["rstd"], 1)
                    c2, u2 = back(k, u, S_LOW, U)
                    if valid(c2, u2, U, CHUNKS):
                        n = c2 * U + u2
                        wait(act, s["low"], n + 1)
                        wait(act, s["rec"], n - 1)
                        act.activation(lowS[u2 % 2][0:C], vl[0:C, 0:N // 2], ACT.Identity,
                                       bias=g.b1[:]).then_inc(s["low_s"], 1)
                    c4, u4 = back(k, u, S_TOK, U)
                    if valid(c4, u4, U, CHUNKS):
                        n = c4 * U + u4
                        wait(act, s["tcentred"], n + 1)
                        wait(act, s["tvar"], n - 1)
                        act.activation(tsq[u4 % 2], tc[:], ACT.Square).then_inc(s["tsquared"], 1)
                    c5, u5 = back(k, u, S_TVAR, U)
                    if valid(c5, u5, U, CHUNKS) and u5 % 2 == 1:
                        pair = c5 * (U // 2) + u5 // 2
                        wait(act, s["tvar"], 2 * pair + 2)
                        wait(act, s["glog"], pair)
                        act.activation(trs, tv[:], ACT.Ln, bias=g.eps[:, 1:2]).then_inc(s["tln"], 1)
                        act.wait_ge(s["tln"], pair + 1)
                        act.activation(trs, trs, ACT.Exp, scale=-0.5).then_inc(s["trstd"], 1)
                pipelined(act, step, CHUNKS, U, LAG)

            @block.vector
            def _(dve):
                def step(k, u):
                    c1, u1 = back(k, u, S_VAR, U)
                    if valid(c1, u1, U, CHUNKS):
                        n = c1 * U + u1
                        wait(dve, s["rstd"], n + 1)
                        wait(dve, s["low"], n - 1)
                        dve.tensor_tensor(nn[u1 % 2], xc[u1 % 2][:], rr[u1 % 2], ALU.mult
                                          ).then_inc(s["normed"], 1)
                    c3, u3 = back(k, u, S_REC, U)
                    if valid(c3, u3, U, CHUNKS):
                        n = c3 * U + u3
                        wait(dve, s["rec"], n + 1)
                        xv = xr[u3].rearrange("p (q v) -> p v q", v=2)
                        dve.tensor_tensor(xv, rec[:].rearrange("p (v q) -> p v q", v=2), xv, ALU.add
                                          ).then_inc(s["x1"], 1)
                    c4, u4 = back(k, u, S_TOK, U)
                    if valid(c4, u4, U, CHUNKS):
                        n = c4 * U + u4
                        wait(dve, s["tturned"], n + 1)
                        wait(dve, tok_out[u4 % 4], (c4 * 2 + u4 // 4) * 16)
                        dve.tensor_copy(ts[u4 % 4], tt[:]).then_inc(s["tcopied"], 1)
                    c5, u5 = back(k, u, S_TVAR, U)
                    if valid(c5, u5, U, CHUNKS) and u5 % 2 == 1:
                        pair = c5 * (U // 2) + u5 // 2
                        p = (u5 % B) // 2
                        wait(dve, s["trstd"], pair + 1)
                        wait(dve, s["logits"], 2 * pair + 2)
                        at = p * (TOK + PAD) + (c5 * (U // B) + u5 // B) * N
                        dve.tensor_tensor(g.E[:, bass.ds(at, N)], lg[:], trs, ALU.mult
                                          ).then_inc(s["glog"], 1)
                pipelined(dve, step, CHUNKS, U, LAG)


def expert_choice(nc, g, a):
    with ExitStack() as ctx:
        m = Mem(nc, ctx, "ec")
        v = Views(g.X, 0)
        e2 = [v.take(TOK + PAD), v.take(TOK + PAD)]
        v = Views(g.X, g.small_at)
        gath, xcg = v.take(2, K0, C), v.take(2, K0, C)
        sqg = gath
        mx, swapm, sel64, sele = v.take(2, 8), v.take(P), v.take(2 * E0), v.take(E0, B)
        own, oth, hpc, thr = v.take(2, 17), v.take(2, 17), v.take(1), v.take(K0)
        mg, nb, zt, rz, base = v.take(2), v.take(2), v.take(2), v.take(2), v.take(2)
        oT = v.take(2, 2, 2, E0)
        v.at -= 4 * K0 * K0
        cmp1, cmp2 = v.take(2, K0, K0), v.take(2, K0, K0)
        cnt, chosen, lst, lst2, wgt = (v.take(2, K0) for _ in range(5))
        jf = v.take(2, K0)
        mean, var, pooled = v.take(2, K0), v.take(2, K0), v.take(2, C)
        pT, hT = v.take(P), v.take(2, E0 * B)
        idx = m.sb("idx", [P, 2, K0], U32)
        jdx = m.sb("jdx", [P, 2, K0], U32)
        rows = m.sb("rows", [P, 2, K0], U32)
        psw, pso, psp, psh, pst = (m.ps(n) for n in ("psw", "pso", "psp", "psh", "pst"))
        chain, swap_ready, swapped, biased, exped, packed, swapped2, rows_ready, gathered = (
            m.sem(n) for n in ("chain", "swr", "sw", "nb", "exp", "pk", "sw2", "rows", "gath"))
        vln, vexp, pooled_r, poolT, pT_r, hid_r, hT_r, out_r, oT_r, outT_r, done = (
            m.sem(n) for n in ("vln", "vexp", "pool", "poolT", "pT", "hid", "hT", "out", "oT", "outT", "dn"))
        pair_of = [g.E[:, 0:TOK], g.E[:, TOK + PAD:2 * TOK + PAD]]
        padded = [g.E[:, 0:TOK + PAD], g.E[:, TOK:2 * TOK + PAD]]
        data_of = [e2[0][:, 0:TOK], e2[1][:, PAD:TOK + PAD]]
        with nc.Block() as block:
            @block.vector
            def _(dve):
                link = Chain(dve, chain)
                for q in range(4):
                    part = slice(q * E0, q * E0 + E0)
                    dve.memset(hpc[part], float(P * (q % 2)))
                    for p in range(2):
                        dve.memset(base[part, p:p + 1], float((2 * p + q // 2) * 2 * TOK + q % 2))
                    dve.tensor_copy(swapm[:, q * E0:q * E0 + E0], g.ident[:, (q ^ 1) * E0:(q ^ 1) * E0 + E0])
                for i in range(K0):
                    dve.memset(thr[:, i:i + 1], float(K0 - i))
                for b2 in range(2):
                    dve.tensor_tensor(sel64[:, b2 * E0:b2 * E0 + E0],
                                      g.ident[:, 2 * b2 * E0:2 * b2 * E0 + E0],
                                      g.ident[:, (2 * b2 + 1) * E0:(2 * b2 + 2) * E0], ALU.add)
                dve.tensor_copy(sele[0:E0], bcast(g.ident[0:E0, 0:E0], 2, B))
                dve.memset(pT[C:C + 1], 1.0)
                for p in range(2):
                    last = dve.max(out=mx[:, p], in_=pair_of[p])
                link(last)
                dve.tensor_copy(mg, mx[:, :, 0]).then_inc(swap_ready, 1)
                dve.wait_ge(swap_ready, 1)
                dve.wait_ge(swapped, 1)
                link(dve.tensor_tensor(mg, psw[:, 0:2], mg, ALU.max))
                link(dve.tensor_scalar(nb, mg, g.gate_b[:], -1.0, ALU.add, ALU.mult))
                dve.tensor_scalar(nb, nb, g.gate_b[:], None, ALU.add).then_inc(biased, 1)
                for p in range(2):
                    dve.wait_ge(exped, p + 1)
                    link(dve.max(out=own[:, p, 0:K0], in_=pair_of[p]))
                    link(dve.max_index(out=idx[:, p], in_max=own[:, p, 0:K0], in_values=pair_of[p]))
                dve.tensor_single_scalar(jdx[:], idx[:], 7, ALU.logical_shift_right)
                link(dve.tensor_copy(own[:, :, K0:2 * K0], idx[:]))
                link(dve.tensor_copy(jf, jdx[:]))
                for p in range(2):
                    last = dve.tensor_scalar(rows[:, p], own[:, p, K0:2 * K0], 2.0, base[:, p:p + 1],
                                             ALU.mult, ALU.add)
                last.then_inc(rows_ready, 1)
                link(dve.scalar_tensor_tensor(jf, jf, float(P), own[:, :, K0:2 * K0], ALU.mult, ALU.add))
                dve.tensor_scalar(own[:, :, K0:2 * K0], jf, hpc, None, ALU.add).then_inc(packed, 1)
                dve.wait_ge(packed, 1)
                dve.wait_ge(swapped2, 1)
                link(dve.tensor_copy(oth, pso[:, 0:34].rearrange("p (a b) -> p a b", a=2)))
                shape = [P, 2, K0, K0]
                mine = [own[:, :, i * K0:i * K0 + K0].unsqueeze(3).to_broadcast(shape) for i in range(2)]
                them = [oth[:, :, i * K0:i * K0 + K0].unsqueeze(2).to_broadcast(shape) for i in range(2)]
                dve.tensor_tensor(cmp1, them[0], mine[0], ALU.is_equal)
                link(dve.tensor_tensor(cmp2, them[1], mine[1], ALU.is_lt))
                link(dve.tensor_tensor(cmp1, cmp1, cmp2, ALU.mult))
                link(dve.tensor_tensor(cmp2, them[0], mine[0], ALU.is_gt))
                link(dve.tensor_tensor(cmp1, cmp1, cmp2, ALU.add))
                link(dve.tensor_reduce(cnt, cmp1, AXX, ALU.add))
                dve.tensor_tensor(zt, own[:, :, 16], oth[:, :, 16], ALU.add)
                link(dve.tensor_tensor(chosen, cnt, bcast(thr, 1, 2), ALU.is_lt))
                dve.reciprocal(rz, zt)
                dve.tensor_tensor(lst, chosen, own[:, :, 0:K0], ALU.mult)
                link(dve.tensor_scalar(lst2, chosen, -SENTINEL, SENTINEL, ALU.mult, ALU.add))
                dve.tensor_tensor(wgt, lst, bcast(rz, 2, K0), ALU.mult)
                link(dve.tensor_tensor(lst2, lst2, lst, ALU.add))
                for p in range(2):
                    link(dve.match_replace(out=e2[p], in_to_replace=lst2[:, p], in_values=padded[p],
                                           imm_value=0.0))
                for p in range(2):
                    dve.tensor_tensor(pair_of[p], pair_of[p], data_of[p], ALU.subtract).then_inc(done, 1)
                dve.wait_ge(gathered, 16 * 2 * K0)
                link(dve.tensor_reduce(mean, gath, AXX, ALU.add))
                link(dve.tensor_scalar(mean, mean, 1.0 / C, None, ALU.mult))
                link(dve.tensor_tensor(xcg, gath, bcast(mean, 3, C), ALU.subtract))
                link(dve.tensor_tensor(sqg, xcg, xcg, ALU.mult))
                link(dve.tensor_reduce(var, sqg, AXX, ALU.add))
                dve.tensor_scalar(var, var, 1.0 / C, None, ALU.mult).then_inc(vln, 1)
                dve.wait_ge(vexp, 2)
                link(dve.tensor_tensor(wgt, wgt, var, ALU.mult))
                link(dve.tensor_tensor(xcg, xcg, bcast(wgt, 3, C), ALU.mult))
                dve.tensor_reduce(pooled, xcg.rearrange("p a k c -> p a c k"), AXX, ALU.add
                                  ).then_inc(pooled_r, 1)
                dve.wait_ge(poolT, 1)
                dve.tensor_copy(pT[0:C], psp[0:C, 0:P]).then_inc(pT_r, 1)
                dve.wait_ge(out_r, 1)
                src = psp[0:C, 256:256 + E0 * B].rearrange("p (e a b) -> p a b e", e=E0, a=2)
                for h in range(2):
                    last = dve.tensor_copy(oT[0:C, :, :, h], src)
                last.then_inc(oT_r, 1)
                dve.wait_ge(outT_r, 1)
                for b in range(B):
                    p, b2 = divmod(b, 2)
                    for h in range(2):
                        q = slice((2 * b2 + h) * E0, (2 * b2 + h + 1) * E0)
                        last = dve.tensor_scalar(g.D[q, b, h * C:h * C + C], pst[q, p * C:p * C + C],
                                                 rz[q, p:p + 1], None, ALU.mult)
                last.then_inc(done, 1)
                dve.wait_ge(done, 3)

            @block.scalar
            def _(act):
                load_ln_exp(nc, act)
                act.wait_ge(biased, 1)
                for p in range(2):
                    act.activation(pair_of[p], pair_of[p], ACT.Exp, bias=nb[:, p:p + 1],
                                   accum_out=own[:, p, 16:17]).then_inc(exped, 1)
                act.wait_ge(vln, 1)
                act.activation(var, var, ACT.Ln, bias=g.eps[:, 1:2]).then_inc(vexp, 1)
                act.wait_ge(vexp, 1)
                act.activation(var, var, ACT.Exp, scale=-0.5).then_inc(vexp, 1)
                act.wait_ge(hid_r, 1)
                act.activation(hT, psh[:, 0:2 * E0 * B].rearrange("p (t n) -> p t n", t=2), ACT.Gelu
                               ).then_inc(hT_r, 1)

            @block.gpsimd
            def _(pool):
                pool.wait_ge(rows_ready, 1)
                for p in range(2):
                    for i in range(K0):
                        pool.indirect_dma_start(
                            out=gath[:, p, i, :], out_offset=None,
                            in_=g.x1tok.rearrange("b j w (h c) -> (b j w h) c", h=2),
                            in_offset=bass.IndirectOffsetOnAxis(ap=rows[:, p, i:i + 1], axis=0),
                        ).then_inc(gathered, 16)

            @block.tensor
            def _(pe):
                pe.wait_ge(swap_ready, 1)
                pe.matmul(psw[:, 0:2], swapm, mg, start=True, stop=True).then_inc(swapped, 1)
                pe.wait_ge(packed, 1)
                pe.matmul(pso[:, 0:34], swapm, own.rearrange("p a b -> p (a b)"), start=True, stop=True
                          ).then_inc(swapped2, 1)
                pe.wait_ge(pooled_r, 1)
                for p in range(2):
                    last = pe.matmul(psp[0:C, p * 2 * E0:(p + 1) * 2 * E0], pooled[:, p], sel64,
                                     start=True, stop=True)
                last.then_inc(poolT, 1)
                pe.wait_ge(pT_r, 1)
                pe.wait_ge(g.experts_loaded, 16 * 3)
                pooled_of = pT[0:C + 1].rearrange("p (b e) -> p e b", b=B)
                for e in range(E0):
                    for t in range(2):
                        at = (t * E0 + e) * B
                        last = pe.matmul(psh[:, at:at + B], g.W1[0:C + 1, e, t * P:t * P + P],
                                         pooled_of[:, e], start=True, stop=True)
                last.then_inc(hid_r, 1)
                pe.wait_ge(hT_r, 1)
                out = psp[0:C, 256:256 + E0 * B]
                pe.matmul(out, g.w2bias[:], sele[0:E0].rearrange("p e b -> p (e b)"),
                          start=True, stop=False, skip_group_check=True)
                for e in range(E0):
                    for t in range(2):
                        last = pe.matmul(out[:, e * B:e * B + B], g.W2[:, e, t, :], hT[:, t, e * B:e * B + B],
                                         start=False, stop=(e == E0 - 1 and t == 1), skip_group_check=True)
                last.then_inc(out_r, 1)
                pe.wait_ge(oT_r, 1)
                for p in range(2):
                    last = pe.transpose(pst[:, p * C:p * C + C], oT[0:C, p].rearrange("p b h e -> p (b h e)"),
                                        g.ident[0:C, 0:C])
                last.then_inc(outT_r, 1)


def apply_choice(nc, g, a):
    U = 4
    S_CEN, S_VAR = 1, 2
    AHEAD = 2
    LAG = S_VAR + 1
    with ExitStack() as ctx:
        m = Mem(nc, ctx, "ac")
        xr = [m.sb(f"xr{i}", [P, N]) for i in range(U)]
        sq = [m.sb(f"sq{i}", [P, N]) for i in range(2)]
        dl, xc, vv = ([m.ps(f"{n}{i}") for i in range(2)] for n in ("dl", "xc", "vv"))
        xin, x2_out = m.sems("xin", U), m.sems("x2o", U)
        s = {n: m.sem(n) for n in ("delta", "x2", "centred", "squared", "var", "lnv", "rstd", "normed",
                                     "settled")}
        Xv = g.X[:].rearrange("p (s n) -> p s n", s=2)
        with nc.Block() as block:
            @block.sync
            def _(sp):
                def load(k, u):
                    wait(sp, x2_out[u], k * 16)
                    settle(sp, s["settled"])
                    wait(sp, s["centred"], k * U + u - U + 1)
                    sp.dma_start(xr[u][:], g.x1s[bass.ds(k * U + u, 1)].rearrange("t p n -> p (t n)")
                                 ).then_inc(xin[u], 16)

                def step(k, u):
                    kk, uu = back(k, u, -AHEAD, U)
                    if valid(kk, uu, U, CHUNKS):
                        load(kk, uu)
                    if valid(k, u, U, CHUNKS):
                        wait(sp, s["x2"], k * U + u + 1)
                        sp.dma_start(g.x2s[bass.ds(k * U + u, 1)].rearrange("t p n -> p (t n)"),
                                     xr[u][:]).then_inc(x2_out[u], 16)
                for u in range(AHEAD):
                    load(0, u)
                pipelined(sp, step, CHUNKS, U, 0, tail=1)
                for u in range(U):
                    sp.wait_ge(x2_out[u], 16 * (CHUNKS // U))

            @block.tensor
            def _(pe):
                def step(k, u):
                    if valid(k, u, U, CHUNKS):
                        n = k * U + u
                        wait(pe, s["x2"], n - 1)
                        pe.matmul(dl[u % 2][:], g.D[:, u], g.E[:, bass.ds((u // 2) * (TOK + PAD) + k * N, N)],
                                  start=True, stop=True).then_inc(s["delta"], 1)
                    c1, u1 = back(k, u, S_CEN, U)
                    if valid(c1, u1, U, CHUNKS):
                        n = c1 * U + u1
                        wait(pe, s["x2"], n + 1)
                        wait(pe, s["normed"], n - 1)
                        src = xr[u1][:].rearrange("p (q v) -> p v q", v=2)
                        for h in range(2):
                            for v in range(2):
                                last = pe.matmul(xc[u1 % 2][v * C:v * C + C, h * (N // 2):(h + 1) * (N // 2)],
                                                 g.Cm[:, h * C:h * C + C], src[:, v], start=True, stop=True)
                        last.then_inc(s["centred"], 1)
                    c2, u2 = back(k, u, S_VAR, U)
                    if valid(c2, u2, U, CHUNKS):
                        n = c2 * U + u2
                        wait(pe, s["squared"], n + 1)
                        wait(pe, s["lnv"], n - 1)
                        pe.matmul(vv[u2 % 2][:], g.J[:], sq[u2 % 2][:], start=True, stop=True
                                  ).then_inc(s["var"], 1)
                pipelined(pe, step, CHUNKS, U, LAG)

            @block.scalar
            def _(act):
                load_ln_exp(nc, act)

                def step(k, u):
                    c1, u1 = back(k, u, S_CEN, U)
                    if valid(c1, u1, U, CHUNKS):
                        n = c1 * U + u1
                        wait(act, s["centred"], n + 1)
                        wait(act, s["normed"], n - 1)
                        act.activation(sq[u1 % 2][:], xc[u1 % 2][:], ACT.Square).then_inc(s["squared"], 1)
                    c2, u2 = back(k, u, S_VAR, U)
                    if valid(c2, u2, U, CHUNKS):
                        n = c2 * U + u2
                        wait(act, s["var"], n + 1)
                        act.activation(sq[u2 % 2][:], vv[u2 % 2][:], ACT.Ln, bias=g.eps[:, 0:1]
                                       ).then_inc(s["lnv"], 1)
                        act.wait_ge(s["lnv"], n + 1)
                        act.activation(sq[u2 % 2][:], sq[u2 % 2][:], ACT.Exp, scale=-0.5
                                       ).then_inc(s["rstd"], 1)
                pipelined(act, step, CHUNKS, U, LAG)

            @block.vector
            def _(dve):
                def step(k, u):
                    if valid(k, u, U, CHUNKS):
                        n = k * U + u
                        wait(dve, s["delta"], n + 1)
                        wait(dve, xin[u], k * 16 + 16)
                        dve.tensor_tensor(xr[u][:], dl[u % 2][:], xr[u][:], ALU.add).then_inc(s["x2"], 1)
                    c2, u2 = back(k, u, S_VAR, U)
                    if valid(c2, u2, U, CHUNKS):
                        n = c2 * U + u2
                        wait(dve, s["rstd"], n + 1)
                        at = u2 * HP * WP + c2 * (JR * WP)
                        dve.tensor_tensor(Xv[:, :, bass.ds(at, JR * WP)],
                                          xc[u2 % 2][:].rearrange("p (s n) -> p s n", s=2),
                                          sq[u2 % 2][:].rearrange("p (s n) -> p s n", s=2), ALU.mult
                                          ).then_inc(s["normed"], 1)
                pipelined(dve, step, CHUNKS, U, LAG)


def scan_weights(nc, g, a):
    with ExitStack() as ctx:
        m = Mem(nc, ctx, "sw")
        wn = [m.sb(f"wn{i}", [C, 2, C * TAPS]) for i in range(4)]
        wf = [m.sb(f"wf{i}", [P, TAPS, C]) for i in range(2)]
        ident = m.sb("id", [P, P])
        psa, psb = ([m.ps(f"{n}{i}") for i in range(2)] for n in ("a", "b"))
        loaded, idr, turned, copied, chain, done = (
            m.sem(n) for n in ("ld", "id", "tn", "cp", "ch", "dn"))
        pads = m.sem("pads")
        A8 = 8

        def blocks(t, pi):
            Tv = t.rearrange("p (d po c) -> p d po c", d=ND, po=2)
            rows = slice(pi * C, pi * C + C)
            if pi == 0:
                return [(Tv[rows, 0:5, 0, :], 0, 5), (Tv[rows, 1:5, 1, :], 1, 4)]
            return [(Tv[rows, 0:4, 0, :], 1, 4), (Tv[rows, 0:5, 1, :], 0, 5)]

        with nc.Block() as block:
            @block.sync
            def _(sp):
                for i, w in enumerate(("w_ud", "w_du", "w_lr", "w_rl")):
                    for h in range(2):
                        sp.dma_start(wn[i][:, h], a[w].rearrange("o c t -> o (c t)")).then_inc(loaded, 16)
                sp.wait_ge(loaded, 128)

            @block.tensor
            def _(pe):
                pe.wait_ge(loaded, 128)
                pe.wait_ge(idr, 1)
                for i in range(4):
                    wait(pe, copied, i - 1)
                    wv = wn[i][:].rearrange("o h (c t) -> o t (h c)", t=TAPS)
                    for t in range(TAPS):
                        dst = psa[i % 2][:, t * C:t * C + C] if t < A8 else psb[i % 2][:, 0:C]
                        last = pe.transpose(dst, wv[:, t], ident[0:C, 0:C])
                    last.then_inc(turned, 1)

            @block.scalar
            def _(act):
                for i in range(4):
                    act.wait_ge(turned, i + 1)
                    wait(act, done, i - 1)
                    act.activation(wf[i % 2][:, 0:A8], psa[i % 2][:].rearrange("p (t c) -> p t c", t=A8), ACT.Copy)
                    act.activation(wf[i % 2][:, A8], psb[i % 2][:, 0:C], ACT.Copy).then_inc(copied, 1)

            @block.vector
            def _(dve):
                link = Chain(dve, chain)
                dve.tensor_tensor(ident[:], g.Cm[:], g.J[:], ALU.add).then_inc(idr, 1)
                for t in (g.yh, g.yl):
                    dve.memset(t[:].bitcast(F32), 0.0).then_inc(pads, 1)
                for i in range(4):
                    for t in (g.Thi[i], g.Tlo[i]):
                        Tv = t[:].rearrange("p (d po c) -> p d po c", d=ND, po=2)
                        dve.memset(Tv[0:C, 0, 1, :].bitcast(F32), 0.0)
                        dve.memset(Tv[C:P, ND - 1, 0, :].bitcast(F32), 0.0)
                    dve.wait_ge(copied, i + 1)
                    for pi in range(2):
                        for dst, t0, n in blocks(g.Thi[i][:], pi):
                            last = dve.tensor_copy(dst, wf[i % 2][pi * C:pi * C + C, t0:t0 + 2 * n - 1:2, :])
                    link(last)
                    for pi in range(2):
                        his = blocks(g.Thi[i][:], pi)
                        for (dst, t0, n), (hi, _, _) in zip(blocks(g.Tlo[i][:], pi), his):
                            last = dve.tensor_tensor(dst, wf[i % 2][pi * C:pi * C + C, t0:t0 + 2 * n - 1:2, :],
                                                     hi.bitcast(F32), ALU.subtract)
                    last.then_inc(done, 1)
                dve.wait_ge(pads, 2)
                dve.wait_ge(done, 4)


def scan_pass(nc, g, i):
    vertical, reverse, turn = i < 2, i % 2 == 1, i == 1
    with ExitStack() as ctx:
        m = Mem(nc, ctx, f"s{i}")
        ps = [m.ps(f"ps{r}") for r in range(2)]
        hi_ready, full_ready, lo_ready, conv_done, turned, settled = (
            m.sem(n) for n in ("hi", "full", "lo", "conv", "turn", "settled"))
        Xv = g.X[:].rearrange("p (s b j w) -> p s b j w", s=2, b=B, j=HP)

        def line(j, slot):
            if vertical:
                return Xv[:, slot, :, bass.ds(j, 1), :].rearrange("p b j w -> p b (j w)")
            return Xv[:, slot, :, :, bass.ds(j, 1)].rearrange("p b j w -> p b (j w)")

        def place(k, r):
            return (63 - k, 1 - r) if reverse else (k, r)

        inner = slice(2, 2 + 64)
        with nc.Block() as block:
            @block.tensor
            def _(pe):
                def step(k, r):
                    n = 2 * k + r
                    out = ps[r][:, 0:B * 64].rearrange("p (b w) -> p b w", b=B)
                    pe.wait_ge(hi_ready, n)
                    for t in (g.Tlo[i], g.Thi[i]):
                        for d in range(ND):
                            pe.matmul(out, t[:, d * P:d * P + P], g.yh[:, :, d:d + 64],
                                      start=(t is g.Tlo[i] and d == 0), stop=False)
                    pe.wait_ge(lo_ready, n)
                    for d in range(ND):
                        last = pe.matmul(out, g.Thi[i][:, d * P:d * P + P], g.yl[:, :, d:d + 64],
                                         start=False, stop=(d == ND - 1))
                    last.then_inc(conv_done, 1)
                step(0, 1)
                with pe.Fori(1, 64) as k:
                    for r in range(2):
                        step(k, r)

            @block.vector
            def _(dve):
                def split(x, n):
                    dve.wait_ge(hi_ready, n + 1)
                    wait(dve, full_ready, n + (1 if turn else 0))
                    dve.tensor_tensor(g.yl[:, :, inner], x, g.yh[:, :, inner].bitcast(F32), ALU.subtract
                                      ).then_inc(lo_ready, 1)

                def step(k, r):
                    n = 2 * k + r
                    j, slot = place(k, r)
                    x = line(j, slot)
                    dve.wait_ge(conv_done, n)
                    settle(dve, settled)
                    conv = ps[r][:, 0:B * 64].rearrange("p (b w) -> p b w", b=B)
                    dve.scalar_tensor_tensor(g.yh[:, :, inner], conv, 0.0, x, ALU.max, ALU.add
                                             ).then_inc(hi_ready, 1)
                    full = x
                    if turn:
                        full = g.ybuf[slot][:]
                        wait(dve, turned, k)
                    dve.scalar_tensor_tensor(full, conv, 0.0, x, ALU.max, ALU.add
                                             ).then_inc(full_ready, 1)
                    split(full, n)

                j, slot = place(0, 0)
                x = line(j, slot)
                dve.tensor_copy(g.yh[:, :, inner], x).then_inc(hi_ready, 1)
                if turn:
                    dve.tensor_copy(g.ybuf[slot][:], x).then_inc(full_ready, 1)
                split(x, 0)
                step(0, 1)
                with dve.Fori(1, 64) as k:
                    for r in range(2):
                        step(k, r)

            if turn:
                @block.scalar
                def _(act):
                    def pair_of_rows(k):
                        act.wait_ge(full_ready, 2 * k + 2)
                        for h in range(2):
                            for v in range(2):
                                dst = Xv[h * C:h * C + C, v, :, bass.ds(63 - k, 1), :]
                                last = act.activation(dst.rearrange("p b j w -> p b (j w)"),
                                                      g.ybuf[h][v * C:v * C + C], ACT.Copy)
                        last.then_inc(turned, 1)
                    pair_of_rows(0)
                    with act.Fori(1, 64) as k:
                        pair_of_rows(k)

def top2_mixture(nc, g, a, y_out):
    PARTS = 3
    G2 = 2 * E1
    ROWS = PARTS * G2
    TILES = N // P
    GR = B * TILES * 2
    UNITS = E1 // 2 * B
    NEVER = -1.0e30
    with ExitStack() as ctx:
        m = Mem(nc, ctx, "tm")
        rt = m.sb("rt", [P, G2])
        rbias = m.sb("rbias", [P, E1])
        wexp = m.sb("wexp", [P, E1 // 2, C])
        bn, bb = m.sb("bn", [ROWS, C]), m.sb("bb", [ROWS, 2, C])
        bpart = [m.sb(f"bpart{i}", [ROWS, 2 * C], BF16) for i in range(PARTS)]
        r16, hmask = m.sb("r16", [ROWS, G2]), m.sb("hmask", [ROWS, 2])
        selb = m.sb("selb", [ROWS, G2, C], BF16)
        ident, identb = m.sb("ident", [P, P]), m.sb("identb", [P, P], BF16)
        rev = m.sb("rev", [P, E1])
        x2 = [m.sb(f"x2_{i}", [P, N]) for i in range(2)]
        yo = [m.sb(f"yo{i}", [P, N]) for i in range(2)]
        nS = [m.sb(f"nS{b}", [P, N]) for b in range(B)]
        nd = [[m.sb(f"nd{r}{b}", [P, 2, N]) for b in range(B)] for r in range(2)]
        sq = [m.sb(f"sq{i}", [P, N]) for i in range(2)]
        Z = [[m.sb(f"Z{i}{h}", [P, N]) for h in range(2)] for i in range(2)]
        L, EX, A_, F1, F2 = (m.sb(n, [P, GR, E1]) for n in ("L", "EX", "A", "F1", "F2"))
        m1 = m.sb("m1", [P, GR])
        gp = m.sb("gp", [P, B * TILES, PARTS, G2], BF16)
        gT = [m.sb(f"gT{i}", [ROWS, N], BF16) for i in range(2)]
        xc, po, pg = ([m.ps(f"{n}{i}") for i in range(2)] for n in ("xc", "po", "pg"))
        vv, pr = m.ps("vv"), m.ps("pr")
        logits_ps = pr[:, 0:B * TILES * G2]
        gates_ps = pr[0:ROWS, N // 2:N].bitcast(BF16)
        xin, y_st = m.sems("xin", 2), m.sems("yst", 2)
        nd_in = m.sems("nd", 2 * B)
        s = {n: m.sem(n) for n in (
            "x3", "centred", "squared", "var", "lnv", "rstd", "normed", "routed", "lread", "shifted",
            "exp", "gates", "turned", "gcopied", "bcast", "z", "zmm", "y",
            "pool_settled", "pe_settled")}
        chain, chain0, ld, prep, prep_done, idr = (
            m.sem(n) for n in ("chain", "chain0", "ld", "prep", "prepd", "idr"))
        Xv = g.X[:].rearrange("p (s n) -> p s n", s=2)
        x_dst = y_out.rearrange("b c (j t) w -> b t c j w", t=2)

        def xview(k, b):
            return Xv[:, :, bass.ds(b * HP * WP + k * (JR * WP), JR * WP)]

        def natural(t):
            return t.rearrange("p (j w v) -> p v j w", j=JR, v=2)

        def ordered(t):
            return t.rearrange("p (v j w) -> p v j w", v=2, j=JR)

        def nd_count(k, r):
            return (k - r) * 32 + 64

        def run(engine, step):
            step(0, 0, True, False)
            step(1, 1, True, True)
            with engine.Fori(1, NG // 2) as kk:
                for r in range(2):
                    step(kk * 2 + r, r, True, True)
            step(NG, 0, False, True)

        with nc.Block() as block:
            @block.sync
            def _(sp):
                def load(dst, src):
                    sp.dma_start(dst, src, allow_slow_non_contiguous=True).then_inc(ld, 16)
                for h in range(2):
                    load(wexp[h * C:h * C + C], a["expert_w"][h:E1:2].rearrange("p d c -> d p c"))
                for q in range(PARTS * 2):
                    load(bn[q * E1:q * E1 + E1], a["expert_b"])
                load(rbias[:], a["router_b"].rearrange("(o e) -> o e", o=1).to_broadcast([P, E1]))
                sp.wait_ge(prep, 1)
                for h in range(2):
                    load(rt[h * C:h * C + C, h * E1:h * E1 + E1], a["router_w"])

                def load_x2(k, b):
                    wait(sp, s["x3"], k * B + b - 1)
                    sp.dma_start(x2[b % 2][:], g.x2s[bass.ds(k * B + b, 1)].rearrange("t p n -> p (t n)")
                                 ).then_inc(xin[b % 2], 16)

                def store_y(k, b):
                    wait(sp, s["y"], k * B + b + 1)
                    for h in range(2):
                        sp.dma_start(x_dst[b, h][:, bass.ds(k * JR, JR), :],
                                     yo[b % 2][h * C:h * C + C].rearrange("p (j w) -> p j w", j=JR)
                                     ).then_inc(y_st[b % 2], 16)

                def step(k, more=True, stores=True):
                    for b in (2, 3):
                        load_x2(k, b)
                    if stores:
                        for b in (0, 1):
                            store_y(k - 1, b)
                    if more:
                        for b in (0, 1):
                            load_x2(k + 1, b)
                    if stores:
                        for b in (2, 3):
                            store_y(k - 1, b)
                for b in (0, 1):
                    load_x2(0, b)
                step(0, stores=False)
                step(1)
                with sp.Fori(1, NG // 2 - 1) as kk:
                    for r in range(2):
                        step(kk * 2 + r)
                step(NG - 2)
                step(NG - 1, more=False)
                for b in range(B):
                    store_y(NG - 1, b)
                for i in range(2):
                    sp.wait_ge(y_st[i], 16 * 2 * CHUNKS // 2)

            @block.gpsimd
            def _(pool):
                def step(k, r, norm, experts):
                    for b in range(B):
                        if norm:
                            wait(pool, s["normed"], k * B + b + 1)
                            wait(pool, s["z"], ((k - 2) * UNITS + (b + 1) * (UNITS // B)) * 2)
                            settle(pool, s["pool_settled"])
                            for h in range(2):
                                for half in range(2):
                                    pool.dma_start(nd[r][b][half * C:half * C + C, h, :],
                                                   nS[b][h * C:h * C + C]).then_inc(nd_in[r * B + b], 16)
                run(pool, step)

            @block.tensor
            def _(pe):
                pe.wait_ge(ld, 16 * (2 + PARTS * 2 + 1 + 2))
                pe.wait_ge(prep_done, 1)

                def centre(k, b):
                    wait(pe, s["x3"], k * B + b + 1)
                    wait(pe, s["normed"], k * B + b - 1)
                    pe.matmul(xc[b % 2][:].rearrange("p (v n) -> p v n", v=2), g.Cm[:], xview(k, b),
                              start=True, stop=True).then_inc(s["centred"], 1)

                def variance(k, b):
                    wait(pe, s["squared"], k * B + b + 1)
                    wait(pe, s["lnv"], k * B + b)
                    pe.matmul(vv[:], g.J[:], sq[b % 2][:], start=True, stop=True).then_inc(s["var"], 1)

                def route(k, b):
                    wait(pe, s["normed"], k * B + b + 1)
                    wait(pe, s["gcopied"], (k - 1) * B + (2, 3, 3, 4)[b])
                    if b == 0:
                        wait(pe, s["lread"], k)
                    for t in range(TILES):
                        at = (b * TILES + t) * G2
                        last = pe.matmul(logits_ps[:, at:at + G2], nS[b][:, t * P:t * P + P], rt[:],
                                         start=True, stop=True)
                    last.then_inc(s["routed"], 1)

                def turn_gates(k, b):
                    n = k * B + b
                    wait(pe, s["gates"], k + 1)
                    wait(pe, s["gcopied"], n)
                    if b == B - 1:
                        wait(pe, s["lread"], k + 1)
                    settle(pe, s["pe_settled"])
                    for t in range(TILES):
                        last = pe.transpose(gates_ps[:, t * P:t * P + P],
                                            gp[:, b * TILES + t].rearrange("p a e -> p (a e)"), identb[:])
                    last.then_inc(s["turned"], 1)

                def broadcast(k, q):
                    b, ep = divmod(q, E1 // 2)
                    for h in range(2):
                        u = (k * UNITS + q) * 2 + h
                        wait(pe, s["z"], u - 1)
                        if ep == 0:
                            wait(pe, s["gcopied"], k * B + b + 1)
                        at = h * E1 + 2 * ep
                        pe.matmul(pg[h][:], selb[:, at:at + 2].rearrange("p e c -> p (e c)"), gT[b % 2][:],
                                  start=True, stop=True).then_inc(s["bcast"], 1)

                def biases(k, b):
                    wait(pe, s["y"], k * B + b - 1)
                    for i in range(PARTS):
                        pe.matmul(po[b % 2][:], bpart[i][:], gT[b % 2][:], start=(i == 0), stop=False,
                                  skip_group_check=True)

                def experts_of(k, q):
                    b, ep = divmod(q, E1 // 2)
                    wait(pe, s["z"], (k * UNITS + q) * 2 + 2)
                    for h in range(2):
                        last = pe.matmul(po[b % 2][h * C:h * C + C, :], wexp[:, ep], Z[q % 2][h][:],
                                         start=False, stop=(ep == E1 // 2 - 1), skip_group_check=True)
                    last.then_inc(s["zmm"], 1)

                def step(k, r, norm, experts):
                    if experts:
                        turn_gates(k - 1, 0)
                        broadcast(k - 1, 0)
                        biases(k - 1, 0)
                    for q in range(UNITS):
                        if norm:
                            b = (q - 1) // 2
                            if q % 2 == 1 and 0 <= b - 2 < B:
                                route(k, b - 2)
                            if q % 2 == 1 and 0 <= b - 1 < B:
                                variance(k, b - 1)
                            if q % 2 == 1 and b < B:
                                centre(k, b)
                        if experts:
                            if q % 4 == 2 and q // 4 + 1 < B:
                                turn_gates(k - 1, q // 4 + 1)
                            if q + 1 < UNITS:
                                broadcast(k - 1, q + 1)
                                if (q + 1) % 4 == 0:
                                    biases(k - 1, (q + 1) // 4)
                            experts_of(k - 1, q)
                run(pe, step)

            @block.scalar
            def _(act):
                load_ln_exp(nc, act)

                def square(k, b):
                    wait(act, s["centred"], k * B + b + 1)
                    wait(act, s["normed"], k * B + b - 1)
                    act.activation(sq[b % 2][:], xc[b % 2][:], ACT.Square).then_inc(s["squared"], 1)

                def rstd(k, b):
                    n = k * B + b
                    wait(act, s["var"], n + 1)
                    act.activation(sq[b % 2][:], vv[:], ACT.Ln, bias=g.eps[:, 1:2]).then_inc(s["lnv"], 1)
                    act.wait_ge(s["lnv"], n + 1)
                    act.activation(sq[b % 2][:], sq[b % 2][:], ACT.Exp, scale=-0.5).then_inc(s["rstd"], 1)

                def copy_gates(k, b):
                    wait(act, s["turned"], k * B + b + 1)
                    wait(act, s["zmm"], (k * B + b - 1) * (E1 // 2))
                    act.activation(gT[b % 2][:], gates_ps, ACT.Copy).then_inc(s["gcopied"], 1)

                def step(k, r, norm, experts):
                    if experts:
                        copy_gates(k - 1, 0)
                    for q in range(UNITS):
                        if norm and q % 2 == 1:
                            b = (q - 1) // 2
                            if 0 <= b - 1 < B:
                                rstd(k, b - 1)
                            if b < B:
                                square(k, b)
                        if experts and q % 4 == 2 and q // 4 + 1 < B:
                            copy_gates(k - 1, q // 4 + 1)
                        if norm and q == 12:
                            wait(act, s["shifted"], k + 1)
                            act.activation(EX[:], L[:], ACT.Exp).then_inc(s["exp"], 1)
                run(act, step)

            @block.vector
            def _(dve):
                link = Chain(dve, chain0)
                link(dve.memset(rt[:], 0.0))
                dve.memset(selb[:, 0, 0:1], 0.0).then_inc(prep, 1)
                dve.tensor_tensor(ident[:], g.Cm[:], g.J[:], ALU.add)
                for e in range(E1):
                    dve.memset(rev[:, e:e + 1], float(E1 - e))
                link(dve.memset(m1[:], 0.0))
                dve.tensor_copy(identb[:], ident[:])
                link(dve.tensor_tensor(r16[:], ident[0:ROWS, 0:G2], ident[0:ROWS, G2:2 * G2], ALU.add))
                link(dve.tensor_tensor(r16[:], r16[:], ident[0:ROWS, 2 * G2:3 * G2], ALU.add))
                dve.tensor_copy(selb[:], bcast(r16[:], 2, C))
                link(dve.tensor_reduce(hmask[:], r16[:].rearrange("p (h e) -> p h e", h=2), AXX, ALU.add))
                dve.wait_ge(ld, 16 * (2 + PARTS * 2 + 1 + 2))
                link(dve.tensor_tensor(bb[:], bcast(bn[:], 1, 2), bcast(hmask[:], 2, C), ALU.mult))
                flat = bb[:].rearrange("p h c -> p (h c)")
                for i in range(PARTS):
                    link(dve.tensor_copy(bpart[i][:], flat))
                    if i < PARTS - 1:
                        link(dve.tensor_tensor(flat, flat, bpart[i][:], ALU.subtract))
                dve.memset(m1[:], 0.0).then_inc(prep_done, 1)
                dve.wait_ge(prep_done, 1)

                def x3(k, b):
                    n = k * B + b
                    wait(dve, xin[b % 2], (n // 2 if isinstance(n, int) else k * (B // 2) + b // 2) * 16 + 16)
                    xv = xview(k, b).rearrange("p v (j w) -> p v j w", j=JR)
                    dve.tensor_tensor(xv, natural(x2[b % 2][:]), xv, ALU.add).then_inc(s["x3"], 1)

                def norm_of(k, b, r):
                    n = k * B + b
                    wait(dve, s["rstd"], n + 1)
                    wait(dve, s["routed"], n + 1 - B)
                    if not isinstance(k, int) or k > 0:
                        wait(dve, nd_in[(1 - r) * B + b], nd_count(k - 1, 1 - r))
                    dve.tensor_tensor(nS[b][:], xc[b % 2][:], sq[b % 2][:], ALU.mult).then_inc(s["normed"], 1)

                def z_of(k, q, r):
                    b, ep = divmod(q, E1 // 2)
                    for h in range(2):
                        u = (k * UNITS + q) * 2 + h
                        wait(dve, s["bcast"], u + 1)
                        wait(dve, s["zmm"], k * UNITS + q - 1)
                        if ep == 0:
                            wait(dve, nd_in[r * B + b], nd_count(k, r))
                        dve.tensor_tensor(Z[q % 2][h][:], pg[h][:], nd[r][b][:, h, :], ALU.mult
                                          ).then_inc(s["z"], 1)

                def y_of(k, b):
                    n = k * B + b
                    wait(dve, s["zmm"], (n + 1) * (E1 // 2))
                    wait(dve, y_st[b % 2], (k * (B // 2) + b // 2) * 32)
                    dve.tensor_tensor(natural(yo[b % 2][:]), ordered(po[b % 2][:]),
                                      xview(k, b).rearrange("p v (j w) -> p v j w", j=JR), ALU.add
                                      ).then_inc(s["y"], 1)

                def gates(k, piece):
                    at = {0: 0, 1: 2, 2: 8, 3: 14}[piece]
                    link = Chain(dve, chain, base=k * 21, count=at)
                    wide = [P, GR, E1]

                    def over(t):
                        return t.unsqueeze(2).to_broadcast(wide)
                    revb = rev[:].unsqueeze(1).to_broadcast(wide)
                    if piece == 0:
                        wait(dve, s["routed"], (k + 1) * B)
                        wait(dve, s["exp"], k)
                        dve.tensor_tensor(L[:], logits_ps.rearrange("p (g e) -> p g e", e=E1),
                                          rbias[:].unsqueeze(1).to_broadcast(wide), ALU.add
                                          ).then_inc(s["lread"], 1)
                        dve.wait_ge(s["lread"], k + 1)
                        link(dve.tensor_reduce(m1[:], L[:], AXX, ALU.max))
                        dve.tensor_tensor(L[:], L[:], over(m1[:]), ALU.subtract).then_inc(s["shifted"], 1)
                        dve.wait_ge(s["shifted"], k + 1)
                        link(dve.tensor_single_scalar(A_[:], L[:], 0.0, ALU.is_equal))
                    elif piece == 1:
                        link(dve.tensor_tensor(A_[:], A_[:], revb, ALU.mult))
                        link(dve.tensor_reduce(m1[:], A_[:], AXX, ALU.max))
                        link(dve.tensor_tensor(F1[:], A_[:], over(m1[:]), ALU.is_equal))
                        dve.wait_ge(s["exp"], k + 1)
                        link(dve.scalar_tensor_tensor(L[:], F1[:], NEVER, L[:], ALU.mult, ALU.add))
                        link(dve.tensor_reduce(m1[:], L[:], AXX, ALU.max))
                        link(dve.tensor_tensor(A_[:], L[:], over(m1[:]), ALU.is_equal))
                    elif piece == 2:
                        link(dve.tensor_tensor(A_[:], A_[:], revb, ALU.mult))
                        link(dve.tensor_reduce(m1[:], A_[:], AXX, ALU.max))
                        link(dve.tensor_tensor(F2[:], A_[:], over(m1[:]), ALU.is_equal))
                        link(dve.tensor_tensor(F1[:], F1[:], F2[:], ALU.add))
                        link(dve.tensor_tensor(F1[:], F1[:], EX[:], ALU.mult))
                        link(dve.tensor_reduce(m1[:], F1[:], AXX, ALU.add))
                    else:
                        link(dve.reciprocal(m1[:], m1[:]))
                        link(dve.tensor_tensor(F1[:], F1[:], over(m1[:]), ALU.mult))
                        rest = F1[:].rearrange("p (t h) e -> p t (h e)", h=2)
                        link(dve.tensor_copy(gp[:, :, 0], rest))
                        link(dve.tensor_tensor(rest, rest, gp[:, :, 0], ALU.subtract))
                        link(dve.tensor_copy(gp[:, :, 1], rest))
                        link(dve.tensor_tensor(rest, rest, gp[:, :, 1], ALU.subtract))
                        link(dve.tensor_copy(gp[:, :, 2], rest))
                        dve.memset(m1[:], 0.0).then_inc(s["gates"], 1)

                def step(k, r, norm, experts):
                    for q in range(UNITS):
                        if norm and q % 2 == 0:
                            b = q // 2
                            if 0 <= b - 2 < B:
                                norm_of(k, b - 2, r)
                            if b < B:
                                x3(k, b)
                        if experts:
                            if q % 4 == 1 and q > 4:
                                y_of(k - 1, q // 4 - 1)
                            z_of(k - 1, q, 1 - r)
                        if norm and q >= 12:
                            gates(k, q - 12)
                    if experts:
                        y_of(k - 1, B - 1)
                run(dve, step)


class Shared:
    pass


def metaformer_kernel(nc, a, out):
    g = Shared()
    with ExitStack() as ctx:
        m = Mem(nc, ctx, "g")
        g.x1s = nc.dram_tensor("x1s", [CHUNKS, P, N], F32).ap()
        g.x1tok = nc.dram_tensor("x1tok", [B, HP, W, P], F32).ap()
        g.x2s = nc.dram_tensor("x2s", [CHUNKS, P, N], F32).ap()
        g.Cm, g.J = m.sb("Cm", [P, P]), m.sb("J", [P, P])
        g.eps = m.sb("eps", [P, 2])
        g.b1, g.gate_b, g.w2bias = m.sb("b1", [C, 1]), m.sb("gate_b", [P, 1]), m.sb("w2bias", [E0, C])
        g.experts_loaded = m.sem("experts_loaded")
        g.X = m.sb("X", [P, 2 * SLOT])
        v = Views(g.X, 0)
        g.xr = [v.take(N) for _ in range(8)]
        g.sq, g.rr, g.nn, g.tsq = ([v.take(N) for _ in range(2)] for _ in range(4))
        g.lowS = [v.take(N // 2, parts=C + 1) for _ in range(2)]
        g.ts = [v.take(N) for _ in range(4)]
        g.trs = v.take(N)
        v = Views(g.X, 2 * (TOK + PAD))
        g.W1, g.W2 = v.take(E0, HID), v.take(E0, 2, C)
        g.ident, g.Alow, g.Brec, g.Gc = v.take(P), v.take(2, C), v.take(2, P), v.take(2 * E0)
        g.small_at = v.at
        with ExitStack() as early:
            me = Mem(nc, early, "g")
            g.D = me.sb("D", [P, B, P])
            g.E = me.sb("E", [P, 2 * TOK + PAD])
            setup_block0(nc, g, a)
            wavelet_mixer(nc, g, a)
            expert_choice(nc, g, a)
            apply_choice(nc, g, a)
        with ExitStack() as mid:
            mm = Mem(nc, mid, "g")
            g.Thi = [mm.sb(f"Thi{i}", [P, ND * P], F32R) for i in range(4)]
            g.Tlo = [mm.sb(f"Tlo{i}", [P, ND * P], F32R) for i in range(4)]
            g.yh, g.yl = mm.sb("yh", [P, B, 68], F32R), mm.sb("yl", [P, B, 68], F32R)
            g.ybuf = [mm.sb(f"yb{r}", [P, B, 64]) for r in range(2)]
            scan_weights(nc, g, a)
            for i in range(4):
                scan_pass(nc, g, i)
        top2_mixture(nc, g, a, out)


_INPUTS = {"x": "x", "s_ll": "L0_conv_s_ll", "s_lh": "L0_conv_s_lh", "s_hl": "L0_conv_s_hl",
           "s_hh": "L0_conv_s_hh", "w1": "L0_conv_w1", "b1": "L0_conv_b1", "w2": "L0_conv_w2",
           "b2": "L0_conv_b2", "gate_w": "L0_ffn_gate_w", "gate_b": "L0_ffn_gate_b",
           "weight1": "L0_ffn_weight1", "weight2": "L0_ffn_weight2", "w_ud": "L1_conv_w_ud",
           "w_du": "L1_conv_w_du", "w_lr": "L1_conv_w_lr", "w_rl": "L1_conv_w_rl",
           "router_w": "L1_ffn_router_w", "router_b": "L1_ffn_router_b",
           "expert_w": "L1_ffn_expert_w", "expert_b": "L1_ffn_expert_b"}


def kernel(**inputs):
    import concourse.bacc as bacc
    from concourse.bass_utils import run_bass_kernel_spmd

    nc = bacc.Bacc("TRN2", target_bir_lowering=False, num_devices=1)
    arrays, args = {}, {}
    for short, name in _INPUTS.items():
        arr = np.ascontiguousarray(inputs[name])
        arrays[f"in_{name}"] = arr
        args[short] = nc.dram_tensor(f"in_{name}", arr.shape, mybir.dt.from_np(arr.dtype),
                                     kind="ExternalInput").ap()
    y = nc.dram_tensor("y", (B, C, H, W), F32, kind="ExternalOutput").ap()
    metaformer_kernel(nc, args, y)
    return run_bass_kernel_spmd(nc, [arrays], core_ids=[0]).results[0]["y"]
```

```python
import numpy as np

import concourse.bass as bass
from concourse import mybir
from contextlib import ExitStack

F32 = mybir.dt.float32
F32R = mybir.dt.float32r
BF16 = mybir.dt.bfloat16
U32 = mybir.dt.uint32
ACT = mybir.ActivationFunctionType
ALU = mybir.AluOpType
AXX = mybir.AxisListType.X

P = 128
B, C, H, W = 4, 64, 128, 128
HP, WP = H // 2, W // 2
JR = 4
N = JR * W
NG = HP // JR
CHUNKS = NG * B
SLOT = B * HP * WP
TOK = HP * W
E0, HID, K0 = 32, 256, 8
E1 = 8
TAPS = 9
ND = 5
PAD = 8
SENTINEL = 2.0
EPS_C, EPS_T = 1e-6, 1e-5


def back(k, u, steps, unroll):
    return k + (u - steps) // unroll, (u - steps) % unroll


def valid(k, u, unroll, total):
    return not isinstance(k, int) or 0 <= k * unroll + u < total


def wait(engine, sem, count):
    if not isinstance(count, int) or count > 0:
        engine.wait_ge(sem, count)


def settle(engine, sem):
    engine.sem_inc(sem, 1)


def pipelined(engine, step, total, unroll, lag, tail=0, head=1):
    for t in range(head * unroll):
        step(t // unroll, t % unroll)
    with engine.Fori(head, total // unroll - tail) as k:
        for u in range(unroll):
            step(k, u)
    for t in range(total - tail * unroll, total + lag):
        step(t // unroll, t % unroll)


LN_EXP_SET = 6


def load_ln_exp(nc, act):
    act.add_instruction(mybir.InstLoadActFuncSet(
        act_func_set_id=LN_EXP_SET, name=nc.get_next_instruction_name(), engine=mybir.EngineType.Activation, ins=[], outs=[]))


class Chain:

    def __init__(self, engine, sem, base=0, count=0):
        self.engine, self.sem, self.base, self.count = engine, sem, base, count

    def __call__(self, instruction):
        self.count += 1
        instruction.then_inc(self.sem, 1)
        self.engine.wait_ge(self.sem, self.base + self.count)


def bcast(ap, axis, count):
    out = ap.unsqueeze(axis)
    shape = list(out.shape)
    shape[axis] = count
    return out.to_broadcast(shape)


class Mem:

    def __init__(self, nc, ctx, phase):
        self.nc, self.ctx, self.phase = nc, ctx, phase

    def sb(self, name, shape, dt=F32):
        return self.ctx.enter_context(self.nc.sbuf_tensor(f"{self.phase}_{name}", shape, dt))

    def ps(self, name, shape=(P, 512), dt=F32):
        return self.ctx.enter_context(self.nc.psum_tensor(f"{self.phase}_{name}", list(shape), dt))

    def sem(self, name):
        return self.ctx.enter_context(self.nc.semaphore(f"{self.phase}_{name}"))

    def sems(self, name, n):
        return [self.sem(f"{name}{i}") for i in range(n)]


class Views:

    def __init__(self, tensor, at):
        self.tensor, self.at = tensor, at

    def take(self, *shape, parts=P):
        n = int(np.prod(shape))
        v = self.tensor[0:parts, self.at:self.at + n]
        self.at += n
        assert self.at <= self.tensor.shape[1]
        if len(shape) == 1:
            return v
        names = "abcde"[:len(shape)]
        sizes = {c: s for c, s in zip(names, shape)}
        return v.rearrange(f"p ({' '.join(names)}) -> p {' '.join(names)}", **sizes)


def setup_block0(nc, g, a):
    with ExitStack() as ctx:
        m = Mem(nc, ctx, "su")
        w1n = m.sb("w1n", [C, 4, 2, C])
        w2n = m.sb("w2n", [P, 4, C + 1])
        s4 = m.sb("s4", [P, 4])
        gwn = m.sb("gwn", [E0, 2, C])
        es = m.sb("es", [P, 4])
        sg = m.sb("sg", [P, 1])
        tmp = m.sb("tmp", [P, 4, C + 1])
        bcomb = m.sb("bcomb", [P, 2, C + 1])
        gtb = m.sb("gtb", [P, 2 * E0])
        psT = m.ps("psT")
        psG = m.ps("psG")
        psB = m.ps("psB")
        loaded, ident_ready, const_ready = m.sem("loaded"), m.sem("ident"), m.sem("const")
        turned, gate_blocks, gate_centred = m.sem("turned"), m.sem("gblk"), m.sem("gcen")
        rec_ready, rec_turned, exp_ready, chain, done = (
            m.sem("rec"), m.sem("recT"), m.sem("es"), m.sem("chain"), m.sem("done"))
        NL = 2 * 8 + 1 + 4 + 1
        with nc.Block() as block:
            @block.sync
            def _(sp):
                def load(dst, src):
                    sp.dma_start(dst, src, allow_slow_non_contiguous=True).then_inc(loaded, 16)

                for h in range(2):
                    part = slice(h * C, h * C + C)
                    load(w1n[:, :, h], a["w1"].rearrange("o (j c) -> o j c", j=4))
                    load(gwn[:, h], a["gate_w"])
                    load(w2n[part, :, 0:C], a["w2"].rearrange("(j c) o -> c j o", j=4))
                    load(w2n[part, :, C:C + 1], a["b2"].rearrange("(j c o) -> c j o", j=4, o=1))
                    for j, s in enumerate(("s_ll", "s_lh", "s_hl", "s_hh")):
                        load(s4[part, j:j + 1], a[s].rearrange("(c o) -> c o", o=1))
                load(g.b1[:], a["b1"].rearrange("(c o) -> c o", o=1))
                for q in range(4):
                    load(g.gate_b[q * E0:q * E0 + E0, :], a["gate_b"].rearrange("(e o) -> e o", o=1))
                load(g.w2bias, a["weight2"][:, HID:HID + 1, :].rearrange("e h o -> e (h o)"))
                sp.dma_start(g.W1[0:C + 1], a["weight1"].rearrange("e d h -> d e h")
                             ).then_inc(g.experts_loaded, 16)
                for t in range(2):
                    sp.dma_start(g.W2[:, :, t, :], a["weight2"][:, t * P:t * P + P, :].rearrange(
                        "e p o -> p e o")).then_inc(g.experts_loaded, 16)
                sp.wait_ge(loaded, 16 * NL)

            @block.gpsimd
            def _(pool):
                pool.memset(g.ident, 0.0).then_inc(ident_ready, 1)
                pool.wait_ge(ident_ready, 1)
                pool.affine_select(out=g.ident, in_=g.ident, compare_op=ALU.not_equal, fill=1.0,
                                   base=0, pattern=[[-1, P]], channel_multiplier=1).then_inc(ident_ready, 1)

            @block.vector
            def _(dve):
                link = Chain(dve, chain)
                link(dve.memset(g.J[:], 0.0))
                dve.memset(g.J[0:C, 0:C], 1.0 / C)
                dve.memset(g.J[C:P, C:P], 1.0 / C)
                dve.memset(g.eps[:, 0:1], EPS_C)
                dve.memset(g.eps[:, 1:2], EPS_T)
                dve.memset(gtb[:], 0.0)
                for low in g.lowS:
                    dve.memset(low[C:C + 1], 1.0)
                dve.memset(g.E[:, TOK:TOK + PAD], SENTINEL)
                dve.memset(sg[0:C], 1.0)
                link(dve.memset(sg[C:P], -1.0))
                dve.wait_ge(ident_ready, 2)
                dve.tensor_tensor(g.Cm[:], g.ident, g.J[:], ALU.subtract).then_inc(const_ready, 1)
                dve.wait_ge(loaded, 16 * NL)
                dve.scalar_tensor_tensor(tmp[:, 0], w2n[:, 1], sg[:], w2n[:, 0], ALU.mult, ALU.add)
                link(dve.scalar_tensor_tensor(tmp[:, 1], w2n[:, 3], sg[:], w2n[:, 2], ALU.mult, ALU.add))
                dve.tensor_tensor(tmp[:, 2], tmp[:, 0], tmp[:, 1], ALU.add)
                link(dve.tensor_tensor(tmp[:, 3], tmp[:, 0], tmp[:, 1], ALU.subtract))
                dve.tensor_scalar(bcomb[:], tmp[:, 2:4], 0.5, None, ALU.mult).then_inc(rec_ready, 1)
                dve.wait_ge(turned, 1)
                for h in range(2):
                    last = dve.tensor_copy(gtb[h * C:h * C + C, h * E0:h * E0 + E0],
                                           psG[h * C:h * C + C, 0:E0])
                last.then_inc(gate_blocks, 1)
                dve.wait_ge(exp_ready, 1)
                link(dve.tensor_scalar(es[:], es[:], 0.5, None, ALU.mult))
                dve.tensor_tensor(es[:, 1:2], es[:, 1:2], sg[:], ALU.mult)
                link(dve.tensor_tensor(es[:, 3:4], es[:, 3:4], sg[:], ALU.mult))
                T = psT[:, 0:4 * C].rearrange("p (j o) -> p j o", j=4)
                dve.tensor_scalar(tmp[:, 0, 0:C], T[:, 0], es[:, 0:1], None, ALU.mult)
                link(dve.tensor_scalar(tmp[:, 1, 0:C], T[:, 2], es[:, 2:3], None, ALU.mult))
                dve.scalar_tensor_tensor(tmp[:, 2, 0:C], T[:, 1], es[:, 1:2], tmp[:, 0, 0:C], ALU.mult, ALU.add)
                link(dve.scalar_tensor_tensor(tmp[:, 3, 0:C], T[:, 3], es[:, 3:4], tmp[:, 1, 0:C],
                                              ALU.mult, ALU.add))
                dve.tensor_tensor(g.Alow[:, 0], tmp[:, 2, 0:C], tmp[:, 3, 0:C], ALU.add)
                link(dve.tensor_tensor(g.Alow[:, 1], tmp[:, 2, 0:C], tmp[:, 3, 0:C], ALU.subtract))
                dve.wait_ge(rec_turned, 1)
                link(dve.tensor_copy(g.Brec[0:C + 1],
                                     psB[0:C + 1, 0:2 * P].rearrange("p (v c) -> p v c", v=2)))
                dve.wait_ge(gate_centred, 1)
                link(dve.tensor_copy(g.Gc, psG[:, 256:256 + 2 * E0]))

            @block.scalar
            def _(act):
                act.wait_ge(loaded, 16 * NL)
                act.activation(es[:], s4[:], ACT.Exp).then_inc(exp_ready, 1)

            @block.tensor
            def _(pe):
                pe.wait_ge(ident_ready, 2)
                pe.wait_ge(loaded, 16 * NL)
                for j in range(4):
                    pe.transpose(psT[:, j * C:j * C + C], w1n[:, j].rearrange("o h c -> o (h c)"), g.ident[0:C, 0:C])
                pe.transpose(psG[:, 0:E0], gwn[:].rearrange("e h c -> e (h c)"), g.ident[0:E0, 0:E0]).then_inc(turned, 1)
                pe.wait_ge(rec_ready, 1)
                for v in range(2):
                    last = pe.transpose(psB[0:C + 1, v * P:v * P + P], bcomb[:, v], g.ident)
                last.then_inc(rec_turned, 1)
                pe.wait_ge(const_ready, 1)
                pe.wait_ge(gate_blocks, 1)
                pe.matmul(psG[:, 256:256 + 2 * E0], g.Cm[:], gtb[:], start=True, stop=True,
                          ).then_inc(gate_centred, 1)


def wavelet_mixer(nc, g, a):
    U = 8
    S_VAR, S_LOW, S_REC, S_TOK, S_TVAR = 1, 2, 3, 4, 5
    AHEAD = 2
    LAG = S_TVAR + 1
    with ExitStack() as ctx:
        m = Mem(nc, ctx, "wm")
        xc = [m.ps("xc0"), m.ps("xc1")]
        vl, rec, tc, tt, lg, tv = (m.ps(n) for n in ("vl", "rec", "tc", "tt", "lg", "tv"))
        xin, x1_out, tok_out = m.sems("xin", U), m.sems("x1o", U), m.sems("tko", 4)
        s = {n: m.sem(n) for n in (
            "centred", "squared", "var", "lnv", "rstd", "normed", "low", "low_s", "rec", "x1",
            "high", "parts", "xhigh", "xparts", "x1high", "x1parts", "tcentred", "tsquared", "tturned", "tcopied", "logits", "tvar", "tln", "trstd", "glog")}
        xh, xl, x1h, x1l, sq_hi, sq_lo = (m.sb(n, [P, N], F32R) for n in ("xh", "xl", "x1h", "x1l", "sqh", "sql"))
        Jr, Cmr, exact_ready = m.sb("Jr", [P, P], F32R), m.sb("Cmr", [P, P], F32R), m.sem("exact")
        xr, sq, rr, nn, lowS, tsq, ts, trs = g.xr, g.sq, g.rr, g.nn, g.lowS, g.tsq, g.ts, g.trs
        x_src = a["x"].rearrange("b c (j t) w -> b t c j w", t=2)
        tok_dst = g.x1tok.rearrange("b j w x -> b w j x")
        with nc.Block() as block:
            @block.sync
            def _(sp):
                def load(k, u):
                    wait(sp, x1_out[u], k * 16)
                    settle(sp, g.settled)
                    wait(sp, s["logits"], k * U + u - U + 1)
                    wait(sp, s["tturned"], k * U + u - U + 1)
                    rows = k * (JR * U // B) + (u // B) * JR
                    for t in range(2):
                        sp.dma_start(xr[u][t * C:t * C + C].rearrange("p (j w) -> p j w", j=JR),
                                     x_src[u % B, t][:, bass.ds(rows, JR), :]).then_inc(xin[u], 16)

                def step(k, u):
                    kk, uu = back(k, u, -AHEAD, U)
                    if valid(kk, uu, U, CHUNKS):
                        load(kk, uu)
                    k3, u3 = back(k, u, S_REC, U)
                    if valid(k3, u3, U, CHUNKS):
                        wait(sp, s["x1"], k3 * U + u3 + 1)
                        sp.dma_start(g.x1s[bass.ds(k3 * U + u3, 1)].rearrange("t p n -> p (t n)"),
                                     xr[u3]).then_inc(x1_out[u3], 16)
                    k4, u4 = back(k, u, S_TOK, U)
                    if valid(k4, u4, U, CHUNKS):
                        wait(sp, s["tcopied"], k4 * U + u4 + 1)
                        rows = k4 * (JR * U // B) + (u4 // B) * JR
                        sp.dma_start(tok_dst[u4 % B][:, bass.ds(rows, JR), :],
                                     ts[u4 % 4].rearrange("p (j x) -> p j x", j=JR)
                                     ).then_inc(tok_out[u4 % 4], 16)
                for u in range(AHEAD):
                    load(0, u)
                pipelined(sp, step, CHUNKS, U, LAG, tail=1)
                for u in range(U):
                    sp.wait_ge(x1_out[u], 16 * (CHUNKS // U))
                for u in range(4):
                    sp.wait_ge(tok_out[u], 16 * (CHUNKS // 4))

            @block.tensor
            def _(pe):
                pe.wait_ge(exact_ready, 1)
                def step(k, u):
                    c3, u3 = back(k, u, S_REC, U)
                    if valid(c3, u3, U, CHUNKS):
                        n = c3 * U + u3
                        wait(pe, s["low_s"], n + 1)
                        wait(pe, s["x1"], n)
                        for v in range(2):
                            last = pe.matmul(rec[:, v * (N // 2):(v + 1) * (N // 2)], g.Brec[0:C + 1, v],
                                             lowS[u3 % 2], start=True, stop=True)
                        last.then_inc(s["rec"], 1)
                    c5, u5 = back(k, u, S_TVAR, U)
                    if valid(c5, u5, U, CHUNKS) and u5 % 2 == 1:
                        pair = c5 * (U // 2) + u5 // 2
                        wait(pe, s["tsquared"], 2 * pair + 2)
                        wait(pe, s["tln"], pair)
                        for half in range(2):
                            last = pe.matmul(tv[half * C:half * C + C, :], g.J[:, C - E0:C + E0],
                                             tsq[half], start=True, stop=True)
                        last.then_inc(s["tvar"], 2)
                        wait(pe, s["glog"], pair)
                        for half in range(2):
                            last = pe.matmul(lg[half * C:half * C + C, :], g.Gc, xr[u5 - 1 + half],
                                             start=True, stop=True)
                        last.then_inc(s["logits"], 2)
                    c4, u4 = back(k, u, S_TOK, U)
                    if valid(c4, u4, U, CHUNKS):
                        n = c4 * U + u4
                        wait(pe, s["x1parts"], n + 1)
                        wait(pe, s["tsquared"], n)
                        pe.matmul(tc[:], Cmr[:], x1h[:], start=True, stop=False)
                        pe.matmul(tc[:], Cmr[:], x1l[:], start=False, stop=True).then_inc(s["tcentred"], 1)
                        wait(pe, s["tcopied"], n)
                        for j in range(JR):
                            last = pe.transpose(tt[:, j * P:j * P + P], xr[u4][:, j * W:j * W + W], g.ident)
                        last.then_inc(s["tturned"], 1)
                    c2, u2 = back(k, u, S_LOW, U)
                    if valid(c2, u2, U, CHUNKS):
                        n = c2 * U + u2
                        wait(pe, s["normed"], n + 1)
                        wait(pe, s["lnv"], n + 1)
                        nv = nn[u2 % 2].rearrange("p (q v) -> p v q", v=2)
                        for v in range(2):
                            last = pe.matmul(vl[0:C, 0:N // 2], g.Alow[:, v], nv[:, v],
                                             start=(v == 0), stop=(v == 1))
                        last.then_inc(s["low"], 1)
                    if valid(k, u, U, CHUNKS):
                        n = k * U + u
                        wait(pe, s["xparts"], n + 1)
                        wait(pe, s["normed"], n - 1)
                        pe.matmul(xc[u % 2][:], Cmr[:], xh[:], start=True, stop=False)
                        pe.matmul(xc[u % 2][:], Cmr[:], xl[:], start=False, stop=True
                                  ).then_inc(s["centred"], 1)
                    c1, u1 = back(k, u, S_VAR, U)
                    if valid(c1, u1, U, CHUNKS):
                        n = c1 * U + u1
                        wait(pe, s["parts"], n + 1)
                        wait(pe, s["low_s"], n)
                        wait(pe, s["lnv"], n)
                        pe.matmul(vl[:], Jr[:], sq_hi[:], start=True, stop=False)
                        pe.matmul(vl[:], Jr[:], sq_lo[:], start=False, stop=True
                                  ).then_inc(s["var"], 1)
                pipelined(pe, step, CHUNKS, U, LAG)

            @block.scalar
            def _(act):
                load_ln_exp(nc, act)

                def step(k, u):
                    c5, u5 = back(k, u, S_TVAR, U)
                    if valid(c5, u5, U, CHUNKS) and u5 % 2 == 1:
                        pair = c5 * (U // 2) + u5 // 2
                        wait(act, s["tvar"], 2 * pair + 2)
                        wait(act, s["glog"], pair)
                        act.activation(trs, tv[:], ACT.Ln, bias=g.eps[:, 1:2]).then_inc(s["tln"], 1)
                        act.wait_ge(s["tln"], pair + 1)
                        act.activation(trs, trs, ACT.Exp, scale=-0.5).then_inc(s["trstd"], 1)
                    c4, u4 = back(k, u, S_TOK, U)
                    if valid(c4, u4, U, CHUNKS):
                        n = c4 * U + u4
                        wait(act, s["tcentred"], n + 1)
                        wait(act, s["tvar"], n - 1)
                        act.activation(tsq[u4 % 2], tc[:], ACT.Square).then_inc(s["tsquared"], 1)
                    c2, u2 = back(k, u, S_LOW, U)
                    if valid(c2, u2, U, CHUNKS):
                        n = c2 * U + u2
                        wait(act, s["low"], n + 1)
                        wait(act, s["rec"], n - 1)
                        act.activation(lowS[u2 % 2][0:C], vl[0:C, 0:N // 2], ACT.Identity,
                                       bias=g.b1[:]).then_inc(s["low_s"], 1)
                    if valid(k, u, U, CHUNKS):
                        n = k * U + u
                        wait(act, s["centred"], n + 1)
                        wait(act, s["var"], n - 1)
                        act.activation(sq[u % 2], xc[u % 2][:], ACT.Square).then_inc(s["squared"], 1)
                    c1, u1 = back(k, u, S_VAR, U)
                    if valid(c1, u1, U, CHUNKS):
                        n = c1 * U + u1
                        wait(act, s["var"], n + 1)
                        wait(act, s["normed"], n - 1)
                        act.activation(rr[u1 % 2], vl[:], ACT.Ln, bias=g.eps[:, 0:1]).then_inc(s["lnv"], 1)
                        act.wait_ge(s["lnv"], n + 1)
                        act.activation(rr[u1 % 2], rr[u1 % 2], ACT.Exp, scale=-0.5).then_inc(s["rstd"], 1)
                pipelined(act, step, CHUNKS, U, LAG)

            @block.gpsimd
            def _(pool):
                def low_part(c, u, source, high, low, ready, done):
                    wait(pool, s[ready], c * U + u + 1)
                    pool.tensor_tensor(low[:], source, high[:].bitcast(F32), ALU.subtract).then_inc(s[done], 1)

                def step(k, u):
                    c3, u3 = back(k, u, S_REC, U)
                    if valid(c3, u3, U, CHUNKS):
                        low_part(c3, u3, xr[u3], x1h, x1l, "x1high", "x1parts")
                    kk, uu = back(k, u, -1, U)
                    if valid(kk, uu, U, CHUNKS):
                        low_part(kk, uu, xr[uu], xh, xl, "xhigh", "xparts")
                    if valid(k, u, U, CHUNKS):
                        low_part(k, u, sq[u % 2], sq_hi, sq_lo, "high", "parts")
                low_part(0, 0, xr[0], xh, xl, "xhigh", "xparts")
                pipelined(pool, step, CHUNKS, U, LAG, tail=1)

            @block.vector
            def _(dve):
                dve.tensor_copy(Cmr[:], g.Cm[:])
                dve.tensor_copy(Jr[:], g.J[:]).then_inc(exact_ready, 1)

                def high_of_x(k, u):
                    wait(dve, xin[u], k * 32 + 32)
                    wait(dve, s["centred"], k * U + u)
                    dve.tensor_copy(xh[:], xr[u]).then_inc(s["xhigh"], 1)

                def step(k, u):
                    c3, u3 = back(k, u, S_REC, U)
                    if valid(c3, u3, U, CHUNKS):
                        n = c3 * U + u3
                        wait(dve, s["rec"], n + 1)
                        xv = xr[u3].rearrange("p (q v) -> p v q", v=2)
                        dve.tensor_tensor(xv, rec[:].rearrange("p (v q) -> p v q", v=2), xv, ALU.add
                                          ).then_inc(s["x1"], 1)
                    c2, u2 = back(k, u, S_LOW, U)
                    if valid(c2, u2, U, CHUNKS):
                        n = c2 * U + u2
                        wait(dve, s["rstd"], n + 1)
                        wait(dve, s["low"], n - 1)
                        dve.tensor_tensor(nn[u2 % 2], xc[u2 % 2][:], rr[u2 % 2], ALU.mult
                                          ).then_inc(s["normed"], 1)
                    c5, u5 = back(k, u, S_TVAR, U)
                    if valid(c5, u5, U, CHUNKS) and u5 % 2 == 1:
                        pair = c5 * (U // 2) + u5 // 2
                        p = (u5 % B) // 2
                        wait(dve, s["trstd"], pair + 1)
                        wait(dve, s["logits"], 2 * pair + 2)
                        at = p * (TOK + PAD) + (c5 * (U // B) + u5 // B) * N
                        dve.tensor_tensor(g.E[:, bass.ds(at, N)], lg[:], trs, ALU.mult
                                          ).then_inc(s["glog"], 1)
                    c4, u4 = back(k, u, S_TOK, U)
                    if valid(c4, u4, U, CHUNKS):
                        n = c4 * U + u4
                        wait(dve, s["tturned"], n + 1)
                        wait(dve, tok_out[u4 % 4], (c4 * 2 + u4 // 4) * 16)
                        dve.tensor_copy(ts[u4 % 4], tt[:]).then_inc(s["tcopied"], 1)
                    if valid(c3, u3, U, CHUNKS):
                        n = c3 * U + u3
                        wait(dve, s["tcentred"], n)
                        wait(dve, s["x1"], n + 1)
                        dve.tensor_copy(x1h[:], xr[u3]).then_inc(s["x1high"], 1)
                    kk, uu = back(k, u, -1, U)
                    if valid(kk, uu, U, CHUNKS):
                        high_of_x(kk, uu)
                    if valid(k, u, U, CHUNKS):
                        n = k * U + u
                        wait(dve, s["squared"], n + 1)
                        wait(dve, s["var"], n)
                        dve.tensor_copy(sq_hi[:], sq[u % 2]).then_inc(s["high"], 1)
                high_of_x(0, 0)
                pipelined(dve, step, CHUNKS, U, LAG, tail=1)


def expert_choice(nc, g, a):
    with ExitStack() as ctx:
        m = Mem(nc, ctx, "ec")
        v = Views(g.X, 0)
        e2 = [v.take(TOK + PAD), v.take(TOK + PAD)]
        v = Views(g.X, g.small_at)
        gath, xcg = v.take(2, K0, C), v.take(2, K0, C)
        sqg = gath
        mx, swapm, sel64, sele = v.take(2, 8), v.take(P), v.take(2 * E0), v.take(E0, B)
        own, oth, hpc, thr = v.take(2, 17), v.take(2, 17), v.take(1), v.take(K0)
        mg, nb, zt, rz, base = v.take(2), v.take(2), v.take(2), v.take(2), v.take(2)
        oT = v.take(2, 2, 2, E0)
        v.at -= 4 * K0 * K0
        cmp1, cmp2 = v.take(2, K0, K0), v.take(2, K0, K0)
        cnt, chosen, lst, lst2, wgt = (v.take(2, K0) for _ in range(5))
        jf = v.take(2, K0)
        mean, var, pooled = v.take(2, K0), v.take(2, K0), v.take(2, C)
        pT, hT = v.take(P), v.take(2, E0 * B)
        idx = m.sb("idx", [P, 2, K0], U32)
        jdx = m.sb("jdx", [P, 2, K0], U32)
        rows = m.sb("rows", [P, 2, K0], U32)
        psw, pso, psp, psh, pst = (m.ps(n) for n in ("psw", "pso", "psp", "psh", "pst"))
        chain, swap_ready, swapped, biased, exped, packed, swapped2, rows_ready, gathered = (
            m.sem(n) for n in ("chain", "swr", "sw", "nb", "exp", "pk", "sw2", "rows", "gath"))
        indexed, vln, vexp, pooled_r, poolT, pT_r, hid_r, hT_r, out_r, oT_r, outT_r, done = (
            m.sem(n) for n in ("mi", "vln", "vexp", "pool", "poolT", "pT", "hid", "hT", "out", "oT", "outT", "dn"))
        pair_of = [g.E[:, 0:TOK], g.E[:, TOK + PAD:2 * TOK + PAD]]
        padded = [g.E[:, 0:TOK + PAD], g.E[:, TOK:2 * TOK + PAD]]
        data_of = [e2[0][:, 0:TOK], e2[1][:, PAD:TOK + PAD]]
        with nc.Block() as block:
            @block.vector
            def _(dve):
                link = Chain(dve, chain)
                link(dve.memset(g.D[:], 0.0))
                for q in range(4):
                    part = slice(q * E0, q * E0 + E0)
                    dve.memset(hpc[part], float(P * (q % 2)))
                    for p in range(2):
                        dve.memset(base[part, p:p + 1], float((2 * p + q // 2) * 2 * TOK + q % 2))
                    dve.tensor_copy(swapm[:, q * E0:q * E0 + E0], g.ident[:, (q ^ 1) * E0:(q ^ 1) * E0 + E0])
                for i in range(K0):
                    dve.memset(thr[:, i:i + 1], float(K0 - i))
                for b2 in range(2):
                    dve.tensor_tensor(sel64[:, b2 * E0:b2 * E0 + E0],
                                      g.ident[:, 2 * b2 * E0:2 * b2 * E0 + E0],
                                      g.ident[:, (2 * b2 + 1) * E0:(2 * b2 + 2) * E0], ALU.add)
                dve.tensor_copy(sele[0:E0], bcast(g.ident[0:E0, 0:E0], 2, B))
                dve.memset(pT[C:C + 1], 1.0)
                for p in range(2):
                    last = dve.max(out=mx[:, p], in_=pair_of[p])
                link(last)
                dve.tensor_copy(mg, mx[:, :, 0]).then_inc(swap_ready, 1)
                dve.wait_ge(swap_ready, 1)
                dve.wait_ge(swapped, 1)
                link(dve.tensor_tensor(mg, psw[:, 0:2], mg, ALU.max))
                link(dve.tensor_scalar(nb, mg, g.gate_b[:], -1.0, ALU.add, ALU.mult))
                dve.tensor_scalar(nb, nb, g.gate_b[:], None, ALU.add).then_inc(biased, 1)
                for p in range(2):
                    dve.max_index(out=idx[:, p], in_max=mx[:, p], in_values=pair_of[p]).then_inc(indexed, 1)
                dve.wait_ge(indexed, 2)
                dve.tensor_single_scalar(jdx[:], idx[:], 7, ALU.logical_shift_right)
                link(dve.tensor_copy(own[:, :, K0:2 * K0], idx[:]))
                link(dve.tensor_copy(jf, jdx[:]))
                for p in range(2):
                    last = dve.tensor_scalar(rows[:, p], own[:, p, K0:2 * K0], 2.0, base[:, p:p + 1],
                                             ALU.mult, ALU.add)
                last.then_inc(rows_ready, 1)
                dve.wait_ge(exped, 4)
                link(dve.scalar_tensor_tensor(jf, jf, float(P), own[:, :, K0:2 * K0], ALU.mult, ALU.add))
                dve.tensor_scalar(own[:, :, K0:2 * K0], jf, hpc, None, ALU.add).then_inc(packed, 1)
                dve.wait_ge(packed, 1)
                dve.wait_ge(swapped2, 1)
                link(dve.tensor_copy(oth, pso[:, 0:34].rearrange("p (a b) -> p a b", a=2)))
                shape = [P, 2, K0, K0]
                mine = [own[:, :, i * K0:i * K0 + K0].unsqueeze(3).to_broadcast(shape) for i in range(2)]
                them = [oth[:, :, i * K0:i * K0 + K0].unsqueeze(2).to_broadcast(shape) for i in range(2)]
                dve.tensor_tensor(cmp1, them[0], mine[0], ALU.is_equal)
                link(dve.tensor_tensor(cmp2, them[1], mine[1], ALU.is_lt))
                link(dve.tensor_tensor(cmp1, cmp1, cmp2, ALU.mult))
                link(dve.tensor_tensor(cmp2, them[0], mine[0], ALU.is_gt))
                link(dve.tensor_tensor(cmp1, cmp1, cmp2, ALU.add))
                link(dve.tensor_reduce(cnt, cmp1, AXX, ALU.add))
                dve.tensor_tensor(zt, own[:, :, 16], oth[:, :, 16], ALU.add)
                link(dve.tensor_tensor(chosen, cnt, bcast(thr, 1, 2), ALU.is_lt))
                dve.reciprocal(rz, zt)
                dve.tensor_tensor(lst, chosen, own[:, :, 0:K0], ALU.mult)
                link(dve.tensor_scalar(lst2, chosen, -SENTINEL, SENTINEL, ALU.mult, ALU.add))
                dve.tensor_tensor(wgt, lst, bcast(rz, 2, K0), ALU.mult)
                link(dve.tensor_tensor(lst2, lst2, lst, ALU.add))
                link(dve.match_replace(out=e2[0], in_to_replace=lst2[:, 0], in_values=padded[0], imm_value=0.0))
                dve.wait_ge(gathered, 16 * 2 * K0)
                link(dve.tensor_reduce(mean, gath, AXX, ALU.add))
                link(dve.tensor_scalar(mean, mean, 1.0 / C, None, ALU.mult))
                link(dve.tensor_tensor(xcg, gath, bcast(mean, 3, C), ALU.subtract))
                link(dve.tensor_tensor(sqg, xcg, xcg, ALU.mult))
                link(dve.tensor_reduce(var, sqg, AXX, ALU.add))
                dve.tensor_scalar(var, var, 1.0 / C, None, ALU.mult).then_inc(vln, 1)
                dve.wait_ge(vexp, 2)
                link(dve.tensor_tensor(wgt, wgt, var, ALU.mult))
                link(dve.tensor_tensor(xcg, xcg, bcast(wgt, 3, C), ALU.mult))
                dve.tensor_reduce(pooled, xcg.rearrange("p a k c -> p a c k"), AXX, ALU.add
                                  ).then_inc(pooled_r, 1)
                dve.wait_ge(poolT, 1)
                dve.tensor_copy(pT[0:C], psp[0:C, 0:P]).then_inc(pT_r, 1)
                link(dve.match_replace(out=e2[1], in_to_replace=lst2[:, 1], in_values=padded[1], imm_value=0.0))
                for p in range(2):
                    dve.tensor_tensor(pair_of[p], pair_of[p], data_of[p], ALU.subtract).then_inc(done, 1)
                dve.wait_ge(out_r, 1)
                src = psp[0:C, 256:256 + E0 * B].rearrange("p (e a b) -> p a b e", e=E0, a=2)
                for h in range(2):
                    last = dve.tensor_copy(oT[0:C, :, :, h], src)
                last.then_inc(oT_r, 1)
                dve.wait_ge(outT_r, 1)
                for b in range(B):
                    p, b2 = divmod(b, 2)
                    for h in range(2):
                        q = slice((2 * b2 + h) * E0, (2 * b2 + h + 1) * E0)
                        last = dve.tensor_scalar(g.D[q, b, h * C:h * C + C], pst[q, p * C:p * C + C],
                                                 rz[q, p:p + 1], None, ALU.mult)
                last.then_inc(done, 1)
                dve.wait_ge(done, 3)

            @block.scalar
            def _(act):
                load_ln_exp(nc, act)
                act.wait_ge(biased, 1)
                for p in range(2):
                    act.activation(own[:, p, 0:K0], mx[:, p], ACT.Exp, bias=nb[:, p:p + 1]).then_inc(exped, 1)
                for p in range(2):
                    act.wait_ge(indexed, p + 1)
                    act.activation(pair_of[p], pair_of[p], ACT.Exp, bias=nb[:, p:p + 1],
                                   accum_out=own[:, p, 16:17]).then_inc(exped, 1)
                act.wait_ge(vln, 1)
                act.activation(var, var, ACT.Ln, bias=g.eps[:, 1:2]).then_inc(vexp, 1)
                act.wait_ge(vexp, 1)
                act.activation(var, var, ACT.Exp, scale=-0.5).then_inc(vexp, 1)
                act.wait_ge(hid_r, 1)
                act.activation(hT, psh[:, 0:2 * E0 * B].rearrange("p (t n) -> p t n", t=2), ACT.Gelu
                               ).then_inc(hT_r, 1)

            @block.gpsimd
            def _(pool):
                pool.wait_ge(rows_ready, 1)
                for p in range(2):
                    for i in range(K0):
                        pool.indirect_dma_start(
                            out=gath[:, p, i, :], out_offset=None,
                            in_=g.x1tok.rearrange("b j w (h c) -> (b j w h) c", h=2),
                            in_offset=bass.IndirectOffsetOnAxis(ap=rows[:, p, i:i + 1], axis=0),
                        ).then_inc(gathered, 16)

            @block.tensor
            def _(pe):
                pe.wait_ge(swap_ready, 1)
                pe.matmul(psw[:, 0:2], swapm, mg, start=True, stop=True).then_inc(swapped, 1)
                pe.wait_ge(packed, 1)
                pe.matmul(pso[:, 0:34], swapm, own.rearrange("p a b -> p (a b)"), start=True, stop=True
                          ).then_inc(swapped2, 1)
                pe.wait_ge(pooled_r, 1)
                for p in range(2):
                    last = pe.matmul(psp[0:C, p * 2 * E0:(p + 1) * 2 * E0], pooled[:, p], sel64,
                                     start=True, stop=True)
                last.then_inc(poolT, 1)
                pe.wait_ge(pT_r, 1)
                pe.wait_ge(g.experts_loaded, 16 * 3)
                pooled_of = pT[0:C + 1].rearrange("p (b e) -> p e b", b=B)
                for e in range(E0):
                    for t in range(2):
                        at = (t * E0 + e) * B
                        last = pe.matmul(psh[:, at:at + B], g.W1[0:C + 1, e, t * P:t * P + P],
                                         pooled_of[:, e], start=True, stop=True)
                last.then_inc(hid_r, 1)
                pe.wait_ge(hT_r, 1)
                out = psp[0:C, 256:256 + E0 * B]
                pe.matmul(out, g.w2bias, sele[0:E0].rearrange("p e b -> p (e b)"),
                          start=True, stop=False, skip_group_check=True)
                for e in range(E0):
                    for t in range(2):
                        last = pe.matmul(out[:, e * B:e * B + B], g.W2[:, e, t, :], hT[:, t, e * B:e * B + B],
                                         start=False, stop=(e == E0 - 1 and t == 1), skip_group_check=True)
                last.then_inc(out_r, 1)
                pe.wait_ge(oT_r, 1)
                for p in range(2):
                    last = pe.transpose(pst[:, p * C:p * C + C], oT[0:C, p].rearrange("p b h e -> p (b h e)"),
                                        g.ident[0:C, 0:C])
                last.then_inc(outT_r, 1)


def apply_choice(nc, g, a):
    U = 4
    S_CEN, S_VAR = 1, 2
    AHEAD = 2
    LAG = S_VAR + 1
    with ExitStack() as ctx:
        m = Mem(nc, ctx, "ac")
        xr = [m.sb(f"xr{i}", [P, N]) for i in range(U)]
        sq = [m.sb(f"sq{i}", [P, N]) for i in range(2)]
        dl, vv = ([m.ps(f"{n}{i}") for i in range(2)] for n in ("dl", "vv"))
        xc = [m.ps(f"xc{i}") for i in range(U)]
        xin, x2_out = m.sems("xin", U), m.sems("x2o", U)
        s = {n: m.sem(n) for n in ("delta", "x2", "centred", "squared", "var", "lnv", "rstd", "normed")}
        Xv = g.X[:].rearrange("p (s n) -> p s n", s=2)
        with nc.Block() as block:
            @block.sync
            def _(sp):
                def load(k, u):
                    wait(sp, x2_out[u], k * 16)
                    settle(sp, g.settled)
                    wait(sp, s["centred"], k * U + u - U + 1)
                    sp.dma_start(xr[u][:], g.x1s[bass.ds(k * U + u, 1)].rearrange("t p n -> p (t n)")
                                 ).then_inc(xin[u], 16)

                def step(k, u):
                    kk, uu = back(k, u, -AHEAD, U)
                    if valid(kk, uu, U, CHUNKS):
                        load(kk, uu)
                    if valid(k, u, U, CHUNKS):
                        wait(sp, s["x2"], k * U + u + 1)
                        sp.dma_start(g.x2s[bass.ds(k * U + u, 1)].rearrange("t p n -> p (t n)"),
                                     xr[u][:]).then_inc(x2_out[u], 16)
                for u in range(AHEAD):
                    load(0, u)
                pipelined(sp, step, CHUNKS, U, 0, tail=1)
                for u in range(U):
                    sp.wait_ge(x2_out[u], 16 * (CHUNKS // U))

            @block.tensor
            def _(pe):
                def step(k, u):
                    if valid(k, u, U, CHUNKS):
                        n = k * U + u
                        wait(pe, s["x2"], n - 1)
                        pe.matmul(dl[u % 2][:], g.D[:, u], g.E[:, bass.ds((u // 2) * (TOK + PAD) + k * N, N)],
                                  start=True, stop=True).then_inc(s["delta"], 1)
                    c1, u1 = back(k, u, S_CEN, U)
                    if valid(c1, u1, U, CHUNKS):
                        n = c1 * U + u1
                        wait(pe, s["x2"], n + 1)
                        wait(pe, s["normed"], n + 1 - U)
                        src = xr[u1][:].rearrange("p (q v) -> p v q", v=2)
                        for h in range(2):
                            for v in range(2):
                                last = pe.matmul(xc[u1][v * C:v * C + C, h * (N // 2):(h + 1) * (N // 2)],
                                                 g.Cm[:, h * C:h * C + C], src[:, v], start=True, stop=True)
                        last.then_inc(s["centred"], 1)
                    c2, u2 = back(k, u, S_VAR, U)
                    if valid(c2, u2, U, CHUNKS):
                        n = c2 * U + u2
                        wait(pe, s["squared"], n + 1)
                        wait(pe, s["lnv"], n - 1)
                        pe.matmul(vv[u2 % 2][:], g.J[:], sq[u2 % 2][:], start=True, stop=True
                                  ).then_inc(s["var"], 1)
                pipelined(pe, step, CHUNKS, U, LAG)

            @block.scalar
            def _(act):
                load_ln_exp(nc, act)

                def step(k, u):
                    c1, u1 = back(k, u, S_CEN, U)
                    if valid(c1, u1, U, CHUNKS):
                        n = c1 * U + u1
                        wait(act, s["centred"], n + 1)
                        wait(act, s["normed"], n - 1)
                        act.activation(sq[u1 % 2][:], xc[u1][:], ACT.Square).then_inc(s["squared"], 1)
                    c2, u2 = back(k, u, S_VAR, U)
                    if valid(c2, u2, U, CHUNKS):
                        n = c2 * U + u2
                        wait(act, s["var"], n + 1)
                        act.activation(sq[u2 % 2][:], vv[u2 % 2][:], ACT.Ln, bias=g.eps[:, 0:1]
                                       ).then_inc(s["lnv"], 1)
                        act.wait_ge(s["lnv"], n + 1)
                        act.activation(sq[u2 % 2][:], sq[u2 % 2][:], ACT.Exp, scale=-0.5
                                       ).then_inc(s["rstd"], 1)
                pipelined(act, step, CHUNKS, U, LAG)

            @block.vector
            def _(dve):
                def step(k, u):
                    if valid(k, u, U, CHUNKS):
                        n = k * U + u
                        wait(dve, s["delta"], n + 1)
                        wait(dve, xin[u], k * 16 + 16)
                        dve.tensor_tensor(xr[u][:], dl[u % 2][:], xr[u][:], ALU.add).then_inc(s["x2"], 1)
                    c2, u2 = back(k, u, S_VAR, U)
                    if valid(c2, u2, U, CHUNKS):
                        n = c2 * U + u2
                        wait(dve, s["rstd"], n + 1)
                        at = u2 * HP * WP + c2 * (JR * WP)
                        dve.tensor_tensor(Xv[:, :, bass.ds(at, JR * WP)],
                                          xc[u2][:].rearrange("p (s n) -> p s n", s=2),
                                          sq[u2 % 2][:].rearrange("p (s n) -> p s n", s=2), ALU.mult
                                          ).then_inc(s["normed"], 1)
                pipelined(dve, step, CHUNKS, U, LAG)


def scan_weights(nc, g, a):
    with ExitStack() as ctx:
        m = Mem(nc, ctx, "sw")
        wn = [m.sb(f"wn{i}", [C, 2, C * TAPS]) for i in range(4)]
        wf = [m.sb(f"wf{i}", [P, TAPS, C]) for i in range(2)]
        ident = m.sb("id", [P, P])
        psa, psb = ([m.ps(f"{n}{i}") for i in range(2)] for n in ("a", "b"))
        loaded, idr, turned, copied, chain, done = (
            m.sem(n) for n in ("ld", "id", "tn", "cp", "ch", "dn"))
        pads = m.sem("pads")
        A8 = 8

        def blocks(t, pi):
            Tv = t.rearrange("p (d po c) -> p d po c", d=ND, po=2)
            rows = slice(pi * C, pi * C + C)
            if pi == 0:
                return [(Tv[rows, 0:5, 0, :], 0, 5), (Tv[rows, 1:5, 1, :], 1, 4)]
            return [(Tv[rows, 0:4, 0, :], 1, 4), (Tv[rows, 0:5, 1, :], 0, 5)]

        with nc.Block() as block:
            @block.sync
            def _(sp):
                for i, w in enumerate(("w_ud", "w_du", "w_lr", "w_rl")):
                    for h in range(2):
                        sp.dma_start(wn[i][:, h], a[w].rearrange("o c t -> o (c t)")).then_inc(loaded, 16)
                sp.wait_ge(loaded, 128)

            @block.tensor
            def _(pe):
                pe.wait_ge(loaded, 128)
                pe.wait_ge(idr, 1)
                for i in range(4):
                    wait(pe, copied, i - 1)
                    wv = wn[i][:].rearrange("o h (c t) -> o t (h c)", t=TAPS)
                    for t in range(TAPS):
                        dst = psa[i % 2][:, t * C:t * C + C] if t < A8 else psb[i % 2][:, 0:C]
                        last = pe.transpose(dst, wv[:, t], ident[0:C, 0:C])
                    last.then_inc(turned, 1)

            @block.scalar
            def _(act):
                for i in range(4):
                    act.wait_ge(turned, i + 1)
                    wait(act, done, i - 1)
                    act.activation(wf[i % 2][:, 0:A8], psa[i % 2][:].rearrange("p (t c) -> p t c", t=A8), ACT.Copy)
                    act.activation(wf[i % 2][:, A8], psb[i % 2][:, 0:C], ACT.Copy).then_inc(copied, 1)

            @block.vector
            def _(dve):
                link = Chain(dve, chain)
                dve.tensor_tensor(ident[:], g.Cm[:], g.J[:], ALU.add).then_inc(idr, 1)
                for t in (g.yh, g.yl):
                    dve.memset(t[:].bitcast(F32), 0.0).then_inc(pads, 1)
                for i in range(4):
                    for t in (g.Thi[i], g.Tlo[i]):
                        Tv = t[:].rearrange("p (d po c) -> p d po c", d=ND, po=2)
                        dve.memset(Tv[0:C, 0, 1, :].bitcast(F32), 0.0)
                        dve.memset(Tv[C:P, ND - 1, 0, :].bitcast(F32), 0.0)
                    dve.wait_ge(copied, i + 1)
                    for pi in range(2):
                        for dst, t0, n in blocks(g.Thi[i][:], pi):
                            last = dve.tensor_copy(dst, wf[i % 2][pi * C:pi * C + C, t0:t0 + 2 * n - 1:2, :])
                    link(last)
                    for pi in range(2):
                        his = blocks(g.Thi[i][:], pi)
                        for (dst, t0, n), (hi, _, _) in zip(blocks(g.Tlo[i][:], pi), his):
                            last = dve.tensor_tensor(dst, wf[i % 2][pi * C:pi * C + C, t0:t0 + 2 * n - 1:2, :],
                                                     hi.bitcast(F32), ALU.subtract)
                    last.then_inc(done, 1)
                dve.wait_ge(pads, 2)
                dve.wait_ge(done, 4)


def scan_pass(nc, g, i):
    vertical, reverse, turn = i < 2, i % 2 == 1, i == 1
    with ExitStack() as ctx:
        m = Mem(nc, ctx, f"s{i}")
        ps = [m.ps(f"ps{r}") for r in range(2)]
        hi_ready, full_ready, lo_ready, conv_done, turned = g.scan_sems[i % 2]
        Xv = g.X[:].rearrange("p (s b j w) -> p s b j w", s=2, b=B, j=HP)

        def line(j, slot):
            if vertical:
                return Xv[:, slot, :, bass.ds(j, 1), :].rearrange("p b j w -> p b (j w)")
            return Xv[:, slot, :, :, bass.ds(j, 1)].rearrange("p b j w -> p b (j w)")

        def place(k, r):
            return (63 - k, 1 - r) if reverse else (k, r)

        inner = slice(2, 2 + 64)
        with nc.Block() as block:
            if i in (1, 2):
                @block.sync
                def _(sp):
                    for sem in g.scan_sems[1 - i % 2]:
                        sp.sem_clear(sem)

            @block.tensor
            def _(pe):
                def step(k, r):
                    n = 2 * k + r
                    out = ps[r][:, 0:B * 64].rearrange("p (b w) -> p b w", b=B)
                    pe.wait_ge(hi_ready, n)
                    for t in (g.Tlo[i], g.Thi[i]):
                        for d in range(ND):
                            pe.matmul(out, t[:, d * P:d * P + P], g.yh[:, :, d:d + 64],
                                      start=(t is g.Tlo[i] and d == 0), stop=False)
                    pe.wait_ge(lo_ready, n)
                    for d in range(ND):
                        last = pe.matmul(out, g.Thi[i][:, d * P:d * P + P], g.yl[:, :, d:d + 64],
                                         start=False, stop=(d == ND - 1))
                    last.then_inc(conv_done, 1)
                step(0, 1)
                with pe.Fori(1, 64) as k:
                    for r in range(2):
                        step(k, r)

            @block.vector
            def _(dve):
                def split(x, n):
                    dve.wait_ge(hi_ready, n + 1)
                    wait(dve, full_ready, n + (1 if turn else 0))
                    dve.tensor_tensor(g.yl[:, :, inner], x, g.yh[:, :, inner].bitcast(F32), ALU.subtract
                                      ).then_inc(lo_ready, 1)

                def step(k, r):
                    n = 2 * k + r
                    j, slot = place(k, r)
                    x = line(j if isinstance(j, int) else dve.snap(j), slot)
                    dve.wait_ge(conv_done, n)
                    if reverse and r == 0:
                        settle(dve, g.settled)
                    conv = ps[r][:, 0:B * 64].rearrange("p (b w) -> p b w", b=B)
                    dve.scalar_tensor_tensor(g.yh[:, :, inner], conv, 0.0, x, ALU.max, ALU.add
                                             ).then_inc(hi_ready, 1)
                    full = x
                    if turn:
                        full = g.ybuf[slot][:]
                        wait(dve, turned, k)
                    dve.scalar_tensor_tensor(full, conv, 0.0, x, ALU.max, ALU.add
                                             ).then_inc(full_ready, 1)
                    split(full, n)

                j, slot = place(0, 0)
                x = line(j, slot)
                dve.tensor_copy(g.yh[:, :, inner], x).then_inc(hi_ready, 1)
                if turn:
                    dve.tensor_copy(g.ybuf[slot][:], x).then_inc(full_ready, 1)
                split(x, 0)
                step(0, 1)
                with dve.Fori(1, 64) as k:
                    for r in range(2):
                        step(k, r)

            if turn:
                @block.scalar
                def _(act):
                    def pair_of_rows(k):
                        act.wait_ge(full_ready, 2 * k + 2)
                        for h in range(2):
                            for v in range(2):
                                dst = Xv[h * C:h * C + C, v, :, bass.ds(63 - k, 1), :]
                                last = act.activation(dst.rearrange("p b j w -> p b (j w)"),
                                                      g.ybuf[h][v * C:v * C + C], ACT.Copy)
                        last.then_inc(turned, 1)
                    pair_of_rows(0)
                    with act.Fori(1, 64) as k:
                        pair_of_rows(k)

def top2_mixture(nc, g, a, y_out):
    G2 = 2 * E1
    BLOCKS = 6
    ROWS = BLOCKS * G2
    TILES = N // P
    TW = P + G2
    GR = 2 * TILES * 2
    EP = E1 // 2
    UNITS = 2 * EP
    PAIRS = CHUNKS // 2
    NEVER = -1.0e30
    LINKS, POOL_LINKS = 10, 5
    ND_SEM = 4 * 16
    with ExitStack() as ctx:
        m = Mem(nc, ctx, "tm")
        rx = m.sb("rx", [P, TW])
        rbias, rev = m.sb("rbias", [P, E1]), m.sb("rev", [P, E1])
        wexp = m.sb("wexp", [P, EP, C])
        bn, bb = m.sb("bn", [ROWS, C]), m.sb("bb", [ROWS, 2, C])
        bhi, bias = m.sb("bhi", [ROWS, 2 * C], F32R), m.sb("bias", [ROWS, 2 * C], F32R)
        r16, hmask = m.sb("r16", [ROWS, G2]), m.sb("hmask", [ROWS, 2])
        sel = m.sb("sel", [ROWS, G2, C], F32R)
        zero = m.sb("zero", [P, 1])
        x2 = [[m.sb(f"x2_{u}{i}", [P, N]) for i in range(2)] for u in range(2)]
        yo = [m.sb(f"yo{i}", [P, N]) for i in range(2)]
        nS = [[m.sb(f"nS{u}{i}", [P, N]) for i in range(2)] for u in range(2)]
        nd = [[m.sb(f"nd{u}{i}", [P, 2, N]) for i in range(2)] for u in range(2)]
        Z = [[m.sb(f"Z{i}{h}", [P, N]) for h in range(2)] for i in range(2)]
        xh, xl, Cmr = m.sb("xh", [P, N], F32R), m.sb("xl", [P, N], F32R), m.sb("Cmr", [P, P], F32R)
        sqt = m.sb("sqt", [P, 4, C])
        V, LV = (m.sb(n, [P, GR]) for n in ("V", "LV"))
        R = [m.sb(f"R{u}", [P, GR]) for u in range(2)]
        L0, L, EX, A_, F1, F2 = (m.sb(n, [P, GR, E1]) for n in ("L0", "L", "EX", "A", "F1", "F2"))
        m1, total = m.sb("m1", [P, GR]), m.sb("total", [P, GR])
        GG = m.sb("GG", [P, 2, 2 * TILES, G2])
        gp = [m.sb(f"gp{u}", [P, 2 * TILES, 3, 2, G2], F32R) for u in range(2)]
        gT = [m.sb(f"gT{i}", [ROWS, N], F32R) for i in range(2)]
        bankA, bankB = m.ps("bankA"), m.ps("bankB")
        po = [m.ps(f"po{i}") for i in range(2)]
        pg = [[m.ps(f"pg{i}{h}") for h in range(2)] for i in range(2)]
        x2_in, nd_in = ([[m.sem(f"{n}{u}{i}") for i in range(2)] for u in range(2)] for n in ("x2i", "nd"))
        y_st = m.sems("yst", 2)
        s = {n: m.sem(n) for n in (
            "x3", "xhigh", "xparts", "centred", "xcs", "tiledA", "tiledB", "readA", "readB", "lnv", "rstd", "logits",
            "logits_used", "scaled", "shifted", "exp", "chosen", "weighed", "inverse", "gates",
            "turned", "gcopied", "bcast", "z", "zmm", "y")}
        chain, pool_chain, act_chain, chain0, ld, prep, prep_done = (
            m.sem(n) for n in ("chain", "pchain", "achain", "chain0", "ld", "prep", "prepd"))
        Xv = g.X[:].rearrange("p (s n) -> p s n", s=2)
        x_dst = y_out.rearrange("b c (j t) w -> b t c j w", t=2)
        wide = [P, GR, E1]

        def xview(k, u, i):
            return Xv[:, :, bass.ds((2 * u + i) * HP * WP + k * (JR * WP), JR * WP)]

        def natural(t):
            return t.rearrange("p (j w v) -> p v j w", j=JR, v=2)

        def over(t):
            return t.unsqueeze(2).to_broadcast(wide)

        def steps(engine, step, tail=0):
            pipelined(engine, step, PAIRS, 2, 4, tail=tail, head=2)

        def now(k, u):
            return valid(k, u, 2, PAIRS)

        with nc.Block() as block:
            @block.sync
            def _(sp):
                def load(dst, src):
                    sp.dma_start(dst, src, allow_slow_non_contiguous=True).then_inc(ld, 16)
                for h in range(2):
                    load(wexp[h * C:h * C + C], a["expert_w"][h:E1:2].rearrange("p d c -> d p c"))
                for q in range(BLOCKS * 2):
                    load(bn[q * E1:q * E1 + E1], a["expert_b"])
                load(rbias[:], a["router_b"].rearrange("(o e) -> o e", o=1).to_broadcast([P, E1]))
                sp.wait_ge(prep, 1)
                for h in range(2):
                    load(rx[h * C:h * C + C, P + h * E1:P + h * E1 + E1], a["router_w"])

                def load_x2(k, u, i):
                    wait(sp, s["x3"], (2 * k + u) * 2 + i - 3)
                    settle(sp, g.settled)
                    sp.dma_start(x2[u][i][:], g.x2s[bass.ds(k * B + 2 * u + i, 1)].rearrange("t p n -> p (t n)")
                                 ).then_inc(x2_in[u][i], 16)

                def copy_tokens(k, u, i):
                    n = (2 * k + u) * 2 + i
                    wait(sp, s["xcs"], n + 1)
                    settle(sp, g.settled)
                    wait(sp, s["z"], (n - 3) * 2 * EP)
                    for h in range(2):
                        for half in range(2):
                            sp.dma_start(nd[u][i][half * C:half * C + C, h, :],
                                         nS[u][i][h * C:h * C + C]).then_inc(nd_in[u][i], 16)

                def store_y(k, u, i):
                    wait(sp, s["y"], (2 * k + u) * 2 + i + 1)
                    settle(sp, g.settled)
                    for h in range(2):
                        sp.dma_start(x_dst[2 * u + i, h][:, bass.ds(k * JR, JR), :],
                                     yo[i][h * C:h * C + C].rearrange("p (j w) -> p j w", j=JR)
                                     ).then_inc(y_st[i], 16)

                def step(k, u):
                    ahead, before, ex, last = (back(k, u, d, 2) for d in (-2, 1, 3, 4))
                    if now(*ahead):
                        load_x2(*ahead, 0)
                    if now(*last):
                        store_y(*last, 1)
                    if now(*before):
                        copy_tokens(*before, 0)
                    if now(*ahead):
                        load_x2(*ahead, 1)
                    if now(*ex):
                        store_y(*ex, 0)
                    if now(*before):
                        copy_tokens(*before, 1)
                for u in range(2):
                    for i in range(2):
                        load_x2(0, u, i)
                steps(sp, step, tail=1)
                for i in range(2):
                    sp.wait_ge(y_st[i], 16 * 2 * PAIRS)

            @block.tensor
            def _(pe):
                pe.wait_ge(ld, 16 * (2 + BLOCKS * 2 + 1 + 2))
                pe.wait_ge(prep_done, 1)

                def centre(k, u, i):
                    n = (2 * k + u) * 2 + i
                    wait(pe, s["xparts"], n + 1)
                    wait(pe, s["readA"], n)
                    pe.matmul(bankA[:], Cmr[:], xh[:], start=True, stop=False)
                    pe.matmul(bankA[:], Cmr[:], xl[:], start=False, stop=True).then_inc(s["centred"], 1)

                def tiles(k, u, i):
                    n = (2 * k + u) * 2 + i
                    wait(pe, s["xcs"], n + 1)
                    wait(pe, s["readB"], n)
                    wait(pe, s["gcopied"], n - 5)
                    for bank, t0, done in ((bankB, 2, "tiledB"), (bankA, 0, "tiledA")):
                        for t in range(2):
                            at = (t0 + t) * P
                            last = pe.matmul(bank[:, t * TW:t * TW + TW], nS[u][i][:, at:at + P], rx[:],
                                             start=True, stop=True)
                        last.then_inc(s[done], 1)

                def turn_gates(k, u, i, read):
                    wait(pe, s["gates"], 2 * k + u + 1)
                    wait(pe, s["gcopied"], (2 * k + u) * 2 + i)
                    wait(pe, s["readB"], read)
                    for t in range(TILES):
                        last = pe.transpose(bankB[0:ROWS, t * P:t * P + P],
                                            gp[u][:, i * TILES + t].rearrange("p a l e -> p (a l e)").bitcast(F32),
                                            rx[:, 0:P])
                    last.then_inc(s["turned"], 1)

                def broadcast(k, u, q):
                    i, ep = divmod(q, EP)
                    t = 2 * k + u
                    if ep == 0:
                        wait(pe, s["gcopied"], 2 * t + i + 1)
                    for h in range(2):
                        wait(pe, s["z"], (t * UNITS + q - 2) * 2 + h + 1)
                        at = h * E1 + 2 * ep
                        pe.matmul(pg[q % 2][h][:], sel[:, at:at + 2].rearrange("p e c -> p (e c)"), gT[i][:],
                                  start=True, stop=True).then_inc(s["bcast"], 1)

                def biases(k, u, i):
                    wait(pe, s["y"], (2 * k + u) * 2 + i - 1)
                    pe.matmul(po[i][:], bias[:], gT[i][:], start=True, stop=False, skip_group_check=True)

                def experts(k, u, q):
                    i, ep = divmod(q, EP)
                    wait(pe, s["z"], ((2 * k + u) * UNITS + q) * 2 + 2)
                    for h in range(2):
                        last = pe.matmul(po[i][h * C:h * C + C, :], wexp[:, ep], Z[q % 2][h][:],
                                         start=False, stop=(ep == EP - 1), skip_group_check=True)
                    last.then_inc(s["zmm"], 1)

                def step(k, u):
                    n = (2 * k + u) * 2
                    near, ex = back(k, u, 2, 2), back(k, u, 3, 2)
                    read = [min(n + c, CHUNKS) if isinstance(k, int) else n + c for c in (1, 2)]
                    for q in range(UNITS):
                        if now(k, u) and q in (0, 3):
                            centre(k, u, q // 3)
                        if now(k, u) and q in (1, 5):
                            tiles(k, u, q // 4)
                        if now(*ex) and q == 2:
                            turn_gates(*ex, 1, read[0])
                        if now(*near) and q == 6:
                            turn_gates(*near, 0, read[1])
                        if now(*ex) and q % EP == 0:
                            biases(*ex, q // EP)
                        if q + 1 < UNITS and now(*ex):
                            broadcast(*ex, q + 1)
                        if q + 1 == UNITS and now(*near):
                            broadcast(*near, 0)
                        if now(*ex):
                            experts(*ex, q)
                steps(pe, step)

            @block.scalar
            def _(act):
                load_ln_exp(nc, act)

                def high_part(k, u, i):
                    n = (2 * k + u) * 2 + i
                    wait(act, s["x3"], n + 1)
                    wait(act, s["centred"], n)
                    settle(act, g.settled)
                    act.activation(xh[:].rearrange("p (v n) -> p v n", v=2), xview(k, u, i), ACT.Copy
                                   ).then_inc(s["xhigh"], 1)

                def copy_centred(k, u, i):
                    n = (2 * k + u) * 2 + i
                    wait(act, s["centred"], n + 1)
                    wait(act, s["tiledA"], n - 3)
                    wait(act, nd_in[u][i], k * ND_SEM)
                    act.activation(nS[u][i][:], bankA[:], ACT.Copy).then_inc(s["xcs"], 1)

                def read_tiles(k, u, i):
                    n = (2 * k + u) * 2 + i
                    if i == 0:
                        wait(act, s["lnv"], 2 * k + u)
                        wait(act, s["logits_used"], 2 * k + u)
                    for bank, t0, done, free in ((bankB, 2, "tiledB", "readB"), (bankA, 0, "tiledA", "readA")):
                        wait(act, s[done], n + 1)
                        rows = (i * TILES + t0) * 2
                        tv = bank[:, 0:2 * TW].rearrange("p (t x) -> p t x", t=2)
                        for t in range(2):
                            for h in range(2):
                                r = rows + 2 * t + h
                                act.activation(sqt[:, 2 * t + h], tv[:, t, h * C:h * C + C], ACT.Square,
                                               accum_out=V[:, r:r + 1]).then_inc(act_chain, 1)
                        act.activation(L0[:, rows:rows + 4, :].rearrange("p (t h) e -> p t (h e)", h=2),
                                       tv[:, :, P:TW], ACT.Copy).then_inc(s["logits"], 1)
                        act.wait_ge(act_chain, (n + 1) * 8 - (4 if t0 else 0))
                        act.wait_ge(s["logits"], 2 * n + (1 if t0 else 2))
                        settle(act, s[free])

                def rstd(k, u):
                    t = 2 * k + u
                    act.activation(LV[:], V[:], ACT.Ln, bias=g.eps[:, 1:2], scale=1.0 / C).then_inc(s["lnv"], 1)
                    wait(act, s["gates"], t - 1)
                    act.wait_ge(s["lnv"], t + 1)
                    act.activation(R[u][:], LV[:], ACT.Exp, scale=-0.5).then_inc(s["rstd"], 1)

                def copy_gates(k, u, i):
                    n = (2 * k + u) * 2 + i
                    wait(act, s["turned"], n + 1)
                    wait(act, s["zmm"], (n - 1) * EP)
                    act.activation(gT[i][:], bankB[0:ROWS, :], ACT.Copy).then_inc(s["gcopied"], 1)

                def step(k, u):
                    after, before, near, ex = (back(k, u, d, 2) for d in (-1, 1, 2, 3))
                    if now(k, u):
                        copy_centred(k, u, 0)
                        high_part(k, u, 1)
                        read_tiles(k, u, 0)
                    if now(*before):
                        wait(act, s["shifted"], 2 * before[0] + before[1] + 1)
                        act.activation(EX[:], L[:], ACT.Exp).then_inc(s["exp"], 1)
                    if now(*ex):
                        copy_gates(*ex, 1)
                    if now(k, u):
                        copy_centred(k, u, 1)
                        read_tiles(k, u, 1)
                    if now(k, u):
                        rstd(k, u)
                    if now(*near):
                        copy_gates(*near, 0)
                    if now(*after):
                        high_part(*after, 0)
                high_part(0, 0, 0)
                steps(act, step, tail=1)

            @block.gpsimd
            def _(pool):
                def low_part(k, u, i):
                    wait(pool, s["xhigh"], (2 * k + u) * 2 + i + 1)
                    settle(pool, g.settled)
                    pool.tensor_tensor(xl[:].rearrange("p (v n) -> p v n", v=2), xview(k, u, i),
                                       xh[:].rearrange("p (v n) -> p v n", v=2).bitcast(F32), ALU.subtract
                                       ).then_inc(s["xparts"], 1)

                def scale(k, u):
                    t = 2 * k + u
                    wait(pool, s["rstd"], t + 1)
                    wait(pool, s["logits"], 4 * t + 4)
                    pool.tensor_tensor(L[:], L0[:], over(R[u][:]), ALU.mult).then_inc(s["logits_used"], 1)
                    pool.wait_ge(s["logits_used"], t + 1)
                    pool.tensor_tensor(L[:], L[:], rbias[:].unsqueeze(1).to_broadcast(wide), ALU.add
                                       ).then_inc(s["scaled"], 1)

                def weigh(k, u):
                    t = 2 * k + u
                    link = Chain(pool, pool_chain, base=t * POOL_LINKS)
                    wait(pool, s["chosen"], t + 1)
                    link(pool.tensor_tensor(F1[:], F1[:], F2[:], ALU.add))
                    wait(pool, s["exp"], t + 1)
                    pool.tensor_tensor(F1[:], F1[:], EX[:], ALU.mult).then_inc(s["weighed"], 1)

                def split(k, u):
                    t = 2 * k + u
                    link = Chain(pool, pool_chain, base=t * POOL_LINKS, count=1)
                    wait(pool, s["inverse"], t + 1)
                    wait(pool, s["turned"], 2 * t - 2)
                    plain = GG[:, 1].rearrange("p t (h e) -> p (t h) e", h=2)
                    scaled = GG[:, 0].rearrange("p t (h e) -> p (t h) e", h=2)
                    both = GG[:].rearrange("p k t e -> p t k e")
                    none = zero[:].unsqueeze(2).unsqueeze(3).to_broadcast(list(both.shape))
                    link(pool.tensor_tensor(plain, F1[:], over(total[:]), ALU.mult))
                    link(pool.tensor_tensor(scaled, plain, over(R[u][:]), ALU.mult))
                    link(pool.tensor_tensor(gp[u][:, :, 0:2, 0], both, none, ALU.add))
                    link(pool.tensor_tensor(gp[u][:, :, 0:2, 1], both, gp[u][:, :, 0:2, 0].bitcast(F32), ALU.subtract))
                    pool.tensor_tensor(gp[u][:, :, 2], gp[u][:, :, 1].bitcast(F32), none, ALU.add).then_inc(s["gates"], 1)

                def step(k, u):
                    after, before = back(k, u, -1, 2), back(k, u, 1, 2)
                    if now(k, u):
                        low_part(k, u, 1)
                    if now(*before):
                        weigh(*before)
                    if now(*after):
                        low_part(*after, 0)
                    if now(k, u):
                        scale(k, u)
                    if now(*before):
                        split(*before)
                pool.wait_ge(prep_done, 1)
                low_part(0, 0, 0)
                steps(pool, step, tail=1)

            @block.vector
            def _(dve):
                link = Chain(dve, chain0)
                link(dve.memset(rx[:, P:TW], 0.0))
                dve.memset(zero[:], 0.0).then_inc(prep, 1)
                link(dve.tensor_tensor(rx[:, 0:P], g.Cm[:], g.J[:], ALU.add))
                dve.tensor_copy(Cmr[:], g.Cm[:])
                for e in range(E1):
                    dve.memset(rev[:, e:e + 1], float(E1 - e))
                link(dve.memset(sel[:].bitcast(F32), 0.0))
                link(dve.memset(bias[:].bitcast(F32), 0.0))
                link(dve.tensor_tensor(r16[:], rx[0:ROWS, 0:G2], rx[0:ROWS, G2:2 * G2], ALU.add))
                for q in range(2, BLOCKS):
                    link(dve.tensor_tensor(r16[:], r16[:], rx[0:ROWS, q * G2:(q + 1) * G2], ALU.add))
                dve.tensor_copy(sel[0:2 * G2], bcast(r16[0:2 * G2], 2, C))
                link(dve.tensor_reduce(hmask[:], r16[:].rearrange("p (h e) -> p h e", h=2), AXX, ALU.add))
                dve.wait_ge(ld, 16 * (2 + BLOCKS * 2 + 1 + 2))
                link(dve.tensor_tensor(bb[:], bcast(bn[:], 1, 2), bcast(hmask[:], 2, C), ALU.mult))
                flat = bb[:].rearrange("p h c -> p (h c)")
                link(dve.tensor_copy(bhi[:], flat))
                dve.tensor_copy(bias[2 * G2:4 * G2], bhi[2 * G2:4 * G2].bitcast(F32))
                link(dve.tensor_tensor(bias[4 * G2:ROWS], flat[4 * G2:ROWS], bhi[4 * G2:ROWS].bitcast(F32),
                                       ALU.subtract))
                dve.memset(m1[:], 0.0).then_inc(prep_done, 1)
                dve.wait_ge(prep_done, 1)

                def x3(k, u, i):
                    wait(dve, x2_in[u][i], k * 16 + 16)
                    xv = xview(k, u, i).rearrange("p v (j w) -> p v j w", j=JR)
                    dve.tensor_tensor(xv, natural(x2[u][i][:]), xv, ALU.add).then_inc(s["x3"], 1)

                def z_of(k, u, q, h):
                    i, ep = divmod(q, EP)
                    t = 2 * k + u
                    wait(dve, s["bcast"], (t * UNITS + q) * 2 + h + 1)
                    wait(dve, s["zmm"], t * UNITS + q - 1)
                    if ep == 0 and h == 0:
                        wait(dve, nd_in[u][i], (k + 1) * ND_SEM)
                    dve.tensor_tensor(Z[q % 2][h][:], pg[q % 2][h][:], nd[u][i][:, h, :], ALU.mult
                                      ).then_inc(s["z"], 1)

                def y_of(k, u, i):
                    n = (2 * k + u) * 2 + i
                    wait(dve, s["zmm"], (n + 1) * EP)
                    wait(dve, y_st[i], (2 * k + u) * 32)
                    dve.tensor_tensor(natural(yo[i][:]), po[i][:].rearrange("p (v j w) -> p v j w", v=2, j=JR),
                                      xview(k, u, i).rearrange("p v (j w) -> p v j w", j=JR), ALU.add
                                      ).then_inc(s["y"], 1)

                def choose(k, u, n):
                    t = 2 * k + u
                    revb = rev[:].unsqueeze(1).to_broadcast(wide)

                    def linked(instruction, count):
                        instruction.then_inc(chain, 1)

                    def before(count):
                        dve.wait_ge(chain, t * LINKS + count)

                    if n == 0:
                        wait(dve, s["scaled"], t + 1)
                        linked(dve.tensor_reduce(m1[:], L[:], AXX, ALU.max), 1)
                    elif n == 1:
                        before(1)
                        dve.tensor_tensor(L[:], L[:], over(m1[:]), ALU.subtract).then_inc(s["shifted"], 1)
                    elif n == 2:
                        dve.wait_ge(s["shifted"], t + 1)
                        linked(dve.scalar_tensor_tensor(A_[:], L[:], 0.0, revb, ALU.is_equal, ALU.mult), 2)
                    elif n == 3:
                        before(2)
                        linked(dve.tensor_reduce(m1[:], A_[:], AXX, ALU.max), 3)
                    elif n == 4:
                        wait(dve, s["gates"], t)
                        before(3)
                        linked(dve.tensor_tensor(F1[:], A_[:], over(m1[:]), ALU.is_equal), 4)
                    elif n == 5:
                        wait(dve, s["exp"], t + 1)
                        before(4)
                        linked(dve.scalar_tensor_tensor(L[:], F1[:], NEVER, L[:], ALU.mult, ALU.add), 5)
                    elif n == 6:
                        before(5)
                        linked(dve.tensor_reduce(m1[:], L[:], AXX, ALU.max), 6)
                    elif n == 7:
                        before(6)
                        linked(dve.tensor_tensor(A_[:], L[:], over(m1[:]), ALU.is_equal), 7)
                    elif n == 8:
                        before(7)
                        linked(dve.tensor_tensor(A_[:], A_[:], revb, ALU.mult), 8)
                    elif n == 9:
                        before(8)
                        linked(dve.tensor_reduce(m1[:], A_[:], AXX, ALU.max), 9)
                    elif n == 10:
                        before(9)
                        dve.tensor_tensor(F2[:], A_[:], over(m1[:]), ALU.is_equal).then_inc(s["chosen"], 1)
                    elif n == 11:
                        wait(dve, s["weighed"], t + 1)
                        linked(dve.tensor_reduce(total[:], F1[:], AXX, ALU.add), 10)
                    elif n == 12:
                        before(10)
                        dve.reciprocal(total[:], total[:]).then_inc(s["inverse"], 1)

                slots = [((0,), (1,)), ((2,), ()), ((3,), (4,)), ((5,), (6,)), ((7,), (8,)), ((9,), (10,)), ((), (11,)), ((), (12,))]

                def step(k, u):
                    after, before, ex, last = (back(k, u, d, 2) for d in (-1, 1, 3, 4))
                    for q in range(UNITS):
                        if now(*after) and q == 6:
                            x3(*after, 0)
                        if now(k, u) and q == 1:
                            x3(k, u, 1)
                        if now(*last) and q == 0:
                            y_of(*last, 1)
                        if now(*ex) and q == 5:
                            y_of(*ex, 0)
                        for h in range(2):
                            if now(*ex):
                                z_of(*ex, q, h)
                            if now(*before):
                                for n in slots[q][h]:
                                    choose(*before, n)
                x3(0, 0, 0)
                steps(dve, step, tail=1)


class Shared:
    pass


def metaformer_kernel(nc, a, out):
    g = Shared()
    with ExitStack() as ctx:
        m = Mem(nc, ctx, "g")
        g.x1s = nc.dram_tensor("x1s", [CHUNKS, P, N], F32).ap()
        g.x1tok = nc.dram_tensor("x1tok", [B, HP, W, P], F32).ap()
        g.x2s = nc.dram_tensor("x2s", [CHUNKS, P, N], F32).ap()
        g.Cm, g.J = m.sb("Cm", [P, P]), m.sb("J", [P, P])
        g.eps = m.sb("eps", [P, 2])
        g.b1, g.gate_b = m.sb("b1", [C, 1]), m.sb("gate_b", [P, 1])
        g.experts_loaded, g.settled = m.sem("experts_loaded"), m.sem("settled")
        g.X = m.sb("X", [P, 2 * SLOT])
        v = Views(g.X, 0)
        g.xr = [v.take(N) for _ in range(8)]
        g.sq, g.rr, g.nn, g.tsq = ([v.take(N) for _ in range(2)] for _ in range(4))
        g.lowS = [v.take(N // 2, parts=C + 1) for _ in range(2)]
        g.ts = [v.take(N) for _ in range(4)]
        g.trs = v.take(N)
        v = Views(g.X, 2 * (TOK + PAD))
        g.W1, g.W2 = v.take(E0, HID), v.take(E0, 2, C)
        g.ident, g.Alow, g.Brec, g.Gc = v.take(P), v.take(2, C), v.take(2, P), v.take(2 * E0)
        g.w2bias = v.take(C, parts=E0)
        g.small_at = v.at
        with ExitStack() as early:
            me = Mem(nc, early, "g")
            g.E = me.sb("E", [P, 2 * TOK + PAD])
            setup_block0(nc, g, a)
            wavelet_mixer(nc, g, a)
            g.D = me.sb("D", [P, B, P])
            expert_choice(nc, g, a)
            apply_choice(nc, g, a)
        with ExitStack() as mid:
            mm = Mem(nc, mid, "g")
            g.Thi = [mm.sb(f"Thi{i}", [P, ND * P], F32R) for i in range(4)]
            g.Tlo = [mm.sb(f"Tlo{i}", [P, ND * P], F32R) for i in range(4)]
            g.yh, g.yl = mm.sb("yh", [P, B, 68], F32R), mm.sb("yl", [P, B, 68], F32R)
            g.ybuf = [mm.sb(f"yb{r}", [P, B, 64]) for r in range(2)]
            g.scan_sems = [[mm.sem(f"{n}{r}") for n in ("hi", "full", "lo", "conv", "turned")] for r in range(2)]
            scan_weights(nc, g, a)
            for i in range(4):
                scan_pass(nc, g, i)
        top2_mixture(nc, g, a, out)


_INPUTS = {"x": "x", "s_ll": "L0_conv_s_ll", "s_lh": "L0_conv_s_lh", "s_hl": "L0_conv_s_hl",
           "s_hh": "L0_conv_s_hh", "w1": "L0_conv_w1", "b1": "L0_conv_b1", "w2": "L0_conv_w2",
           "b2": "L0_conv_b2", "gate_w": "L0_ffn_gate_w", "gate_b": "L0_ffn_gate_b",
           "weight1": "L0_ffn_weight1", "weight2": "L0_ffn_weight2", "w_ud": "L1_conv_w_ud",
           "w_du": "L1_conv_w_du", "w_lr": "L1_conv_w_lr", "w_rl": "L1_conv_w_rl",
           "router_w": "L1_ffn_router_w", "router_b": "L1_ffn_router_b",
           "expert_w": "L1_ffn_expert_w", "expert_b": "L1_ffn_expert_b"}


def kernel(**inputs):
    import concourse.bacc as bacc
    from concourse.bass_utils import run_bass_kernel_spmd

    nc = bacc.Bacc("TRN2", target_bir_lowering=False, num_devices=1)
    arrays, args = {}, {}
    for short, name in _INPUTS.items():
        arr = np.ascontiguousarray(inputs[name])
        arrays[f"in_{name}"] = arr
        args[short] = nc.dram_tensor(f"in_{name}", arr.shape, mybir.dt.from_np(arr.dtype),
                                     kind="ExternalInput").ap()
    y = nc.dram_tensor("y", (B, C, H, W), F32, kind="ExternalOutput").ap()
    metaformer_kernel(nc, args, y)
    return run_bass_kernel_spmd(nc, [arrays], core_ids=[0]).results[0]["y"]
```

```python
import numpy as np

import concourse.bass as bass
from concourse import mybir
from contextlib import ExitStack

F32 = mybir.dt.float32
F32R = mybir.dt.float32r
BF16 = mybir.dt.bfloat16
U32 = mybir.dt.uint32
ACT = mybir.ActivationFunctionType
ALU = mybir.AluOpType
AXX = mybir.AxisListType.X

P = 128
B, C, H, W = 4, 64, 128, 128
HP, WP = H // 2, W // 2
JR = 4
N = JR * W
NG = HP // JR
CHUNKS = NG * B
SLOT = B * HP * WP
TOK = HP * W
E0, HID, K0 = 32, 256, 8
E1 = 8
TAPS = 9
ND = 5
PAD = 8
SENTINEL = 2.0
EPS_C, EPS_T = 1e-6, 1e-5


def back(k, u, steps, unroll):
    return k + (u - steps) // unroll, (u - steps) % unroll


def valid(k, u, unroll, total):
    return not isinstance(k, int) or 0 <= k * unroll + u < total


def wait(engine, sem, count):
    if not isinstance(count, int) or count > 0:
        engine.wait_ge(sem, count)


def settle(engine, sem):
    engine.sem_inc(sem, 1)


def pipelined(engine, step, total, unroll, lag, tail=0, head=1):
    for t in range(head * unroll):
        step(t // unroll, t % unroll)
    with engine.Fori(head, total // unroll - tail) as k:
        for u in range(unroll):
            step(k, u)
    for t in range(total - tail * unroll, total + lag):
        step(t // unroll, t % unroll)


LN_EXP_SET = 6


def load_ln_exp(nc, act):
    act.add_instruction(mybir.InstLoadActFuncSet(
        act_func_set_id=LN_EXP_SET, name=nc.get_next_instruction_name(), engine=mybir.EngineType.Activation, ins=[], outs=[]))


class Chain:

    def __init__(self, engine, sem, base=0, count=0):
        self.engine, self.sem, self.base, self.count = engine, sem, base, count

    def __call__(self, instruction):
        self.count += 1
        instruction.then_inc(self.sem, 1)
        self.engine.wait_ge(self.sem, self.base + self.count)


def bcast(ap, axis, count):
    out = ap.unsqueeze(axis)
    shape = list(out.shape)
    shape[axis] = count
    return out.to_broadcast(shape)


class Mem:

    def __init__(self, nc, ctx, phase):
        self.nc, self.ctx, self.phase = nc, ctx, phase

    def sb(self, name, shape, dt=F32):
        return self.ctx.enter_context(self.nc.sbuf_tensor(f"{self.phase}_{name}", shape, dt))

    def ps(self, name, shape=(P, 512), dt=F32):
        return self.ctx.enter_context(self.nc.psum_tensor(f"{self.phase}_{name}", list(shape), dt))

    def sem(self, name):
        return self.ctx.enter_context(self.nc.semaphore(f"{self.phase}_{name}"))

    def sems(self, name, n):
        return [self.sem(f"{name}{i}") for i in range(n)]


MIX_LOADS = 2 + 12 + 1 + 2


def load_mixture(sp, g, a):
    def load(dst, src):
        sp.dma_start(dst, src, allow_slow_non_contiguous=True).then_inc(g.mix_loaded, 16)
    for h in range(2):
        load(g.wexp[h * C:h * C + C], a["expert_w"][h:E1:2].rearrange("p d c -> d p c"))
        load(g.rt[h * C:h * C + C, h * E1:h * E1 + E1], a["router_w"])
    for q in range(12):
        load(g.bn[q * E1:q * E1 + E1], a["expert_b"])
    load(g.rbias[:], a["router_b"].rearrange("(o e) -> o e", o=1).to_broadcast([P, E1]))


class Views:

    def __init__(self, tensor, at):
        self.tensor, self.at = tensor, at

    def take(self, *shape, parts=P):
        n = int(np.prod(shape))
        v = self.tensor[0:parts, self.at:self.at + n]
        self.at += n
        assert self.at <= self.tensor.shape[1]
        if len(shape) == 1:
            return v
        names = "abcde"[:len(shape)]
        sizes = {c: s for c, s in zip(names, shape)}
        return v.rearrange(f"p ({' '.join(names)}) -> p {' '.join(names)}", **sizes)


def setup_block0(nc, g, a):
    with ExitStack() as ctx:
        m = Mem(nc, ctx, "su")
        w1n = m.sb("w1n", [C, 4, 2, C])
        w2n = m.sb("w2n", [P, 4, C + 1])
        s4 = m.sb("s4", [P, 4])
        gwn = m.sb("gwn", [E0, 2, C])
        es = m.sb("es", [P, 4])
        sg = m.sb("sg", [P, 1])
        tmp = m.sb("tmp", [P, 4, C + 1])
        bcomb = m.sb("bcomb", [P, 2, C + 1])
        gtb = m.sb("gtb", [P, 2 * E0])
        psT = m.ps("psT")
        psG = m.ps("psG")
        psB = m.ps("psB")
        loaded, ident_ready, const_ready = m.sem("loaded"), m.sem("ident"), m.sem("const")
        turned, gate_blocks, gate_centred = m.sem("turned"), m.sem("gblk"), m.sem("gcen")
        rec_ready, rec_turned, exp_ready, chain, done = (
            m.sem("rec"), m.sem("recT"), m.sem("es"), m.sem("chain"), m.sem("done"))
        NL = 2 * 8 + 1 + 4 + 1
        with nc.Block() as block:
            @block.sync
            def _(sp):
                def load(dst, src):
                    sp.dma_start(dst, src, allow_slow_non_contiguous=True).then_inc(loaded, 16)

                for h in range(2):
                    part = slice(h * C, h * C + C)
                    load(w1n[:, :, h], a["w1"].rearrange("o (j c) -> o j c", j=4))
                    load(gwn[:, h], a["gate_w"])
                    load(w2n[part, :, 0:C], a["w2"].rearrange("(j c) o -> c j o", j=4))
                    load(w2n[part, :, C:C + 1], a["b2"].rearrange("(j c o) -> c j o", j=4, o=1))
                    for j, s in enumerate(("s_ll", "s_lh", "s_hl", "s_hh")):
                        load(s4[part, j:j + 1], a[s].rearrange("(c o) -> c o", o=1))
                load(g.b1[:], a["b1"].rearrange("(c o) -> c o", o=1))
                for q in range(4):
                    load(g.gate_b[q * E0:q * E0 + E0, :], a["gate_b"].rearrange("(e o) -> e o", o=1))
                load(g.w2bias, a["weight2"][:, HID:HID + 1, :].rearrange("e h o -> e (h o)"))
                sp.wait_ge(loaded, 16 * NL)

            @block.gpsimd
            def _(pool):
                pool.memset(g.ident, 0.0).then_inc(ident_ready, 1)
                pool.wait_ge(ident_ready, 1)
                pool.affine_select(out=g.ident, in_=g.ident, compare_op=ALU.not_equal, fill=1.0,
                                   base=0, pattern=[[-1, P]], channel_multiplier=1).then_inc(ident_ready, 1)

            @block.vector
            def _(dve):
                link = Chain(dve, chain)
                link(dve.memset(g.J[:], 0.0))
                dve.memset(g.J[0:C, 0:C], 1.0 / C)
                dve.memset(g.J[C:P, C:P], 1.0 / C)
                dve.memset(g.eps[:, 0:1], EPS_C)
                dve.memset(g.eps[:, 1:2], EPS_T)
                dve.memset(gtb[:], 0.0)
                for low in g.lowS:
                    dve.memset(low[C:C + 1], 1.0)
                dve.memset(g.E[:, TOK:TOK + PAD], SENTINEL)
                dve.memset(sg[0:C], 1.0)
                link(dve.memset(sg[C:P], -1.0))
                dve.wait_ge(ident_ready, 2)
                dve.tensor_tensor(g.Cm[:], g.ident, g.J[:], ALU.subtract).then_inc(const_ready, 1)
                dve.wait_ge(loaded, 16 * NL)
                dve.scalar_tensor_tensor(tmp[:, 0], w2n[:, 1], sg[:], w2n[:, 0], ALU.mult, ALU.add)
                link(dve.scalar_tensor_tensor(tmp[:, 1], w2n[:, 3], sg[:], w2n[:, 2], ALU.mult, ALU.add))
                dve.tensor_tensor(tmp[:, 2], tmp[:, 0], tmp[:, 1], ALU.add)
                link(dve.tensor_tensor(tmp[:, 3], tmp[:, 0], tmp[:, 1], ALU.subtract))
                dve.tensor_scalar(bcomb[:], tmp[:, 2:4], 0.5, None, ALU.mult).then_inc(rec_ready, 1)
                dve.wait_ge(turned, 1)
                for h in range(2):
                    last = dve.tensor_copy(gtb[h * C:h * C + C, h * E0:h * E0 + E0],
                                           psG[h * C:h * C + C, 0:E0])
                last.then_inc(gate_blocks, 1)
                dve.wait_ge(exp_ready, 1)
                link(dve.tensor_scalar(es[:], es[:], 0.5, None, ALU.mult))
                dve.tensor_tensor(es[:, 1:2], es[:, 1:2], sg[:], ALU.mult)
                link(dve.tensor_tensor(es[:, 3:4], es[:, 3:4], sg[:], ALU.mult))
                T = psT[:, 0:4 * C].rearrange("p (j o) -> p j o", j=4)
                dve.tensor_scalar(tmp[:, 0, 0:C], T[:, 0], es[:, 0:1], None, ALU.mult)
                link(dve.tensor_scalar(tmp[:, 1, 0:C], T[:, 2], es[:, 2:3], None, ALU.mult))
                dve.scalar_tensor_tensor(tmp[:, 2, 0:C], T[:, 1], es[:, 1:2], tmp[:, 0, 0:C], ALU.mult, ALU.add)
                link(dve.scalar_tensor_tensor(tmp[:, 3, 0:C], T[:, 3], es[:, 3:4], tmp[:, 1, 0:C],
                                              ALU.mult, ALU.add))
                dve.tensor_tensor(g.Alow[:, 0], tmp[:, 2, 0:C], tmp[:, 3, 0:C], ALU.add)
                link(dve.tensor_tensor(g.Alow[:, 1], tmp[:, 2, 0:C], tmp[:, 3, 0:C], ALU.subtract))
                dve.wait_ge(rec_turned, 1)
                link(dve.tensor_copy(g.Brec[0:C + 1],
                                     psB[0:C + 1, 0:2 * P].rearrange("p (v c) -> p v c", v=2)))
                dve.wait_ge(gate_centred, 1)
                link(dve.tensor_copy(g.Gc, psG[:, 256:256 + 2 * E0]))

            @block.scalar
            def _(act):
                act.wait_ge(loaded, 16 * NL)
                act.activation(es[:], s4[:], ACT.Exp).then_inc(exp_ready, 1)

            @block.tensor
            def _(pe):
                pe.wait_ge(ident_ready, 2)
                pe.wait_ge(loaded, 16 * NL)
                for j in range(4):
                    pe.transpose(psT[:, j * C:j * C + C], w1n[:, j].rearrange("o h c -> o (h c)"), g.ident[0:C, 0:C])
                pe.transpose(psG[:, 0:E0], gwn[:].rearrange("e h c -> e (h c)"), g.ident[0:E0, 0:E0]).then_inc(turned, 1)
                pe.wait_ge(rec_ready, 1)
                for v in range(2):
                    last = pe.transpose(psB[0:C + 1, v * P:v * P + P], bcomb[:, v], g.ident)
                last.then_inc(rec_turned, 1)
                pe.wait_ge(const_ready, 1)
                pe.wait_ge(gate_blocks, 1)
                pe.matmul(psG[:, 256:256 + 2 * E0], g.Cm[:], gtb[:], start=True, stop=True,
                          ).then_inc(gate_centred, 1)


def wavelet_mixer(nc, g, a):
    U = 8
    S_VAR, S_LOW, S_REC, S_TOK, S_TVAR = 1, 2, 3, 4, 5
    AHEAD = 2
    LAG = S_TVAR + 1
    with ExitStack() as ctx:
        m = Mem(nc, ctx, "wm")
        xc = [m.ps("xc0"), m.ps("xc1")]
        vl, rec, tc, tt, lg, tv = (m.ps(n) for n in ("vl", "rec", "tc", "tt", "lg", "tv"))
        xin, x1_out, tok_out = m.sems("xin", U), m.sems("x1o", U), m.sems("tko", 4)
        s = {n: m.sem(n) for n in (
            "centred", "squared", "var", "lnv", "rstd", "normed", "low", "low_s", "rec", "x1",
            "high", "parts", "xhigh", "xparts", "x1high", "x1parts", "tcentred", "tsquared", "tturned", "tcopied", "logits", "tvar", "tln", "trstd", "glog")}
        xh, xl, x1h, x1l, sq_hi, sq_lo = (m.sb(n, [P, N], F32R) for n in ("xh", "xl", "x1h", "x1l", "sqh", "sql"))
        Jr, Cmr, exact_ready = m.sb("Jr", [P, P], F32R), m.sb("Cmr", [P, P], F32R), m.sem("exact")
        xr, sq, rr, nn, lowS, tsq, ts, trs = g.xr, g.sq, g.rr, g.nn, g.lowS, g.tsq, g.ts, g.trs
        x_src = a["x"].rearrange("b c (j t) w -> b t c j w", t=2)
        tok_dst = g.x1tok.rearrange("b j w x -> b w j x")
        with nc.Block() as block:
            @block.sync
            def _(sp):
                def load(k, u):
                    wait(sp, x1_out[u], k * 16)
                    settle(sp, g.settled)
                    wait(sp, s["logits"], k * U + u - U + 1)
                    wait(sp, s["tturned"], k * U + u - U + 1)
                    rows = k * (JR * U // B) + (u // B) * JR
                    for t in range(2):
                        sp.dma_start(xr[u][t * C:t * C + C].rearrange("p (j w) -> p j w", j=JR),
                                     x_src[u % B, t][:, bass.ds(rows, JR), :]).then_inc(xin[u], 16)

                def load_experts(q):
                    e = slice(q * E0 // U, (q + 1) * E0 // U)
                    sp.dma_start(g.W1[0:C + 1, e], a["weight1"][e].rearrange("e d h -> d e h")
                                 ).then_inc(g.experts_loaded, 16)
                    for t in range(2):
                        sp.dma_start(g.W2[:, e, t, :], a["weight2"][e, t * P:t * P + P, :].rearrange(
                            "e p o -> p e o")).then_inc(g.experts_loaded, 16)

                def step(k, u):
                    kk, uu = back(k, u, -AHEAD, U)
                    if valid(kk, uu, U, CHUNKS):
                        load(kk, uu)
                    if isinstance(k, int) and k == 0:
                        load_experts(u)
                    k3, u3 = back(k, u, S_REC, U)
                    if valid(k3, u3, U, CHUNKS):
                        wait(sp, s["x1"], k3 * U + u3 + 1)
                        sp.dma_start(g.x1s[bass.ds(k3 * U + u3, 1)].rearrange("t p n -> p (t n)"),
                                     xr[u3]).then_inc(x1_out[u3], 16)
                    k4, u4 = back(k, u, S_TOK, U)
                    if valid(k4, u4, U, CHUNKS):
                        wait(sp, s["tcopied"], k4 * U + u4 + 1)
                        rows = k4 * (JR * U // B) + (u4 // B) * JR
                        sp.dma_start(tok_dst[u4 % B][:, bass.ds(rows, JR), :],
                                     ts[u4 % 4].rearrange("p (j x) -> p j x", j=JR)
                                     ).then_inc(tok_out[u4 % 4], 16)
                for u in range(AHEAD):
                    load(0, u)
                pipelined(sp, step, CHUNKS, U, LAG, tail=1)
                for u in range(U):
                    sp.wait_ge(x1_out[u], 16 * (CHUNKS // U))
                for u in range(4):
                    sp.wait_ge(tok_out[u], 16 * (CHUNKS // 4))

            @block.tensor
            def _(pe):
                pe.wait_ge(exact_ready, 1)
                def step(k, u):
                    c3, u3 = back(k, u, S_REC, U)
                    if valid(c3, u3, U, CHUNKS):
                        n = c3 * U + u3
                        wait(pe, s["low_s"], n + 1)
                        wait(pe, s["x1"], n)
                        for v in range(2):
                            last = pe.matmul(rec[:, v * (N // 2):(v + 1) * (N // 2)], g.Brec[0:C + 1, v],
                                             lowS[u3 % 2], start=True, stop=True)
                        last.then_inc(s["rec"], 1)
                    c5, u5 = back(k, u, S_TVAR, U)
                    if valid(c5, u5, U, CHUNKS) and u5 % 2 == 1:
                        pair = c5 * (U // 2) + u5 // 2
                        wait(pe, s["tsquared"], 2 * pair + 2)
                        wait(pe, s["tln"], pair)
                        for half in range(2):
                            last = pe.matmul(tv[half * C:half * C + C, :], g.J[:, C - E0:C + E0],
                                             tsq[half], start=True, stop=True)
                        last.then_inc(s["tvar"], 2)
                        wait(pe, s["glog"], pair)
                        for half in range(2):
                            last = pe.matmul(lg[half * C:half * C + C, :], g.Gc, xr[u5 - 1 + half],
                                             start=True, stop=True)
                        last.then_inc(s["logits"], 2)
                    c4, u4 = back(k, u, S_TOK, U)
                    if valid(c4, u4, U, CHUNKS):
                        n = c4 * U + u4
                        wait(pe, s["x1parts"], n + 1)
                        wait(pe, s["tsquared"], n)
                        pe.matmul(tc[:], Cmr[:], x1h[:], start=True, stop=False)
                        pe.matmul(tc[:], Cmr[:], x1l[:], start=False, stop=True).then_inc(s["tcentred"], 1)
                        wait(pe, s["tcopied"], n)
                        for j in range(JR):
                            last = pe.transpose(tt[:, j * P:j * P + P], xr[u4][:, j * W:j * W + W], g.ident)
                        last.then_inc(s["tturned"], 1)
                    c2, u2 = back(k, u, S_LOW, U)
                    if valid(c2, u2, U, CHUNKS):
                        n = c2 * U + u2
                        wait(pe, s["normed"], n + 1)
                        wait(pe, s["lnv"], n + 1)
                        nv = nn[u2 % 2].rearrange("p (q v) -> p v q", v=2)
                        for v in range(2):
                            last = pe.matmul(vl[0:C, 0:N // 2], g.Alow[:, v], nv[:, v],
                                             start=(v == 0), stop=(v == 1))
                        last.then_inc(s["low"], 1)
                    if valid(k, u, U, CHUNKS):
                        n = k * U + u
                        wait(pe, s["xparts"], n + 1)
                        wait(pe, s["normed"], n - 1)
                        pe.matmul(xc[u % 2][:], Cmr[:], xh[:], start=True, stop=False)
                        pe.matmul(xc[u % 2][:], Cmr[:], xl[:], start=False, stop=True
                                  ).then_inc(s["centred"], 1)
                    c1, u1 = back(k, u, S_VAR, U)
                    if valid(c1, u1, U, CHUNKS):
                        n = c1 * U + u1
                        wait(pe, s["parts"], n + 1)
                        wait(pe, s["low_s"], n)
                        wait(pe, s["lnv"], n)
                        pe.matmul(vl[:], Jr[:], sq_hi[:], start=True, stop=False)
                        pe.matmul(vl[:], Jr[:], sq_lo[:], start=False, stop=True
                                  ).then_inc(s["var"], 1)
                pipelined(pe, step, CHUNKS, U, LAG)

            @block.scalar
            def _(act):
                load_ln_exp(nc, act)

                def step(k, u):
                    c5, u5 = back(k, u, S_TVAR, U)
                    if valid(c5, u5, U, CHUNKS) and u5 % 2 == 1:
                        pair = c5 * (U // 2) + u5 // 2
                        wait(act, s["tvar"], 2 * pair + 2)
                        wait(act, s["glog"], pair)
                        act.activation(trs, tv[:], ACT.Ln, bias=g.eps[:, 1:2]).then_inc(s["tln"], 1)
                        act.wait_ge(s["tln"], pair + 1)
                        act.activation(trs, trs, ACT.Exp, scale=-0.5).then_inc(s["trstd"], 1)
                    c4, u4 = back(k, u, S_TOK, U)
                    if valid(c4, u4, U, CHUNKS):
                        n = c4 * U + u4
                        wait(act, s["tcentred"], n + 1)
                        wait(act, s["tvar"], n - 1)
                        act.activation(tsq[u4 % 2], tc[:], ACT.Square).then_inc(s["tsquared"], 1)
                    c2, u2 = back(k, u, S_LOW, U)
                    if valid(c2, u2, U, CHUNKS):
                        n = c2 * U + u2
                        wait(act, s["low"], n + 1)
                        wait(act, s["rec"], n - 1)
                        act.activation(lowS[u2 % 2][0:C], vl[0:C, 0:N // 2], ACT.Identity,
                                       bias=g.b1[:]).then_inc(s["low_s"], 1)
                    if valid(k, u, U, CHUNKS):
                        n = k * U + u
                        wait(act, s["centred"], n + 1)
                        wait(act, s["var"], n - 1)
                        act.activation(sq[u % 2], xc[u % 2][:], ACT.Square).then_inc(s["squared"], 1)
                    c1, u1 = back(k, u, S_VAR, U)
                    if valid(c1, u1, U, CHUNKS):
                        n = c1 * U + u1
                        wait(act, s["var"], n + 1)
                        wait(act, s["normed"], n - 1)
                        act.activation(rr[u1 % 2], vl[:], ACT.Ln, bias=g.eps[:, 0:1]).then_inc(s["lnv"], 1)
                        act.wait_ge(s["lnv"], n + 1)
                        act.activation(rr[u1 % 2], rr[u1 % 2], ACT.Exp, scale=-0.5).then_inc(s["rstd"], 1)
                pipelined(act, step, CHUNKS, U, LAG)

            @block.gpsimd
            def _(pool):
                def low_part(c, u, source, high, low, ready, done):
                    wait(pool, s[ready], c * U + u + 1)
                    pool.tensor_tensor(low[:], source, high[:].bitcast(F32), ALU.subtract).then_inc(s[done], 1)

                def step(k, u):
                    c3, u3 = back(k, u, S_REC, U)
                    if valid(c3, u3, U, CHUNKS):
                        low_part(c3, u3, xr[u3], x1h, x1l, "x1high", "x1parts")
                    kk, uu = back(k, u, -1, U)
                    if valid(kk, uu, U, CHUNKS):
                        low_part(kk, uu, xr[uu], xh, xl, "xhigh", "xparts")
                    if valid(k, u, U, CHUNKS):
                        low_part(k, u, sq[u % 2], sq_hi, sq_lo, "high", "parts")
                low_part(0, 0, xr[0], xh, xl, "xhigh", "xparts")
                pipelined(pool, step, CHUNKS, U, LAG, tail=1)

            @block.vector
            def _(dve):
                dve.tensor_copy(Cmr[:], g.Cm[:])
                dve.tensor_copy(Jr[:], g.J[:]).then_inc(exact_ready, 1)

                def high_of_x(k, u):
                    wait(dve, xin[u], k * 32 + 32)
                    wait(dve, s["centred"], k * U + u)
                    dve.tensor_copy(xh[:], xr[u]).then_inc(s["xhigh"], 1)

                def step(k, u):
                    c2, u2 = back(k, u, S_LOW, U)
                    if valid(c2, u2, U, CHUNKS):
                        n = c2 * U + u2
                        wait(dve, s["rstd"], n + 1)
                        wait(dve, s["low"], n - 1)
                        dve.tensor_tensor(nn[u2 % 2], xc[u2 % 2][:], rr[u2 % 2], ALU.mult
                                          ).then_inc(s["normed"], 1)
                    c3, u3 = back(k, u, S_REC, U)
                    if valid(c3, u3, U, CHUNKS):
                        n = c3 * U + u3
                        wait(dve, s["rec"], n + 1)
                        xv = xr[u3].rearrange("p (q v) -> p v q", v=2)
                        dve.tensor_tensor(xv, rec[:].rearrange("p (v q) -> p v q", v=2), xv, ALU.add
                                          ).then_inc(s["x1"], 1)
                    c5, u5 = back(k, u, S_TVAR, U)
                    if valid(c5, u5, U, CHUNKS) and u5 % 2 == 1:
                        pair = c5 * (U // 2) + u5 // 2
                        p = (u5 % B) // 2
                        wait(dve, s["trstd"], pair + 1)
                        wait(dve, s["logits"], 2 * pair + 2)
                        at = p * (TOK + PAD) + (c5 * (U // B) + u5 // B) * N
                        dve.tensor_tensor(g.E[:, bass.ds(at, N)], lg[:], trs, ALU.mult
                                          ).then_inc(s["glog"], 1)
                    c4, u4 = back(k, u, S_TOK, U)
                    if valid(c4, u4, U, CHUNKS):
                        n = c4 * U + u4
                        wait(dve, s["tturned"], n + 1)
                        wait(dve, tok_out[u4 % 4], (c4 * 2 + u4 // 4) * 16)
                        dve.tensor_copy(ts[u4 % 4], tt[:]).then_inc(s["tcopied"], 1)
                    if valid(c3, u3, U, CHUNKS):
                        n = c3 * U + u3
                        wait(dve, s["tcentred"], n)
                        wait(dve, s["x1"], n + 1)
                        dve.tensor_copy(x1h[:], xr[u3]).then_inc(s["x1high"], 1)
                    kk, uu = back(k, u, -1, U)
                    if valid(kk, uu, U, CHUNKS):
                        high_of_x(kk, uu)
                    if valid(k, u, U, CHUNKS):
                        n = k * U + u
                        wait(dve, s["squared"], n + 1)
                        wait(dve, s["var"], n)
                        dve.tensor_copy(sq_hi[:], sq[u % 2]).then_inc(s["high"], 1)
                high_of_x(0, 0)
                pipelined(dve, step, CHUNKS, U, LAG, tail=1)


def expert_choice(nc, g, a):
    with ExitStack() as ctx:
        m = Mem(nc, ctx, "ec")
        v = Views(g.X, 0)
        e2 = [v.take(TOK + PAD), v.take(TOK + PAD)]
        v = Views(g.X, g.small_at)
        gath, xcg = v.take(2, K0, C), v.take(2, K0, C)
        sqg = gath
        mx, swapm, sel64, sele = v.take(2, 8), v.take(P), v.take(2 * E0), v.take(E0, B)
        own, oth, hpc, thr = v.take(2, 17), v.take(2, 17), v.take(1), v.take(K0)
        mg, nb, zt, rz, base = v.take(2), v.take(2), v.take(2), v.take(2), v.take(2)
        oT = v.take(2, 2, 2, E0)
        v.at -= 4 * K0 * K0
        cmp1, cmp2 = v.take(2, K0, K0), v.take(2, K0, K0)
        cnt, chosen, lst, lst2, wgt = (v.take(2, K0) for _ in range(5))
        jf = v.take(2, K0)
        mean, var, pooled = v.take(2, K0), v.take(2, K0), v.take(2, C)
        pT, hT = v.take(P), v.take(2, E0 * B)
        idx = m.sb("idx", [P, 2, K0], U32)
        jdx = m.sb("jdx", [P, 2, K0], U32)
        rows = m.sb("rows", [P, 2, K0], U32)
        psw, pso, psp, psh, pst = (m.ps(n) for n in ("psw", "pso", "psp", "psh", "pst"))
        chain, swap_ready, swapped, biased, exped, packed, swapped2, rows_ready, gathered = (
            m.sem(n) for n in ("chain", "swr", "sw", "nb", "exp", "pk", "sw2", "rows", "gath"))
        indexed, vln, vexp, pooled_r, poolT, pT_r, hid_r, hT_r, out_r, oT_r, outT_r, done = (
            m.sem(n) for n in ("mi", "vln", "vexp", "pool", "poolT", "pT", "hid", "hT", "out", "oT", "outT", "dn"))
        pair_of = [g.E[:, 0:TOK], g.E[:, TOK + PAD:2 * TOK + PAD]]
        padded = [g.E[:, 0:TOK + PAD], g.E[:, TOK:2 * TOK + PAD]]
        data_of = [e2[0][:, 0:TOK], e2[1][:, PAD:TOK + PAD]]
        with nc.Block() as block:
            @block.vector
            def _(dve):
                link = Chain(dve, chain)
                link(dve.memset(g.D[:], 0.0))
                for q in range(4):
                    part = slice(q * E0, q * E0 + E0)
                    dve.memset(hpc[part], float(P * (q % 2)))
                    for p in range(2):
                        dve.memset(base[part, p:p + 1], float((2 * p + q // 2) * 2 * TOK + q % 2))
                    dve.tensor_copy(swapm[:, q * E0:q * E0 + E0], g.ident[:, (q ^ 1) * E0:(q ^ 1) * E0 + E0])
                for i in range(K0):
                    dve.memset(thr[:, i:i + 1], float(K0 - i))
                for b2 in range(2):
                    dve.tensor_tensor(sel64[:, b2 * E0:b2 * E0 + E0],
                                      g.ident[:, 2 * b2 * E0:2 * b2 * E0 + E0],
                                      g.ident[:, (2 * b2 + 1) * E0:(2 * b2 + 2) * E0], ALU.add)
                dve.tensor_copy(sele[0:E0], bcast(g.ident[0:E0, 0:E0], 2, B))
                dve.memset(pT[C:C + 1], 1.0)
                for p in range(2):
                    last = dve.max(out=mx[:, p], in_=pair_of[p])
                link(last)
                dve.tensor_copy(mg, mx[:, :, 0]).then_inc(swap_ready, 1)
                dve.wait_ge(swap_ready, 1)
                dve.wait_ge(swapped, 1)
                link(dve.tensor_tensor(mg, psw[:, 0:2], mg, ALU.max))
                link(dve.tensor_scalar(nb, mg, g.gate_b[:], -1.0, ALU.add, ALU.mult))
                dve.tensor_scalar(nb, nb, g.gate_b[:], None, ALU.add).then_inc(biased, 1)
                for p in range(2):
                    dve.max_index(out=idx[:, p], in_max=mx[:, p], in_values=pair_of[p]).then_inc(indexed, 1)
                dve.wait_ge(indexed, 2)
                dve.tensor_single_scalar(jdx[:], idx[:], 7, ALU.logical_shift_right)
                link(dve.tensor_copy(own[:, :, K0:2 * K0], idx[:]))
                link(dve.tensor_copy(jf, jdx[:]))
                for p in range(2):
                    last = dve.tensor_scalar(rows[:, p], own[:, p, K0:2 * K0], 2.0, base[:, p:p + 1],
                                             ALU.mult, ALU.add)
                last.then_inc(rows_ready, 1)
                dve.wait_ge(exped, 4)
                link(dve.scalar_tensor_tensor(jf, jf, float(P), own[:, :, K0:2 * K0], ALU.mult, ALU.add))
                dve.tensor_scalar(own[:, :, K0:2 * K0], jf, hpc, None, ALU.add).then_inc(packed, 1)
                dve.wait_ge(packed, 1)
                dve.wait_ge(swapped2, 1)
                link(dve.tensor_copy(oth, pso[:, 0:34].rearrange("p (a b) -> p a b", a=2)))
                shape = [P, 2, K0, K0]
                mine = [own[:, :, i * K0:i * K0 + K0].unsqueeze(3).to_broadcast(shape) for i in range(2)]
                them = [oth[:, :, i * K0:i * K0 + K0].unsqueeze(2).to_broadcast(shape) for i in range(2)]
                dve.tensor_tensor(cmp1, them[0], mine[0], ALU.is_equal)
                link(dve.tensor_tensor(cmp2, them[1], mine[1], ALU.is_lt))
                link(dve.tensor_tensor(cmp1, cmp1, cmp2, ALU.mult))
                link(dve.tensor_tensor(cmp2, them[0], mine[0], ALU.is_gt))
                link(dve.tensor_tensor(cmp1, cmp1, cmp2, ALU.add))
                link(dve.tensor_reduce(cnt, cmp1, AXX, ALU.add))
                dve.tensor_tensor(zt, own[:, :, 16], oth[:, :, 16], ALU.add)
                link(dve.tensor_tensor(chosen, cnt, bcast(thr, 1, 2), ALU.is_lt))
                dve.reciprocal(rz, zt)
                dve.tensor_tensor(lst, chosen, own[:, :, 0:K0], ALU.mult)
                link(dve.tensor_scalar(lst2, chosen, -SENTINEL, SENTINEL, ALU.mult, ALU.add))
                dve.tensor_tensor(wgt, lst, bcast(rz, 2, K0), ALU.mult)
                link(dve.tensor_tensor(lst2, lst2, lst, ALU.add))
                link(dve.match_replace(out=e2[0], in_to_replace=lst2[:, 0], in_values=padded[0], imm_value=0.0))
                dve.wait_ge(gathered, 16 * 2 * K0)
                link(dve.tensor_reduce(mean, gath, AXX, ALU.add))
                link(dve.tensor_scalar(mean, mean, 1.0 / C, None, ALU.mult))
                link(dve.tensor_tensor(xcg, gath, bcast(mean, 3, C), ALU.subtract))
                link(dve.tensor_tensor(sqg, xcg, xcg, ALU.mult))
                link(dve.tensor_reduce(var, sqg, AXX, ALU.add))
                dve.tensor_scalar(var, var, 1.0 / C, None, ALU.mult).then_inc(vln, 1)
                dve.wait_ge(vexp, 2)
                link(dve.tensor_tensor(wgt, wgt, var, ALU.mult))
                link(dve.tensor_tensor(xcg, xcg, bcast(wgt, 3, C), ALU.mult))
                dve.tensor_reduce(pooled, xcg.rearrange("p a k c -> p a c k"), AXX, ALU.add
                                  ).then_inc(pooled_r, 1)
                dve.wait_ge(poolT, 1)
                dve.tensor_copy(pT[0:C], psp[0:C, 0:P]).then_inc(pT_r, 1)
                link(dve.match_replace(out=e2[1], in_to_replace=lst2[:, 1], in_values=padded[1], imm_value=0.0))
                for p in range(2):
                    dve.tensor_tensor(pair_of[p], pair_of[p], data_of[p], ALU.subtract).then_inc(done, 1)
                dve.wait_ge(out_r, 1)
                src = psp[0:C, 256:256 + E0 * B].rearrange("p (e a b) -> p a b e", e=E0, a=2)
                for h in range(2):
                    last = dve.tensor_copy(oT[0:C, :, :, h], src)
                last.then_inc(oT_r, 1)
                dve.wait_ge(outT_r, 1)
                for b in range(B):
                    p, b2 = divmod(b, 2)
                    for h in range(2):
                        q = slice((2 * b2 + h) * E0, (2 * b2 + h + 1) * E0)
                        last = dve.tensor_scalar(g.D[q, b, h * C:h * C + C], pst[q, p * C:p * C + C],
                                                 rz[q, p:p + 1], None, ALU.mult)
                last.then_inc(done, 1)
                dve.wait_ge(done, 3)

            @block.scalar
            def _(act):
                load_ln_exp(nc, act)
                act.wait_ge(biased, 1)
                for p in range(2):
                    act.activation(own[:, p, 0:K0], mx[:, p], ACT.Exp, bias=nb[:, p:p + 1]).then_inc(exped, 1)
                for p in range(2):
                    act.wait_ge(indexed, p + 1)
                    act.activation(pair_of[p], pair_of[p], ACT.Exp, bias=nb[:, p:p + 1],
                                   accum_out=own[:, p, 16:17]).then_inc(exped, 1)
                act.wait_ge(vln, 1)
                act.activation(var, var, ACT.Ln, bias=g.eps[:, 1:2]).then_inc(vexp, 1)
                act.wait_ge(vexp, 1)
                act.activation(var, var, ACT.Exp, scale=-0.5).then_inc(vexp, 1)
                act.wait_ge(hid_r, 1)
                act.activation(hT, psh[:, 0:2 * E0 * B].rearrange("p (t n) -> p t n", t=2), ACT.Gelu
                               ).then_inc(hT_r, 1)

            @block.gpsimd
            def _(pool):
                pool.wait_ge(rows_ready, 1)
                for p in range(2):
                    for i in range(K0):
                        pool.indirect_dma_start(
                            out=gath[:, p, i, :], out_offset=None,
                            in_=g.x1tok.rearrange("b j w (h c) -> (b j w h) c", h=2),
                            in_offset=bass.IndirectOffsetOnAxis(ap=rows[:, p, i:i + 1], axis=0),
                        ).then_inc(gathered, 16)

            @block.tensor
            def _(pe):
                pe.wait_ge(swap_ready, 1)
                pe.matmul(psw[:, 0:2], swapm, mg, start=True, stop=True).then_inc(swapped, 1)
                pe.wait_ge(packed, 1)
                pe.matmul(pso[:, 0:34], swapm, own.rearrange("p a b -> p (a b)"), start=True, stop=True
                          ).then_inc(swapped2, 1)
                pe.wait_ge(pooled_r, 1)
                for p in range(2):
                    last = pe.matmul(psp[0:C, p * 2 * E0:(p + 1) * 2 * E0], pooled[:, p], sel64,
                                     start=True, stop=True)
                last.then_inc(poolT, 1)
                pe.wait_ge(pT_r, 1)
                pe.wait_ge(g.experts_loaded, 16 * 3 * 8)
                pooled_of = pT[0:C + 1].rearrange("p (b e) -> p e b", b=B)
                for e in range(E0):
                    for t in range(2):
                        at = (t * E0 + e) * B
                        last = pe.matmul(psh[:, at:at + B], g.W1[0:C + 1, e, t * P:t * P + P],
                                         pooled_of[:, e], start=True, stop=True)
                last.then_inc(hid_r, 1)
                pe.wait_ge(hT_r, 1)
                out = psp[0:C, 256:256 + E0 * B]
                pe.matmul(out, g.w2bias, sele[0:E0].rearrange("p e b -> p (e b)"),
                          start=True, stop=False, skip_group_check=True)
                for e in range(E0):
                    for t in range(2):
                        last = pe.matmul(out[:, e * B:e * B + B], g.W2[:, e, t, :], hT[:, t, e * B:e * B + B],
                                         start=False, stop=(e == E0 - 1 and t == 1), skip_group_check=True)
                last.then_inc(out_r, 1)
                pe.wait_ge(oT_r, 1)
                for p in range(2):
                    last = pe.transpose(pst[:, p * C:p * C + C], oT[0:C, p].rearrange("p b h e -> p (b h e)"),
                                        g.ident[0:C, 0:C])
                last.then_inc(outT_r, 1)


def apply_and_first_scan(nc, g, a):
    LINES = 2 * JR
    BEHIND = LINES + 2
    SWITCH = NG // 2
    with ExitStack() as ctx:
        m = Mem(nc, ctx, "af")
        sq = [m.sb(f"sq{i}", [P, N]) for i in range(2)]
        dl, vv = m.ps("dl"), m.ps("vv")
        xc = [m.ps(f"xc{b}") for b in range(B)]
        ps = [m.ps(f"ps{r}") for r in range(2)]
        xin, x2_out = m.sems("xin", B), m.sems("x2o", B)
        s = {n: m.sem(n) for n in ("delta", "x2", "centred", "squared", "var", "lnv", "rstd", "normed")}
        s.update(zip(("hi", "full", "lo", "conv"), g.scan_sems[0]))
        Xv = g.X[:].rearrange("p (s n) -> p s n", s=2)
        Xl = g.X[:].rearrange("p (s b j w) -> p s b j w", s=2, b=B, j=HP)
        early = [Xv[:, 1, (b + 1) * HP * WP - N:(b + 1) * HP * WP] for b in range(B)]
        late = [g.E[:, b * N:b * N + N] for b in range(B)]
        inner = slice(2, 2 + 64)

        def run(engine, body):
            def static(k):
                body(k, late if k >= SWITCH else early, late if k + 1 >= SWITCH else early)
            static(0)
            static(1)
            with engine.Fori(2, SWITCH - 1) as k:
                body(k, early, early)
            static(SWITCH - 1)
            with engine.Fori(SWITCH, NG - 1) as k:
                body(k, late, late)
            static(NG - 1)
            static(NG)

        def lines(k):
            return [(j, LINES * k - BEHIND + j) for j in range(LINES + 2 if isinstance(k, int) and k == NG else LINES)]

        def exists(k):
            return not isinstance(k, int) or k < NG

        with nc.Block() as block:
            @block.sync
            def _(sp):
                def load(k, b, buf):
                    wait(sp, x2_out[b], k * 16)
                    settle(sp, g.settled)
                    wait(sp, s["centred"], k * B + b - B + 1)
                    sp.dma_start(buf[b], g.x1s[bass.ds(k * B + b, 1)].rearrange("t p n -> p (t n)")
                                 ).then_inc(xin[b], 16)

                def body(k, buf, following):
                    for b in range(B):
                        if exists(k):
                            if b < 2:
                                load(k, b + 2, buf)
                            elif exists(k + 1):
                                load(k + 1, b - 2, following)
                            wait(sp, s["x2"], k * B + b + 1)
                            sp.dma_start(g.x2s[bass.ds(k * B + b, 1)].rearrange("t p n -> p (t n)"),
                                         buf[b]).then_inc(x2_out[b], 16)
                for sem in g.weight_sems:
                    sp.sem_clear(sem)
                for b in range(2):
                    load(0, b, early)
                run(sp, body)
                for b in range(B):
                    sp.wait_ge(x2_out[b], 16 * NG)

            @block.tensor
            def _(pe):
                def convolve(j, n):
                    out = ps[j % 2][:, 0:B * 64].rearrange("p (b w) -> p b w", b=B)
                    pe.wait_ge(s["hi"], n)
                    for t in (g.Tlo[0], g.Thi[0]):
                        for d in range(ND):
                            pe.matmul(out, t[:, d * P:d * P + P], g.yh[:, :, d:d + 64],
                                      start=(t is g.Tlo[0] and d == 0), stop=False)
                    pe.wait_ge(s["lo"], n)
                    for d in range(ND):
                        last = pe.matmul(out, g.Thi[0][:, d * P:d * P + P], g.yl[:, :, d:d + 64],
                                         start=False, stop=(d == ND - 1))
                    last.then_inc(s["conv"], 1)

                def delta(k, b):
                    wait(pe, s["x2"], k * B + b)
                    pe.matmul(dl[:], g.D[:, b], g.E[:, bass.ds((b // 2) * (TOK + PAD) + k * N, N)],
                              start=True, stop=True).then_inc(s["delta"], 1)

                def centre(k, b, buf):
                    wait(pe, s["x2"], k * B + b + 1)
                    wait(pe, s["normed"], k * B + b + 1 - B)
                    src = buf[b].rearrange("p (q v) -> p v q", v=2)
                    for h in range(2):
                        for v in range(2):
                            last = pe.matmul(xc[b][v * C:v * C + C, h * (N // 2):(h + 1) * (N // 2)],
                                             g.Cm[:, h * C:h * C + C], src[:, v], start=True, stop=True)
                    last.then_inc(s["centred"], 1)

                def variance(n, b):
                    wait(pe, s["squared"], n + 1)
                    wait(pe, s["lnv"], n)
                    pe.matmul(vv[:], g.J[:], sq[b % 2][:], start=True, stop=True).then_inc(s["var"], 1)

                def body(k, buf, following):
                    for j, n in lines(k):
                        if not isinstance(n, int) or n >= 1:
                            convolve(j, n)
                        b = j // 2
                        if j % 2 == 0 and exists(k):
                            delta(k, b)
                        if j % 2 == 0 and (exists(k) or j == 0) and not (isinstance(k, int) and k * B + b == 0):
                            variance(k * B + b - 1, (b - 1) % B)
                        if j % 2 == 1 and exists(k):
                            centre(k, b, buf)
                run(pe, body)

            @block.scalar
            def _(act):
                load_ln_exp(nc, act)

                def body(k, buf, following):
                    for b in range(B):
                        n = k * B + b
                        if (exists(k) or b == 0) and not (isinstance(n, int) and n == 0):
                            wait(act, s["var"], n)
                            old = sq[(b - 1) % 2][:]
                            act.activation(old, vv[:], ACT.Ln, bias=g.eps[:, 0:1]).then_inc(s["lnv"], 1)
                            act.wait_ge(s["lnv"], n)
                            act.activation(old, old, ACT.Exp, scale=-0.5).then_inc(s["rstd"], 1)
                        if exists(k):
                            wait(act, s["centred"], n + 1)
                            wait(act, s["normed"], n - 1)
                            act.activation(sq[b % 2][:], xc[b][:], ACT.Square).then_inc(s["squared"], 1)
                run(act, body)

            @block.vector
            def _(dve):
                def split(x, n):
                    dve.wait_ge(s["hi"], n + 1)
                    wait(dve, s["full"], n)
                    dve.tensor_tensor(g.yl[:, :, inner], x, g.yh[:, :, inner].bitcast(F32), ALU.subtract
                                      ).then_inc(s["lo"], 1)

                def scan_line(k, j, n):
                    jj = JR * k - BEHIND // 2 + j // 2
                    x = Xl[:, j % 2, :, bass.ds(jj, 1), :].rearrange("p b j w -> p b (j w)")
                    if j == 2:
                        wait(dve, s["normed"], k * B)
                    if isinstance(n, int) and n == 0:
                        dve.tensor_copy(g.yh[:, :, inner], x).then_inc(s["hi"], 1)
                        split(x, 0)
                        return
                    conv = ps[j % 2][:, 0:B * 64].rearrange("p (b w) -> p b w", b=B)
                    dve.wait_ge(s["conv"], n)
                    dve.scalar_tensor_tensor(g.yh[:, :, inner], conv, 0.0, x, ALU.max, ALU.add
                                             ).then_inc(s["hi"], 1)
                    dve.scalar_tensor_tensor(x, conv, 0.0, x, ALU.max, ALU.add).then_inc(s["full"], 1)
                    split(x, n)

                def norm(k, b, n):
                    kk, bb = back(k, b, 1, B)
                    wait(dve, s["rstd"], n + 1)
                    at = bb * HP * WP + kk * (JR * WP)
                    dve.tensor_tensor(Xv[:, :, bass.ds(at, JR * WP)],
                                      xc[bb][:].rearrange("p (s n) -> p s n", s=2),
                                      sq[bb % 2][:].rearrange("p (s n) -> p s n", s=2), ALU.mult
                                      ).then_inc(s["normed"], 1)

                def body(k, buf, following):
                    for j, n in lines(k):
                        if not isinstance(n, int) or n >= 0:
                            scan_line(k, j, n)
                        b = j // 2
                        if j % 2 == 0 and exists(k):
                            wait(dve, s["delta"], k * B + b + 1)
                            wait(dve, xin[b], k * 16 + 16)
                            dve.tensor_tensor(buf[b], dl[:], buf[b], ALU.add).then_inc(s["x2"], 1)
                        if j % 2 == 1 and (exists(k) or j == 1) and not (isinstance(k, int) and k * B + b == 0):
                            norm(k, b, k * B + b - 1)
                run(dve, body)


def scan_weights(nc, g, a, passes, in_x):
    with ExitStack() as ctx:
        m = Mem(nc, ctx, f"sw{passes[0]}")
        v = Views(g.X, 0)
        wn = {i: v.take(2, C * TAPS, parts=C) if in_x else m.sb(f"wn{i}", [C, 2, C * TAPS]) for i in passes}
        wf = [v.take(TAPS, C) if in_x else m.sb(f"wf{i}", [P, TAPS, C]) for i in range(2)]
        ident = v.take(P) if in_x else m.sb("id", [P, P])
        loads = 16 * 2 * len(passes)
        psa, psb = ([m.ps(f"{n}{i}") for i in range(2)] for n in ("a", "b"))
        loaded, idr, turned, copied, chain, done, pads = g.weight_sems
        A8 = 8

        def blocks(t, pi):
            Tv = t.rearrange("p (d po c) -> p d po c", d=ND, po=2)
            rows = slice(pi * C, pi * C + C)
            if pi == 0:
                return [(Tv[rows, 0:5, 0, :], 0, 5), (Tv[rows, 1:5, 1, :], 1, 4)]
            return [(Tv[rows, 0:4, 0, :], 1, 4), (Tv[rows, 0:5, 1, :], 0, 5)]

        with nc.Block() as block:
            @block.sync
            def _(sp):
                for i in passes:
                    w = ("w_ud", "w_du", "w_lr", "w_rl")[i]
                    for h in range(2):
                        sp.dma_start(wn[i][:, h], a[w].rearrange("o c t -> o (c t)")).then_inc(loaded, 16)
                sp.wait_ge(loaded, loads)

            @block.tensor
            def _(pe):
                pe.wait_ge(loaded, loads)
                pe.wait_ge(idr, 1)
                for n, i in enumerate(passes):
                    wait(pe, copied, n - 1)
                    wv = wn[i][:].rearrange("o h (c t) -> o t (h c)", t=TAPS)
                    for t in range(TAPS):
                        dst = psa[n % 2][:, t * C:t * C + C] if t < A8 else psb[n % 2][:, 0:C]
                        last = pe.transpose(dst, wv[:, t], ident[0:C, 0:C])
                    last.then_inc(turned, 1)

            @block.scalar
            def _(act):
                for n in range(len(passes)):
                    act.wait_ge(turned, n + 1)
                    wait(act, done, n - 1)
                    act.activation(wf[n % 2][:, 0:A8], psa[n % 2][:].rearrange("p (t c) -> p t c", t=A8), ACT.Copy)
                    act.activation(wf[n % 2][:, A8], psb[n % 2][:, 0:C], ACT.Copy).then_inc(copied, 1)

            @block.vector
            def _(dve):
                link = Chain(dve, chain)
                dve.tensor_tensor(ident[:], g.Cm[:], g.J[:], ALU.add).then_inc(idr, 1)
                if not in_x:
                    dve.memset(g.rt[:], 0.0).then_inc(pads, 1)
                for t in (g.yh, g.yl):
                    dve.memset(t[:].bitcast(F32), 0.0).then_inc(pads, 1)
                for n, i in enumerate(passes):
                    for t in (g.Thi[i], g.Tlo[i]):
                        Tv = t[:].rearrange("p (d po c) -> p d po c", d=ND, po=2)
                        dve.memset(Tv[0:C, 0, 1, :].bitcast(F32), 0.0)
                        dve.memset(Tv[C:P, ND - 1, 0, :].bitcast(F32), 0.0)
                    dve.wait_ge(copied, n + 1)
                    for pi in range(2):
                        for dst, t0, taps in blocks(g.Thi[i][:], pi):
                            last = dve.tensor_copy(dst, wf[n % 2][pi * C:pi * C + C, t0:t0 + 2 * taps - 1:2, :])
                    link(last)
                    for pi in range(2):
                        his = blocks(g.Thi[i][:], pi)
                        for (dst, t0, taps), (hi, _, _) in zip(blocks(g.Tlo[i][:], pi), his):
                            last = dve.tensor_tensor(dst, wf[n % 2][pi * C:pi * C + C, t0:t0 + 2 * taps - 1:2, :],
                                                     hi.bitcast(F32), ALU.subtract)
                    last.then_inc(done, 1)
                dve.wait_ge(pads, 2 if in_x else 3)
                dve.wait_ge(done, len(passes))


def scan_pass(nc, g, a, i):
    vertical, reverse, turn = i < 2, i % 2 == 1, i == 1
    with ExitStack() as ctx:
        m = Mem(nc, ctx, f"s{i}")
        ps = [m.ps(f"ps{r}") for r in range(2)]
        hi_ready, full_ready, lo_ready, conv_done, turned = g.scan_sems[i % 2]
        Xv = g.X[:].rearrange("p (s b j w) -> p s b j w", s=2, b=B, j=HP)

        def line(j, slot):
            if vertical:
                return Xv[:, slot, :, bass.ds(j, 1), :].rearrange("p b j w -> p b (j w)")
            return Xv[:, slot, :, :, bass.ds(j, 1)].rearrange("p b j w -> p b (j w)")

        def place(k, r):
            return (63 - k, 1 - r) if reverse else (k, r)

        inner = slice(2, 2 + 64)
        with nc.Block() as block:
            if i in (1, 2):
                @block.sync
                def _(sp):
                    for sem in g.scan_sems[1 - i % 2]:
                        sp.sem_clear(sem)
                    if i == 2:
                        load_mixture(sp, g, a)

            @block.tensor
            def _(pe):
                def step(k, r):
                    n = 2 * k + r
                    out = ps[r][:, 0:B * 64].rearrange("p (b w) -> p b w", b=B)
                    pe.wait_ge(hi_ready, n)
                    for t in (g.Tlo[i], g.Thi[i]):
                        for d in range(ND):
                            pe.matmul(out, t[:, d * P:d * P + P], g.yh[:, :, d:d + 64],
                                      start=(t is g.Tlo[i] and d == 0), stop=False)
                    pe.wait_ge(lo_ready, n)
                    for d in range(ND):
                        last = pe.matmul(out, g.Thi[i][:, d * P:d * P + P], g.yl[:, :, d:d + 64],
                                         start=False, stop=(d == ND - 1))
                    last.then_inc(conv_done, 1)
                step(0, 1)
                with pe.Fori(1, 64) as k:
                    for r in range(2):
                        step(k, r)

            @block.vector
            def _(dve):
                def split(x, n):
                    dve.wait_ge(hi_ready, n + 1)
                    wait(dve, full_ready, n + (1 if turn else 0))
                    dve.tensor_tensor(g.yl[:, :, inner], x, g.yh[:, :, inner].bitcast(F32), ALU.subtract
                                      ).then_inc(lo_ready, 1)

                def step(k, r):
                    n = 2 * k + r
                    j, slot = place(k, r)
                    x = line(j if isinstance(j, int) else dve.snap(j), slot)
                    dve.wait_ge(conv_done, n)
                    if reverse and r == 0:
                        settle(dve, g.settled)
                    conv = ps[r][:, 0:B * 64].rearrange("p (b w) -> p b w", b=B)
                    dve.scalar_tensor_tensor(g.yh[:, :, inner], conv, 0.0, x, ALU.max, ALU.add
                                             ).then_inc(hi_ready, 1)
                    full = x
                    if turn:
                        full = g.ybuf[slot][:]
                        wait(dve, turned, k)
                    dve.scalar_tensor_tensor(full, conv, 0.0, x, ALU.max, ALU.add
                                             ).then_inc(full_ready, 1)
                    split(full, n)

                j, slot = place(0, 0)
                x = line(j, slot)
                dve.tensor_copy(g.yh[:, :, inner], x).then_inc(hi_ready, 1)
                if turn:
                    dve.tensor_copy(g.ybuf[slot][:], x).then_inc(full_ready, 1)
                split(x, 0)
                step(0, 1)
                with dve.Fori(1, 64) as k:
                    for r in range(2):
                        step(k, r)

            if turn:
                @block.scalar
                def _(act):
                    def pair_of_rows(k):
                        act.wait_ge(full_ready, 2 * k + 2)
                        for h in range(2):
                            for v in range(2):
                                dst = Xv[h * C:h * C + C, v, :, bass.ds(63 - k, 1), :]
                                last = act.activation(dst.rearrange("p b j w -> p b (j w)"),
                                                      g.ybuf[h][v * C:v * C + C], ACT.Copy)
                        last.then_inc(turned, 1)
                    pair_of_rows(0)
                    with act.Fori(1, 64) as k:
                        pair_of_rows(k)

def top2_mixture(nc, g, a, y_out):
    G2 = 2 * E1
    BLOCKS = 6
    ROWS = BLOCKS * G2
    TILES = N // P
    TW = P + G2
    GR = 2 * TILES * 2
    EP = E1 // 2
    UNITS = 2 * EP
    PAIRS = CHUNKS // 2
    NEVER = -1.0e30
    LINKS, POOL_LINKS = 10, 5
    ND_SEM = 4 * 16
    with ExitStack() as ctx:
        m = Mem(nc, ctx, "tm")
        rx = m.sb("rx", [P, TW])
        rev, bb = m.sb("rev", [P, E1]), m.sb("bb", [ROWS, 2, C])
        rbias, wexp, bn = g.rbias, g.wexp, g.bn
        bhi, bias = m.sb("bhi", [ROWS, 2 * C], F32R), m.sb("bias", [ROWS, 2 * C], F32R)
        r16, hmask = m.sb("r16", [ROWS, G2]), m.sb("hmask", [ROWS, 2])
        sel = m.sb("sel", [ROWS, G2, C], F32R)
        zero = m.sb("zero", [P, 1])
        x2 = [[m.sb(f"x2_{u}{i}", [P, N]) for i in range(2)] for u in range(2)]
        yo = [m.sb(f"yo{i}", [P, N]) for i in range(2)]
        nS = [[m.sb(f"nS{u}{i}", [P, N]) for i in range(2)] for u in range(2)]
        nd = [[m.sb(f"nd{u}{i}", [P, 2, N]) for i in range(2)] for u in range(2)]
        Z = [[m.sb(f"Z{i}{h}", [P, N]) for h in range(2)] for i in range(2)]
        xh, xl, Cmr = m.sb("xh", [P, N], F32R), m.sb("xl", [P, N], F32R), m.sb("Cmr", [P, P], F32R)
        sqt = m.sb("sqt", [P, 4, C])
        V, LV = (m.sb(n, [P, GR]) for n in ("V", "LV"))
        R = [m.sb(f"R{u}", [P, GR]) for u in range(2)]
        L0, L, EX, A_, F1, F2 = (m.sb(n, [P, GR, E1]) for n in ("L0", "L", "EX", "A", "F1", "F2"))
        m1, total = m.sb("m1", [P, GR]), m.sb("total", [P, GR])
        GG = m.sb("GG", [P, 2, 2 * TILES, G2])
        gp = [m.sb(f"gp{u}", [P, 2 * TILES, 3, 2, G2], F32R) for u in range(2)]
        gT = [m.sb(f"gT{i}", [ROWS, N], F32R) for i in range(2)]
        bankA, bankB = m.ps("bankA"), m.ps("bankB")
        po = [m.ps(f"po{i}") for i in range(2)]
        pg = [[m.ps(f"pg{i}{h}") for h in range(2)] for i in range(2)]
        x2_in, nd_in = ([[m.sem(f"{n}{u}{i}") for i in range(2)] for u in range(2)] for n in ("x2i", "nd"))
        y_st = m.sems("yst", 2)
        s = {n: m.sem(n) for n in (
            "x3", "xhigh", "xparts", "centred", "xcs", "tiledA", "tiledB", "readA", "readB", "lnv", "rstd", "logits",
            "logits_used", "scaled", "shifted", "exp", "chosen", "weighed", "inverse", "gates",
            "turned", "gcopied", "bcast", "z", "zmm", "y")}
        chain, pool_chain, act_chain, chain0, prep_done = (
            m.sem(n) for n in ("chain", "pchain", "achain", "chain0", "prepd"))
        Xv = g.X[:].rearrange("p (s n) -> p s n", s=2)
        x_dst = y_out.rearrange("b c (j t) w -> b t c j w", t=2)
        wide = [P, GR, E1]

        def xview(k, u, i):
            return Xv[:, :, bass.ds((2 * u + i) * HP * WP + k * (JR * WP), JR * WP)]

        def natural(t):
            return t.rearrange("p (j w v) -> p v j w", j=JR, v=2)

        def over(t):
            return t.unsqueeze(2).to_broadcast(wide)

        def steps(engine, step, tail=0):
            pipelined(engine, step, PAIRS, 2, 4, tail=tail, head=2)

        def now(k, u):
            return valid(k, u, 2, PAIRS)

        with nc.Block() as block:
            @block.sync
            def _(sp):
                def load_x2(k, u, i):
                    wait(sp, s["x3"], (2 * k + u) * 2 + i - 3)
                    settle(sp, g.settled)
                    sp.dma_start(x2[u][i][:], g.x2s[bass.ds(k * B + 2 * u + i, 1)].rearrange("t p n -> p (t n)")
                                 ).then_inc(x2_in[u][i], 16)

                def copy_tokens(k, u, i):
                    n = (2 * k + u) * 2 + i
                    wait(sp, s["xcs"], n + 1)
                    settle(sp, g.settled)
                    wait(sp, s["z"], (n - 3) * 2 * EP)
                    for h in range(2):
                        for half in range(2):
                            sp.dma_start(nd[u][i][half * C:half * C + C, h, :],
                                         nS[u][i][h * C:h * C + C]).then_inc(nd_in[u][i], 16)

                def store_y(k, u, i):
                    wait(sp, s["y"], (2 * k + u) * 2 + i + 1)
                    settle(sp, g.settled)
                    for h in range(2):
                        sp.dma_start(x_dst[2 * u + i, h][:, bass.ds(k * JR, JR), :],
                                     yo[i][h * C:h * C + C].rearrange("p (j w) -> p j w", j=JR)
                                     ).then_inc(y_st[i], 16)

                def step(k, u):
                    ahead, before, ex, last = (back(k, u, d, 2) for d in (-2, 1, 3, 4))
                    if now(*ahead):
                        load_x2(*ahead, 0)
                    if now(*last):
                        store_y(*last, 1)
                    if now(*before):
                        copy_tokens(*before, 0)
                    if now(*ahead):
                        load_x2(*ahead, 1)
                    if now(*ex):
                        store_y(*ex, 0)
                    if now(*before):
                        copy_tokens(*before, 1)
                for u in range(2):
                    for i in range(2):
                        load_x2(0, u, i)
                steps(sp, step, tail=1)
                for i in range(2):
                    sp.wait_ge(y_st[i], 16 * 2 * PAIRS)

            @block.tensor
            def _(pe):
                pe.wait_ge(prep_done, 1)

                def centre(k, u, i):
                    n = (2 * k + u) * 2 + i
                    wait(pe, s["xparts"], n + 1)
                    wait(pe, s["readA"], n)
                    pe.matmul(bankA[:], Cmr[:], xh[:], start=True, stop=False)
                    pe.matmul(bankA[:], Cmr[:], xl[:], start=False, stop=True).then_inc(s["centred"], 1)

                def tiles(k, u, i):
                    n = (2 * k + u) * 2 + i
                    wait(pe, s["xcs"], n + 1)
                    wait(pe, s["readB"], n)
                    wait(pe, s["gcopied"], n - 5)
                    for bank, t0, done in ((bankB, 2, "tiledB"), (bankA, 0, "tiledA")):
                        for t in range(2):
                            at = (t0 + t) * P
                            last = pe.matmul(bank[:, t * TW:t * TW + TW], nS[u][i][:, at:at + P], rx[:],
                                             start=True, stop=True)
                        last.then_inc(s[done], 1)

                def turn_gates(k, u, i, read):
                    wait(pe, s["gates"], 2 * k + u + 1)
                    wait(pe, s["gcopied"], (2 * k + u) * 2 + i)
                    wait(pe, s["readB"], read)
                    for t in range(TILES):
                        last = pe.transpose(bankB[0:ROWS, t * P:t * P + P],
                                            gp[u][:, i * TILES + t].rearrange("p a l e -> p (a l e)").bitcast(F32),
                                            rx[:, 0:P])
                    last.then_inc(s["turned"], 1)

                def broadcast(k, u, q):
                    i, ep = divmod(q, EP)
                    t = 2 * k + u
                    if ep == 0:
                        wait(pe, s["gcopied"], 2 * t + i + 1)
                    for h in range(2):
                        wait(pe, s["z"], (t * UNITS + q - 2) * 2 + h + 1)
                        at = h * E1 + 2 * ep
                        pe.matmul(pg[q % 2][h][:], sel[:, at:at + 2].rearrange("p e c -> p (e c)"), gT[i][:],
                                  start=True, stop=True).then_inc(s["bcast"], 1)

                def biases(k, u, i):
                    wait(pe, s["y"], (2 * k + u) * 2 + i - 1)
                    pe.matmul(po[i][:], bias[:], gT[i][:], start=True, stop=False, skip_group_check=True)

                def experts(k, u, q):
                    i, ep = divmod(q, EP)
                    wait(pe, s["z"], ((2 * k + u) * UNITS + q) * 2 + 2)
                    for h in range(2):
                        last = pe.matmul(po[i][h * C:h * C + C, :], wexp[:, ep], Z[q % 2][h][:],
                                         start=False, stop=(ep == EP - 1), skip_group_check=True)
                    last.then_inc(s["zmm"], 1)

                def step(k, u):
                    n = (2 * k + u) * 2
                    near, ex = back(k, u, 2, 2), back(k, u, 3, 2)
                    read = [min(n + c, CHUNKS) if isinstance(k, int) else n + c for c in (1, 2)]
                    for q in range(UNITS):
                        if now(k, u) and q in (0, 3):
                            centre(k, u, q // 3)
                        if now(k, u) and q in (1, 5):
                            tiles(k, u, q // 4)
                        if now(*ex) and q == 2:
                            turn_gates(*ex, 1, read[0])
                        if now(*near) and q == 6:
                            turn_gates(*near, 0, read[1])
                        if now(*ex) and q % EP == 0:
                            biases(*ex, q // EP)
                        if q + 1 < UNITS and now(*ex):
                            broadcast(*ex, q + 1)
                        if q + 1 == UNITS and now(*near):
                            broadcast(*near, 0)
                        if now(*ex):
                            experts(*ex, q)
                steps(pe, step)

            @block.scalar
            def _(act):
                load_ln_exp(nc, act)

                def high_part(k, u, i):
                    n = (2 * k + u) * 2 + i
                    wait(act, s["x3"], n + 1)
                    wait(act, s["centred"], n)
                    settle(act, g.settled)
                    act.activation(xh[:].rearrange("p (v n) -> p v n", v=2), xview(k, u, i), ACT.Copy
                                   ).then_inc(s["xhigh"], 1)

                def copy_centred(k, u, i):
                    n = (2 * k + u) * 2 + i
                    wait(act, s["centred"], n + 1)
                    wait(act, s["tiledA"], n - 3)
                    wait(act, nd_in[u][i], k * ND_SEM)
                    act.activation(nS[u][i][:], bankA[:], ACT.Copy).then_inc(s["xcs"], 1)

                def read_tiles(k, u, i):
                    n = (2 * k + u) * 2 + i
                    if i == 0:
                        wait(act, s["lnv"], 2 * k + u)
                        wait(act, s["logits_used"], 2 * k + u)
                    for bank, t0, done, free in ((bankB, 2, "tiledB", "readB"), (bankA, 0, "tiledA", "readA")):
                        wait(act, s[done], n + 1)
                        rows = (i * TILES + t0) * 2
                        tv = bank[:, 0:2 * TW].rearrange("p (t x) -> p t x", t=2)
                        for t in range(2):
                            for h in range(2):
                                r = rows + 2 * t + h
                                act.activation(sqt[:, 2 * t + h], tv[:, t, h * C:h * C + C], ACT.Square,
                                               accum_out=V[:, r:r + 1]).then_inc(act_chain, 1)
                        act.activation(L0[:, rows:rows + 4, :].rearrange("p (t h) e -> p t (h e)", h=2),
                                       tv[:, :, P:TW], ACT.Copy).then_inc(s["logits"], 1)
                        act.wait_ge(act_chain, (n + 1) * 8 - (4 if t0 else 0))
                        act.wait_ge(s["logits"], 2 * n + (1 if t0 else 2))
                        settle(act, s[free])

                def rstd(k, u):
                    t = 2 * k + u
                    act.activation(LV[:], V[:], ACT.Ln, bias=g.eps[:, 1:2], scale=1.0 / C).then_inc(s["lnv"], 1)
                    wait(act, s["gates"], t - 1)
                    act.wait_ge(s["lnv"], t + 1)
                    act.activation(R[u][:], LV[:], ACT.Exp, scale=-0.5).then_inc(s["rstd"], 1)

                def copy_gates(k, u, i):
                    n = (2 * k + u) * 2 + i
                    wait(act, s["turned"], n + 1)
                    wait(act, s["zmm"], (n - 1) * EP)
                    act.activation(gT[i][:], bankB[0:ROWS, :], ACT.Copy).then_inc(s["gcopied"], 1)

                def step(k, u):
                    after, before, near, ex = (back(k, u, d, 2) for d in (-1, 1, 2, 3))
                    if now(k, u):
                        copy_centred(k, u, 0)
                        high_part(k, u, 1)
                        read_tiles(k, u, 0)
                    if now(*before):
                        wait(act, s["shifted"], 2 * before[0] + before[1] + 1)
                        act.activation(EX[:], L[:], ACT.Exp).then_inc(s["exp"], 1)
                    if now(*ex):
                        copy_gates(*ex, 1)
                    if now(k, u):
                        copy_centred(k, u, 1)
                        read_tiles(k, u, 1)
                    if now(k, u):
                        rstd(k, u)
                    if now(*near):
                        copy_gates(*near, 0)
                    if now(*after):
                        high_part(*after, 0)
                high_part(0, 0, 0)
                steps(act, step, tail=1)

            @block.gpsimd
            def _(pool):
                def low_part(k, u, i):
                    wait(pool, s["xhigh"], (2 * k + u) * 2 + i + 1)
                    settle(pool, g.settled)
                    pool.tensor_tensor(xl[:].rearrange("p (v n) -> p v n", v=2), xview(k, u, i),
                                       xh[:].rearrange("p (v n) -> p v n", v=2).bitcast(F32), ALU.subtract
                                       ).then_inc(s["xparts"], 1)

                def scale(k, u):
                    t = 2 * k + u
                    wait(pool, s["rstd"], t + 1)
                    wait(pool, s["logits"], 4 * t + 4)
                    pool.tensor_tensor(L[:], L0[:], over(R[u][:]), ALU.mult).then_inc(s["logits_used"], 1)
                    pool.wait_ge(s["logits_used"], t + 1)
                    pool.tensor_tensor(L[:], L[:], rbias[:].unsqueeze(1).to_broadcast(wide), ALU.add
                                       ).then_inc(s["scaled"], 1)

                def weigh(k, u):
                    t = 2 * k + u
                    link = Chain(pool, pool_chain, base=t * POOL_LINKS)
                    wait(pool, s["chosen"], t + 1)
                    link(pool.tensor_tensor(F1[:], F1[:], F2[:], ALU.add))
                    wait(pool, s["exp"], t + 1)
                    pool.tensor_tensor(F1[:], F1[:], EX[:], ALU.mult).then_inc(s["weighed"], 1)

                def split(k, u):
                    t = 2 * k + u
                    link = Chain(pool, pool_chain, base=t * POOL_LINKS, count=1)
                    wait(pool, s["inverse"], t + 1)
                    wait(pool, s["turned"], 2 * t - 2)
                    plain = GG[:, 1].rearrange("p t (h e) -> p (t h) e", h=2)
                    scaled = GG[:, 0].rearrange("p t (h e) -> p (t h) e", h=2)
                    both = GG[:].rearrange("p k t e -> p t k e")
                    none = zero[:].unsqueeze(2).unsqueeze(3).to_broadcast(list(both.shape))
                    link(pool.tensor_tensor(plain, F1[:], over(total[:]), ALU.mult))
                    link(pool.tensor_tensor(scaled, plain, over(R[u][:]), ALU.mult))
                    link(pool.tensor_tensor(gp[u][:, :, 0:2, 0], both, none, ALU.add))
                    link(pool.tensor_tensor(gp[u][:, :, 0:2, 1], both, gp[u][:, :, 0:2, 0].bitcast(F32), ALU.subtract))
                    pool.tensor_tensor(gp[u][:, :, 2], gp[u][:, :, 1].bitcast(F32), none, ALU.add).then_inc(s["gates"], 1)

                def step(k, u):
                    after, before = back(k, u, -1, 2), back(k, u, 1, 2)
                    if now(k, u):
                        low_part(k, u, 1)
                    if now(*before):
                        weigh(*before)
                    if now(*after):
                        low_part(*after, 0)
                    if now(k, u):
                        scale(k, u)
                    if now(*before):
                        split(*before)
                pool.wait_ge(prep_done, 1)
                low_part(0, 0, 0)
                steps(pool, step, tail=1)

            @block.vector
            def _(dve):
                link = Chain(dve, chain0)
                dve.memset(zero[:], 0.0)
                dve.wait_ge(g.mix_loaded, 16 * MIX_LOADS)
                dve.tensor_copy(rx[:, P:TW], g.rt[:])
                link(dve.tensor_tensor(rx[:, 0:P], g.Cm[:], g.J[:], ALU.add))
                dve.tensor_copy(Cmr[:], g.Cm[:])
                for e in range(E1):
                    dve.memset(rev[:, e:e + 1], float(E1 - e))
                link(dve.memset(sel[:].bitcast(F32), 0.0))
                link(dve.memset(bias[:].bitcast(F32), 0.0))
                link(dve.tensor_tensor(r16[:], rx[0:ROWS, 0:G2], rx[0:ROWS, G2:2 * G2], ALU.add))
                for q in range(2, BLOCKS):
                    link(dve.tensor_tensor(r16[:], r16[:], rx[0:ROWS, q * G2:(q + 1) * G2], ALU.add))
                dve.tensor_copy(sel[0:2 * G2], bcast(r16[0:2 * G2], 2, C))
                link(dve.tensor_reduce(hmask[:], r16[:].rearrange("p (h e) -> p h e", h=2), AXX, ALU.add))
                link(dve.tensor_tensor(bb[:], bcast(bn[:], 1, 2), bcast(hmask[:], 2, C), ALU.mult))
                flat = bb[:].rearrange("p h c -> p (h c)")
                link(dve.tensor_copy(bhi[:], flat))
                dve.tensor_copy(bias[2 * G2:4 * G2], bhi[2 * G2:4 * G2].bitcast(F32))
                link(dve.tensor_tensor(bias[4 * G2:ROWS], flat[4 * G2:ROWS], bhi[4 * G2:ROWS].bitcast(F32),
                                       ALU.subtract))
                dve.memset(m1[:], 0.0).then_inc(prep_done, 1)
                dve.wait_ge(prep_done, 1)

                def x3(k, u, i):
                    wait(dve, x2_in[u][i], k * 16 + 16)
                    xv = xview(k, u, i).rearrange("p v (j w) -> p v j w", j=JR)
                    dve.tensor_tensor(xv, natural(x2[u][i][:]), xv, ALU.add).then_inc(s["x3"], 1)

                def z_of(k, u, q, h):
                    i, ep = divmod(q, EP)
                    t = 2 * k + u
                    wait(dve, s["bcast"], (t * UNITS + q) * 2 + h + 1)
                    wait(dve, s["zmm"], t * UNITS + q - 1)
                    if ep == 0 and h == 0:
                        wait(dve, nd_in[u][i], (k + 1) * ND_SEM)
                    dve.tensor_tensor(Z[q % 2][h][:], pg[q % 2][h][:], nd[u][i][:, h, :], ALU.mult
                                      ).then_inc(s["z"], 1)

                def y_of(k, u, i):
                    n = (2 * k + u) * 2 + i
                    wait(dve, s["zmm"], (n + 1) * EP)
                    wait(dve, y_st[i], (2 * k + u) * 32)
                    dve.tensor_tensor(natural(yo[i][:]), po[i][:].rearrange("p (v j w) -> p v j w", v=2, j=JR),
                                      xview(k, u, i).rearrange("p v (j w) -> p v j w", j=JR), ALU.add
                                      ).then_inc(s["y"], 1)

                def choose(k, u, n):
                    t = 2 * k + u
                    revb = rev[:].unsqueeze(1).to_broadcast(wide)

                    def linked(instruction, count):
                        instruction.then_inc(chain, 1)

                    def before(count):
                        dve.wait_ge(chain, t * LINKS + count)

                    if n == 0:
                        wait(dve, s["scaled"], t + 1)
                        linked(dve.tensor_reduce(m1[:], L[:], AXX, ALU.max), 1)
                    elif n == 1:
                        before(1)
                        dve.tensor_tensor(L[:], L[:], over(m1[:]), ALU.subtract).then_inc(s["shifted"], 1)
                    elif n == 2:
                        dve.wait_ge(s["shifted"], t + 1)
                        linked(dve.scalar_tensor_tensor(A_[:], L[:], 0.0, revb, ALU.is_equal, ALU.mult), 2)
                    elif n == 3:
                        before(2)
                        linked(dve.tensor_reduce(m1[:], A_[:], AXX, ALU.max), 3)
                    elif n == 4:
                        wait(dve, s["gates"], t)
                        before(3)
                        linked(dve.tensor_tensor(F1[:], A_[:], over(m1[:]), ALU.is_equal), 4)
                    elif n == 5:
                        wait(dve, s["exp"], t + 1)
                        before(4)
                        linked(dve.scalar_tensor_tensor(L[:], F1[:], NEVER, L[:], ALU.mult, ALU.add), 5)
                    elif n == 6:
                        before(5)
                        linked(dve.tensor_reduce(m1[:], L[:], AXX, ALU.max), 6)
                    elif n == 7:
                        before(6)
                        linked(dve.tensor_tensor(A_[:], L[:], over(m1[:]), ALU.is_equal), 7)
                    elif n == 8:
                        before(7)
                        linked(dve.tensor_tensor(A_[:], A_[:], revb, ALU.mult), 8)
                    elif n == 9:
                        before(8)
                        linked(dve.tensor_reduce(m1[:], A_[:], AXX, ALU.max), 9)
                    elif n == 10:
                        before(9)
                        dve.tensor_tensor(F2[:], A_[:], over(m1[:]), ALU.is_equal).then_inc(s["chosen"], 1)
                    elif n == 11:
                        wait(dve, s["weighed"], t + 1)
                        linked(dve.tensor_reduce(total[:], F1[:], AXX, ALU.add), 10)
                    elif n == 12:
                        before(10)
                        dve.reciprocal(total[:], total[:]).then_inc(s["inverse"], 1)

                slots = [((0,), (1,)), ((2,), ()), ((3,), (4,)), ((5,), (6,)), ((7,), (8,)), ((9,), (10,)), ((), (11,)), ((), (12,))]

                def step(k, u):
                    after, before, ex, last = (back(k, u, d, 2) for d in (-1, 1, 3, 4))
                    for q in range(UNITS):
                        if now(*after) and q == 6:
                            x3(*after, 0)
                        if now(k, u) and q == 1:
                            x3(k, u, 1)
                        if now(*last) and q == 0:
                            y_of(*last, 1)
                        if now(*ex) and q == 5:
                            y_of(*ex, 0)
                        for h in range(2):
                            if now(*ex):
                                z_of(*ex, q, h)
                            if now(*before):
                                for n in slots[q][h]:
                                    choose(*before, n)
                x3(0, 0, 0)
                steps(dve, step, tail=1)


class Shared:
    pass


def metaformer_kernel(nc, a, out):
    g = Shared()
    with ExitStack() as ctx:
        m = Mem(nc, ctx, "g")
        g.x1s = nc.dram_tensor("x1s", [CHUNKS, P, N], F32).ap()
        g.x1tok = nc.dram_tensor("x1tok", [B, HP, W, P], F32).ap()
        g.x2s = nc.dram_tensor("x2s", [CHUNKS, P, N], F32).ap()
        g.Cm, g.J = m.sb("Cm", [P, P]), m.sb("J", [P, P])
        g.eps = m.sb("eps", [P, 2])
        g.b1, g.gate_b = m.sb("b1", [C, 1]), m.sb("gate_b", [P, 1])
        g.experts_loaded, g.settled = m.sem("experts_loaded"), m.sem("settled")
        g.wexp, g.bn = m.sb("wexp", [P, E1 // 2, C]), m.sb("bn", [12 * E1, C])
        g.rbias, g.rt, g.mix_loaded = m.sb("rbias", [P, E1]), m.sb("rt", [P, 2 * E1]), m.sem("mix_loaded")
        g.weight_sems = [m.sem(f"w_{n}") for n in ("ld", "id", "tn", "cp", "ch", "dn", "pads")]
        g.scan_sems = [[m.sem(f"{n}{r}") for n in ("hi", "full", "lo", "conv", "turned")] for r in range(2)]
        g.X = m.sb("X", [P, 2 * SLOT])
        v = Views(g.X, 0)
        g.xr = [v.take(N) for _ in range(8)]
        g.sq, g.rr, g.nn, g.tsq = ([v.take(N) for _ in range(2)] for _ in range(4))
        g.lowS = [v.take(N // 2, parts=C + 1) for _ in range(2)]
        g.ts = [v.take(N) for _ in range(4)]
        g.trs = v.take(N)
        v = Views(g.X, 2 * (TOK + PAD))
        g.W1, g.W2 = v.take(E0, HID), v.take(E0, 2, C)
        g.ident, g.Alow, g.Brec, g.Gc = v.take(P), v.take(2, C), v.take(2, P), v.take(2 * E0)
        g.w2bias = v.take(C, parts=E0)
        g.small_at = v.at
        with ExitStack() as early:
            me = Mem(nc, early, "g")
            g.E = me.sb("E", [P, 2 * TOK + PAD])
            setup_block0(nc, g, a)
            wavelet_mixer(nc, g, a)
            g.D = me.sb("D", [P, B, P])
            expert_choice(nc, g, a)
            g.Thi, g.Tlo = ({0: me.sb(n, [P, ND * P], F32R)} for n in ("Th", "Tl"))
            g.yh, g.yl = me.sb("yh0", [P, B, 68], F32R), me.sb("yl0", [P, B, 68], F32R)
            scan_weights(nc, g, a, (0,), True)
            apply_and_first_scan(nc, g, a)
        with ExitStack() as mid:
            mm = Mem(nc, mid, "g")
            g.Thi, g.Tlo = ({i: mm.sb(f"{n}{i}", [P, ND * P], F32R) for i in (1, 2, 3)} for n in ("Thi", "Tlo"))
            g.yh, g.yl = mm.sb("yh", [P, B, 68], F32R), mm.sb("yl", [P, B, 68], F32R)
            g.ybuf = [mm.sb(f"yb{r}", [P, B, 64]) for r in range(2)]
            scan_weights(nc, g, a, (1, 2, 3), False)
            for i in (1, 2, 3):
                scan_pass(nc, g, a, i)
        top2_mixture(nc, g, a, out)


_INPUTS = {"x": "x", "s_ll": "L0_conv_s_ll", "s_lh": "L0_conv_s_lh", "s_hl": "L0_conv_s_hl",
           "s_hh": "L0_conv_s_hh", "w1": "L0_conv_w1", "b1": "L0_conv_b1", "w2": "L0_conv_w2",
           "b2": "L0_conv_b2", "gate_w": "L0_ffn_gate_w", "gate_b": "L0_ffn_gate_b",
           "weight1": "L0_ffn_weight1", "weight2": "L0_ffn_weight2", "w_ud": "L1_conv_w_ud",
           "w_du": "L1_conv_w_du", "w_lr": "L1_conv_w_lr", "w_rl": "L1_conv_w_rl",
           "router_w": "L1_ffn_router_w", "router_b": "L1_ffn_router_b",
           "expert_w": "L1_ffn_expert_w", "expert_b": "L1_ffn_expert_b"}


def kernel(**inputs):
    import concourse.bacc as bacc
    from concourse.bass_utils import run_bass_kernel_spmd

    nc = bacc.Bacc("TRN2", target_bir_lowering=False, num_devices=1)
    arrays, args = {}, {}
    for short, name in _INPUTS.items():
        arr = np.ascontiguousarray(inputs[name])
        arrays[f"in_{name}"] = arr
        args[short] = nc.dram_tensor(f"in_{name}", arr.shape, mybir.dt.from_np(arr.dtype),
                                     kind="ExternalInput").ap()
    y = nc.dram_tensor("y", (B, C, H, W), F32, kind="ExternalOutput").ap()
    metaformer_kernel(nc, args, y)
    return run_bass_kernel_spmd(nc, [arrays], core_ids=[0]).results[0]["y"]
```
